# Optimizing a Trainium2 kernel written in Bass

```python
import numpy as np
import jax
import jax.numpy as jnp

def _softmax(x, axis=-1):
    return jax.nn.softmax(x, axis=axis)

def _gelu(x):
    return jax.nn.gelu(x, approximate=True)

def _silu(x):
    return jax.nn.silu(x)

def _sigmoid(x):
    return jax.nn.sigmoid(x)

def _layernorm(x, axis=-1, eps=1e-05):
    m = jnp.mean(x, axis=axis, keepdims=True)
    v = jnp.var(x, axis=axis, keepdims=True)
    return (x - m) / jnp.sqrt(v + eps)

def _scatter_add(tgt, idx, src, axis=0):
    return tgt.at[idx].add(src)

def _segment_sum(src, seg, n):
    return jax.ops.segment_sum(src, seg, n)
kernel_name = 'mk_decoder_postln_d2_seqx_r4_9d2732'

def setup_inputs(seed: int=0):
    np.random.seed(seed)
    _w = jnp.asarray

    def _rec_inputs():
        import jax
        import jax.numpy as jnp
        _rk = jax.random.key(seed)
        x = -0.0003929 + 0.9999 * jax.random.normal(jax.random.fold_in(_rk, 1), (4, 512, 256), jnp.float32)
        _lenS = 512 - jax.random.randint(jax.random.fold_in(_rk, 7), (4,), 0, max(1, 512 // 4) + 1, jnp.int32)
        _lenS2 = 1601 - jax.random.randint(jax.random.fold_in(_rk, 8), (4,), 0, max(1, 1601 // 4) + 1, jnp.int32)
        _ctx_512P = jax.random.normal(jax.random.fold_in(_rk, 11), (4, 16, 128), jnp.float32)
        _ctx_512c = jax.random.dirichlet(jax.random.fold_in(_rk, 511), 0.3 * jnp.ones((16,), jnp.float32), (4, 1601))
        _ctx_512t = jnp.einsum('bsk,bkd->bsd', _ctx_512c, _ctx_512P)
        _ctx_512t = _ctx_512t * jax.lax.rsqrt(jnp.mean(jnp.square(_ctx_512t)) + 1e-12) * 0.953939
        ctx_512 = 4.13588e-05 + 0.999923 * (_ctx_512t + 0.3 * jax.random.normal(jax.random.fold_in(_rk, 611), (4, 1601, 128), jnp.float32))
        return (x, ctx_512)
    x, ctx_512 = _rec_inputs()

    def _L0_attn_setup():
        import jax, jax.numpy as jnp
        import numpy as np
        NUM_HEADS = 16
        key = jax.random.key(seed)
        k1, k2, k3 = jax.random.split(key, 3)
        S, B, E = (512, 4, 256)
        std = float(np.sqrt(2.0 / (E + E)))
        query = jax.random.normal(k1, (S, B, E), dtype=jnp.float32)
        in_proj_weight = jax.random.normal(k2, (3 * E, E), dtype=jnp.float32) * std
        in_proj_bias = jnp.zeros((3 * E,), dtype=jnp.float32)
        out_proj_weight = jax.random.normal(k3, (E, E), dtype=jnp.float32) * std
        out_proj_bias = jnp.zeros((E,), dtype=jnp.float32)
        return {'query': query, 'in_proj_weight': in_proj_weight, 'in_proj_bias': in_proj_bias, 'out_proj_weight': out_proj_weight, 'out_proj_bias': out_proj_bias}
    _L0_attn_all = _L0_attn_setup()
    _L0_attn_in = {k: v for k, v in _L0_attn_all.items() if k in ('in_proj_weight', 'in_proj_bias', 'out_proj_weight', 'out_proj_bias')}
    del _L0_attn_all

    def _L0_xattn_setup():
        import jax, jax.numpy as jnp
        import numpy as np
        B, LQ, LK = (8, 512, 512)
        QD, KD, VD = (256, 128, 128)
        key = jax.random.key(seed)
        ks = jax.random.split(key, 9)
        s = 0.02
        return {'query': jax.random.normal(ks[0], (B, LQ, QD), jnp.float32), 'key': jax.random.normal(ks[1], (B, LK, KD), jnp.float32), 'value': jax.random.normal(ks[2], (B, LK, VD), jnp.float32), 'Wq': jax.random.normal(ks[3], (QD, QD), jnp.float32) * s, 'bq': jnp.zeros((QD,), jnp.float32), 'Wk': jax.random.normal(ks[4], (KD, QD), jnp.float32) * s, 'bk': jnp.zeros((QD,), jnp.float32), 'Wv': jax.random.normal(ks[5], (VD, QD), jnp.float32) * s, 'bv': jnp.zeros((QD,), jnp.float32)}
    _L0_xattn_all = _L0_xattn_setup()
    _L0_xattn_in = {k: v for k, v in _L0_xattn_all.items() if k in ('Wq', 'bq', 'Wk', 'bk', 'Wv', 'bv')}
    del _L0_xattn_all

    def _L0_ffn_setup():
        import jax, jax.numpy as jnp
        import numpy as np
        E = 16
        H = 256
        F = 512
        TOP_K = 1
        B, S = (2, 256)
        key = jax.random.key(seed)
        ks = jax.random.split(key, 7)
        s = 0.02
        return {'hidden_states': jax.random.normal(ks[0], (B, S, H), jnp.float32), 'w_router': jax.random.normal(ks[1], (E, H), jnp.float32) * s, 'gate_up_proj': jax.random.normal(ks[2], (E, H, 2 * F), jnp.float32) * s, 'down_proj': jax.random.normal(ks[3], (E, F, H), jnp.float32) * s, 'w_gate': jax.random.normal(ks[4], (F, H), jnp.float32) * s, 'w_up': jax.random.normal(ks[5], (F, H), jnp.float32) * s, 'w_down': jax.random.normal(ks[6], (H, F), jnp.float32) * s}
    _L0_ffn_all = _L0_ffn_setup()
    _L0_ffn_in = {k: v for k, v in _L0_ffn_all.items() if k in ('w_router', 'gate_up_proj', 'down_proj', 'w_gate', 'w_up', 'w_down')}
    del _L0_ffn_all

    def _L1_attn_setup():
        import jax, jax.numpy as jnp
        import numpy as np
        ROPE_BASE = 2500
        B, L, D, NH = (2, 512, 256, 16)
        HD = D // NH

        def apply_rope(inputs, positions, base_frequency):
            head_dim = inputs.shape[-1]
            fraction = 2 * jnp.arange(0, head_dim // 2) / head_dim
            timescale = base_frequency ** fraction
            sinusoid = positions[..., None] / timescale[None, None, :]
            sinusoid = sinusoid[..., None, :]
            sin, cos = (jnp.sin(sinusoid), jnp.cos(sinusoid))
            first, second = jnp.split(inputs, 2, axis=-1)
            out = jnp.concatenate([first * cos - second * sin, second * cos + first * sin], axis=-1)
            return out.astype(inputs.dtype)
        key = jax.random.key(seed)
        ks = jax.random.split(key, 5)
        s = 0.02
        return {'x': jax.random.normal(ks[0], (B, L, D), jnp.float32), 'wq_w': jax.random.normal(ks[1], (D, D), jnp.float32) * s, 'wq_b': jnp.zeros((D,), jnp.float32), 'wk_w': jax.random.normal(ks[2], (D, D), jnp.float32) * s, 'wk_b': jnp.zeros((D,), jnp.float32), 'wv_w': jax.random.normal(ks[3], (D, D), jnp.float32) * s, 'wv_b': jnp.zeros((D,), jnp.float32), 'wo_w': jax.random.normal(ks[4], (D, D), jnp.float32) * s, 'wo_b': jnp.zeros((D,), jnp.float32)}
    _L1_attn_all = _L1_attn_setup()
    _L1_attn_in = {k: v for k, v in _L1_attn_all.items() if k in ('wq_w', 'wq_b', 'wk_w', 'wk_b', 'wv_w', 'wv_b', 'wo_w', 'wo_b')}
    del _L1_attn_all

    def _L1_xattn_setup():
        import jax, jax.numpy as jnp
        import numpy as np
        HEADS = 16
        D_MODEL = 256
        IMG_MODEL = 128
        D_K = D_MODEL // HEADS
        key = jax.random.key(seed)
        ks = jax.random.split(key, 12)
        B, LQ, LKV = (8, 512, 256)
        s_dm = 1.0 / np.sqrt(D_MODEL)
        s_im = 1.0 / np.sqrt(IMG_MODEL)
        return {'q': jax.random.normal(ks[0], (B, LQ, D_MODEL), jnp.float32), 'k': jax.random.normal(ks[1], (B, LKV, IMG_MODEL), jnp.float32), 'v': jax.random.normal(ks[2], (B, LKV, IMG_MODEL), jnp.float32), 'Wq': jax.random.normal(ks[3], (D_MODEL, D_MODEL), jnp.float32) * s_dm, 'bq': jnp.zeros((D_MODEL,), jnp.float32), 'Wk': jax.random.normal(ks[4], (IMG_MODEL, D_MODEL), jnp.float32) * s_im, 'bk': jnp.zeros((D_MODEL,), jnp.float32), 'Wv': jax.random.normal(ks[5], (IMG_MODEL, D_MODEL), jnp.float32) * s_im, 'bv': jnp.zeros((D_MODEL,), jnp.float32), 'Wo': jax.random.normal(ks[6], (D_MODEL, D_MODEL), jnp.float32) * s_dm, 'bo': jnp.zeros((D_MODEL,), jnp.float32)}
    _L1_xattn_all = _L1_xattn_setup()
    _L1_xattn_in = {k: v for k, v in _L1_xattn_all.items() if k in ('Wq', 'bq', 'Wk', 'bk', 'Wv', 'bv', 'Wo', 'bo')}
    del _L1_xattn_all

    def _L1_ffn_setup():
        import jax, jax.numpy as jnp
        import numpy as np
        D_MODEL = 256
        DEPTH = 8
        M = 2 ** DEPTH
        N_INTERNAL = M - 1
        B, T = (8, 1024)

        def _leaf_probs(gate):
            BT = gate.shape[0]
            lp = jnp.ones((BT, M), dtype=gate.dtype)
            for level in range(DEPTH):
                n = 2 ** level
                half = M // (2 * n)
                g = gate[:, n - 1:2 * n - 1]
                f = jnp.stack([1.0 - g, g], axis=-1)
                f = jnp.broadcast_to(f[..., None], (BT, n, 2, half))
                lp = lp * f.reshape(BT, M)
            return lp
        key = jax.random.key(seed)
        ks = jax.random.split(key, 7)
        x = jax.random.normal(ks[0], (B, T, D_MODEL), dtype=jnp.float32)
        Wq = jax.random.normal(ks[1], (D_MODEL, D_MODEL), dtype=jnp.float32) * 0.02
        routers = jax.random.normal(ks[2], (N_INTERNAL, D_MODEL), dtype=jnp.float32) * 0.02
        leaf_keys = jax.random.normal(ks[3], (M, D_MODEL), dtype=jnp.float32) * 0.02
        leaf_values = jax.random.normal(ks[4], (M, D_MODEL), dtype=jnp.float32) * 0.02
        Wout_w = jax.random.normal(ks[5], (D_MODEL, D_MODEL), dtype=jnp.float32) * 0.02
        Wout_b = jax.random.normal(ks[6], (D_MODEL,), dtype=jnp.float32) * 0.02
        return {'x': x, 'Wq': Wq, 'routers': routers, 'leaf_keys': leaf_keys, 'leaf_values': leaf_values, 'Wout_w': Wout_w, 'Wout_b': Wout_b}
    _L1_ffn_all = _L1_ffn_setup()
    _L1_ffn_in = {k: v for k, v in _L1_ffn_all.items() if k in ('Wq', 'routers', 'leaf_keys', 'leaf_values', 'Wout_w', 'Wout_b')}
    del _L1_ffn_all
    return {'x': x, 'ctx_512': ctx_512, 'L0_attn_in_proj_weight': _L0_attn_in['in_proj_weight'], 'L0_attn_in_proj_bias': _L0_attn_in['in_proj_bias'], 'L0_attn_out_proj_weight': _L0_attn_in['out_proj_weight'], 'L0_attn_out_proj_bias': _L0_attn_in['out_proj_bias'], 'L0_xattn_Wq': _L0_xattn_in['Wq'], 'L0_xattn_bq': _L0_xattn_in['bq'], 'L0_xattn_Wk': _L0_xattn_in['Wk'], 'L0_xattn_bk': _L0_xattn_in['bk'], 'L0_xattn_Wv': _L0_xattn_in['Wv'], 'L0_xattn_bv': _L0_xattn_in['bv'], 'L0_ffn_w_router': _L0_ffn_in['w_router'], 'L0_ffn_gate_up_proj': _L0_ffn_in['gate_up_proj'], 'L0_ffn_down_proj': _L0_ffn_in['down_proj'], 'L0_ffn_w_gate': _L0_ffn_in['w_gate'], 'L0_ffn_w_up': _L0_ffn_in['w_up'], 'L0_ffn_w_down': _L0_ffn_in['w_down'], 'L1_attn_wq_w': _L1_attn_in['wq_w'], 'L1_attn_wq_b': _L1_attn_in['wq_b'], 'L1_attn_wk_w': _L1_attn_in['wk_w'], 'L1_attn_wk_b': _L1_attn_in['wk_b'], 'L1_attn_wv_w': _L1_attn_in['wv_w'], 'L1_attn_wv_b': _L1_attn_in['wv_b'], 'L1_attn_wo_w': _L1_attn_in['wo_w'], 'L1_attn_wo_b': _L1_attn_in['wo_b'], 'L1_xattn_Wq': _L1_xattn_in['Wq'], 'L1_xattn_bq': _L1_xattn_in['bq'], 'L1_xattn_Wk': _L1_xattn_in['Wk'], 'L1_xattn_bk': _L1_xattn_in['bk'], 'L1_xattn_Wv': _L1_xattn_in['Wv'], 'L1_xattn_bv': _L1_xattn_in['bv'], 'L1_xattn_Wo': _L1_xattn_in['Wo'], 'L1_xattn_bo': _L1_xattn_in['bo'], 'L1_ffn_Wq': _L1_ffn_in['Wq'], 'L1_ffn_routers': _L1_ffn_in['routers'], 'L1_ffn_leaf_keys': _L1_ffn_in['leaf_keys'], 'L1_ffn_leaf_values': _L1_ffn_in['leaf_values'], 'L1_ffn_Wout_w': _L1_ffn_in['Wout_w'], 'L1_ffn_Wout_b': _L1_ffn_in['Wout_b']}

def reference(x, ctx_512, L0_attn_in_proj_weight, L0_attn_in_proj_bias, L0_attn_out_proj_weight, L0_attn_out_proj_bias, L0_xattn_Wq, L0_xattn_bq, L0_xattn_Wk, L0_xattn_bk, L0_xattn_Wv, L0_xattn_bv, L0_ffn_w_router, L0_ffn_gate_up_proj, L0_ffn_down_proj, L0_ffn_w_gate, L0_ffn_w_up, L0_ffn_w_down, L1_attn_wq_w, L1_attn_wq_b, L1_attn_wk_w, L1_attn_wk_b, L1_attn_wv_w, L1_attn_wv_b, L1_attn_wo_w, L1_attn_wo_b, L1_xattn_Wq, L1_xattn_bq, L1_xattn_Wk, L1_xattn_bk, L1_xattn_Wv, L1_xattn_bv, L1_xattn_Wo, L1_xattn_bo, L1_ffn_Wq, L1_ffn_routers, L1_ffn_leaf_keys, L1_ffn_leaf_values, L1_ffn_Wout_w, L1_ffn_Wout_b):
    import jax
    import jax.numpy as jnp

    def _L0_attn_ref(query, in_proj_weight, in_proj_bias, out_proj_weight, out_proj_bias):
        import jax, jax.numpy as jnp
        import numpy as np
        NUM_HEADS = 16
        S, B, E = query.shape
        H = NUM_HEADS
        hd = E // H
        scale = hd ** (-0.5)
        lin = jnp.einsum('sbe,fe->sbf', query, in_proj_weight) + in_proj_bias
        lin = lin.reshape(S, B * H, 3, hd)
        q = lin[:, :, 0, :]
        k = lin[:, :, 1, :]
        v = lin[:, :, 2, :]
        scores = jnp.einsum('sbd,tbd->bst', q, k) * scale
        attn = jax.nn.softmax(scores.astype(jnp.float32), axis=-1).astype(scores.dtype)
        ctx = jnp.einsum('bst,tbd->sbd', attn, v).reshape(S, B, E)
        out = jnp.einsum('sbe,fe->sbf', ctx, out_proj_weight) + out_proj_bias
        return out

    def _L0_xattn_ref(query, key, value, Wq, bq, Wk, bk, Wv, bv):
        import jax, jax.numpy as jnp
        import numpy as np
        B, LQ, LK = (8, 512, 512)
        QD, KD, VD = (256, 128, 128)
        q = jnp.einsum('bld,de->ble', query, Wq) + bq
        k = jnp.einsum('bld,de->ble', key, Wk) + bk
        v = jnp.einsum('bld,de->ble', value, Wv) + bv
        scores = jnp.einsum('bqe,bke->bqk', q, k)
        attn = jax.nn.softmax(scores, axis=-1)
        out = jnp.einsum('bqk,bke->bqe', attn, v)
        return out

    def _L0_ffn_ref(hidden_states, w_router, gate_up_proj, down_proj, w_gate, w_up, w_down):
        import jax, jax.numpy as jnp
        import numpy as np
        E = 16
        H = 256
        F = 512
        TOP_K = 1
        B, S = (2, 256)
        b, s, h = hidden_states.shape
        x = hidden_states.reshape(-1, h)
        logits = x @ w_router.T
        _, top_idx = jax.lax.top_k(logits, TOP_K)
        mask = jax.nn.one_hot(top_idx, E, dtype=logits.dtype).sum(axis=1)
        scores = jax.nn.sigmoid(logits) * mask
        masked_inputs = scores.T[:, :, None] * x[None, :, :]
        gate_up = jnp.einsum('eth,ehf->etf', masked_inputs, gate_up_proj)
        gate, up = jnp.split(gate_up, 2, axis=-1)
        expert_out = jnp.einsum('etf,efh->eth', up * jax.nn.silu(gate), down_proj)
        shared = jax.nn.silu(x @ w_gate.T) * (x @ w_up.T) @ w_down.T
        out = shared + expert_out.sum(axis=0)
        return out.reshape(b, s, h)

    def _L1_attn_ref(x, wq_w, wq_b, wk_w, wk_b, wv_w, wv_b, wo_w, wo_b):
        import jax, jax.numpy as jnp
        import numpy as np
        ROPE_BASE = 2500
        B, L, D, NH = (2, 512, 256, 16)
        HD = D // NH

        def apply_rope(inputs, positions, base_frequency):
            head_dim = inputs.shape[-1]
            fraction = 2 * jnp.arange(0, head_dim // 2) / head_dim
            timescale = base_frequency ** fraction
            sinusoid = positions[..., None] / timescale[None, None, :]
            sinusoid = sinusoid[..., None, :]
            sin, cos = (jnp.sin(sinusoid), jnp.cos(sinusoid))
            first, second = jnp.split(inputs, 2, axis=-1)
            out = jnp.concatenate([first * cos - second * sin, second * cos + first * sin], axis=-1)
            return out.astype(inputs.dtype)
        b, l, _ = x.shape
        q = (x @ wq_w + wq_b).reshape(b, l, NH, HD)
        k = (x @ wk_w + wk_b).reshape(b, l, NH, HD)
        v = (x @ wv_w + wv_b).reshape(b, l, NH, HD)
        pos = jnp.arange(l)
        q = apply_rope(q, pos, ROPE_BASE)
        k = apply_rope(k, pos, ROPE_BASE)
        q = q.transpose(0, 2, 1, 3)
        k = k.transpose(0, 2, 1, 3)
        v = v.transpose(0, 2, 1, 3)
        scale = jnp.sqrt(jnp.asarray(HD, q.dtype))
        scores = jnp.einsum('bnqh,bnkh->bnqk', q, k) / scale
        causal = jnp.tril(jnp.ones((l, l), bool))
        scores = jnp.where(causal, scores, jnp.finfo(scores.dtype).min)
        attn = jax.nn.softmax(scores, axis=-1)
        ctx = jnp.einsum('bnqk,bnkh->bnqh', attn, v)
        ctx = ctx.transpose(0, 2, 1, 3).reshape(b, l, D)
        return ctx @ wo_w + wo_b

    def _L1_xattn_ref(q, k, v, Wq, bq, Wk, bk, Wv, bv, Wo, bo):
        import jax, jax.numpy as jnp
        import numpy as np
        HEADS = 16
        D_MODEL = 256
        IMG_MODEL = 128
        D_K = D_MODEL // HEADS
        B, LQ, _ = q.shape
        LKV = k.shape[1]
        qh = (q @ Wq + bq).reshape(B, LQ, HEADS, D_K).transpose(0, 2, 1, 3)
        kh = (k @ Wk + bk).reshape(B, LKV, HEADS, D_K).transpose(0, 2, 1, 3)
        vh = (v @ Wv + bv).reshape(B, LKV, HEADS, D_K).transpose(0, 2, 1, 3)
        scale = 1.0 / np.sqrt(D_K)
        scores = jnp.einsum('bhqd,bhkd->bhqk', qh, kh) * scale
        attn = jax.nn.softmax(scores, axis=-1)
        out = jnp.einsum('bhqk,bhkd->bhqd', attn, vh)
        concat = out.transpose(0, 2, 1, 3).reshape(B, LQ, D_MODEL)
        return concat @ Wo + bo

    def _L1_ffn_ref(x, Wq, routers, leaf_keys, leaf_values, Wout_w, Wout_b):
        import jax, jax.numpy as jnp
        import numpy as np
        D_MODEL = 256
        DEPTH = 8
        M = 2 ** DEPTH
        N_INTERNAL = M - 1
        B, T = (8, 1024)

        def _leaf_probs(gate):
            BT = gate.shape[0]
            lp = jnp.ones((BT, M), dtype=gate.dtype)
            for level in range(DEPTH):
                n = 2 ** level
                half = M // (2 * n)
                g = gate[:, n - 1:2 * n - 1]
                f = jnp.stack([1.0 - g, g], axis=-1)
                f = jnp.broadcast_to(f[..., None], (BT, n, 2, half))
                lp = lp * f.reshape(BT, M)
            return lp
        Bv, Tv, d = x.shape
        q = jnp.einsum('btd,ed->bte', x, Wq)
        q_flat = q.reshape(Bv * Tv, d)
        gate = jax.nn.sigmoid(q_flat @ routers.T)
        leaf_prob = _leaf_probs(gate)
        ret = (leaf_prob @ leaf_values).reshape(Bv, Tv, d)
        return jnp.einsum('btd,ed->bte', ret, Wout_w) + Wout_b
    x = _layernorm(x + _L0_attn_ref(x, L0_attn_in_proj_weight, L0_attn_in_proj_bias, L0_attn_out_proj_weight, L0_attn_out_proj_bias), axis=-1)
    x = _layernorm(x + _L0_xattn_ref(x, ctx_512, ctx_512, L0_xattn_Wq, L0_xattn_bq, L0_xattn_Wk, L0_xattn_bk, L0_xattn_Wv, L0_xattn_bv), axis=-1)
    x = _layernorm(x + _L0_ffn_ref(x, L0_ffn_w_router, L0_ffn_gate_up_proj, L0_ffn_down_proj, L0_ffn_w_gate, L0_ffn_w_up, L0_ffn_w_down), axis=-1)
    x = _layernorm(x + _L1_attn_ref(x, L1_attn_wq_w, L1_attn_wq_b, L1_attn_wk_w, L1_attn_wk_b, L1_attn_wv_w, L1_attn_wv_b, L1_attn_wo_w, L1_attn_wo_b), axis=-1)
    x = _layernorm(x + _L1_xattn_ref(x, ctx_512, ctx_512, L1_xattn_Wq, L1_xattn_bq, L1_xattn_Wk, L1_xattn_bk, L1_xattn_Wv, L1_xattn_bv, L1_xattn_Wo, L1_xattn_bo), axis=-1)
    x = _layernorm(x + _L1_ffn_ref(x, L1_ffn_Wq, L1_ffn_routers, L1_ffn_leaf_keys, L1_ffn_leaf_values, L1_ffn_Wout_w, L1_ffn_Wout_b), axis=-1)
    return x

_drawn_inputs = setup_inputs


def setup_inputs(seed=0):
    import zlib

    import numpy as np

    out = dict(_drawn_inputs(seed))
    spreads = {'L0_attn_in_proj_bias': (0.0, 0.1),
     'L0_attn_out_proj_bias': (0.0, 0.1),
     'L0_xattn_bq': (0.0, 0.405),
     'L0_xattn_bk': (0.0, 0.8),
     'L0_xattn_bv': (0.0, 0.1),
     'L1_attn_wq_b': (0.0, 0.8),
     'L1_attn_wk_b': (0.0, 0.8),
     'L1_attn_wv_b': (0.0, 0.284),
     'L1_attn_wo_b': (0.0, 0.1),
     'L1_xattn_bq': (0.0, 0.409),
     'L1_xattn_bk': (0.0, 0.8),
     'L1_xattn_bv': (0.0, 0.1),
     'L1_xattn_bo': (0.0, 0.1)}
    factors = {'L0_ffn_w_router': 6.682,
     'L0_ffn_gate_up_proj': 6.383,
     'L0_ffn_down_proj': 6.393,
     'L0_ffn_w_gate': 2.686,
     'L0_ffn_w_up': 2.679,
     'L1_attn_wq_w': 8.0,
     'L1_attn_wk_w': 8.0,
     'L1_attn_wv_w': 2.978,
     'L1_ffn_Wq': 8.0,
     'L1_ffn_routers': 8.0,
     'L1_ffn_leaf_values': 8.0,
     'L1_ffn_Wout_w': 8.0,
     'L1_ffn_Wout_b': 2.727}
    for name, (base, spread) in spreads.items():
        noise = np.random.default_rng([zlib.crc32(name.encode()), seed]).standard_normal(out[name].shape)
        drawn = base * np.exp(spread * noise) if base else spread * noise
        out[name] = jnp.asarray(drawn.astype(out[name].dtype))
    for name, factor in factors.items():
        out[name] = (out[name] * factor).astype(out[name].dtype)
    return out
```

```python
from contextlib import ExitStack

import numpy as np

import concourse.bass as bass
from concourse import mybir

F32 = mybir.dt.float32
BF16 = mybir.dt.bfloat16
I32 = mybir.dt.int32
ALU = mybir.AluOpType
ACT = mybir.ActivationFunctionType
AX = mybir.AxisListType.X

P = 128
B, L, D = 4, 512, 256
N = B * L
T = N // P
TB = L // P
KD = D // P
H, HD = 16, 16
CTX, CD = 1601, 128
CT = -(-CTX // P)
E, F = 16, 512
FC = F // P
BANK = 512
EPS = 1e-5
SCALE = HD ** -0.5
G = 4
GROUPS = B * H // G
VW = 32
K_PARTS = (0, 1, 2, 0, 1, 0)
Q_PARTS = (0, 0, 0, 1, 1, 2)
QK_ROWS = HD * len(K_PARTS)
ETILES = N // P + E


def ctx_rows(kt):
    return min(P, CTX - kt * P)


class Env:
    pass


class Tail:
    def __init__(self, env, c, name, banks, tiles, kc, last=False):
        self.env, self.tiles, self.kc, self.last = env, tiles, kc, last
        self.cT_ps, self.pr_ps, self.xT_ps = (env.PS[:, b * BANK:(b + 2) * BANK] for b in banks)
        sb, sem = env.alloc(c)
        self.cT = sb(name + "_cT", [P, KD, TB * P], F32)
        self.r = sb(name + "_r", [P, TB, D], F32)
        self.st = sb(name + "_st", [P, TB, 6], F32)
        self.mv = sb(name + "_mv", [P, TB, 2], F32)
        self.ve = sb(name + "_ve", [P, TB], F32)
        self.rstd = sb(name + "_rstd", [P, TB], F32)
        self.s_cT_ps = sem(name + "_cT_ps")
        self.s_cT = sem(name + "_cT")
        self.s_proj = sem(name + "_proj")
        self.s_xb = sem(name + "_xb")
        self.s_r = sem(name + "_r")
        self.s_st = sem(name + "_st")
        self.s_mv = sem(name + "_mv")
        self.s_ve = sem(name + "_ve")
        self.s_rstd = sem(name + "_rstd")
        self.s_xn = sem(name + "_xn")
        self.s_xT_ps = sem(name + "_xT_ps")
        self.s_xT = sem(name + "_xT")

    def pool_residual(self, pool, c, add):
        x = self.env.x
        for t in self.tiles(c):
            last = pool.tensor_tensor(x[:, t, :], x[:, t, :], add(t), ALU.add)
        last.then_inc(self.s_xb, 1)

    def pe_in(self, pe, c, nat, ready):
        if c >= 1:
            pe.wait_ge(self.s_cT, c)
        for i in range(TB):
            ready(i)
            for k in range(KD):
                last = pe.transpose(self.cT_ps[:, k * BANK + i * P:k * BANK + (i + 1) * P],
                                    nat(i)[:, k * P:(k + 1) * P], self.env.ident)
        last.then_inc(self.s_cT_ps, 1)

    def act_in(self, act, c):
        act.wait_ge(self.s_cT_ps, c + 1)
        if c >= 1:
            act.wait_ge(self.s_proj, c)
        act.activation(self.cT[:, :, :].rearrange("p k n -> p (k n)"), self.cT_ps,
                       ACT.Copy).then_inc(self.s_cT, 1)

    def pe_proj(self, pe, c, w, lhs=None):
        if lhs is None:
            pe.wait_ge(self.s_cT, c + 1)
            lhs = lambda i, k: self.cT[:, k, i * P:(i + 1) * P]
        if c >= 1:
            pe.wait_ge(self.s_r, c)
        for i in range(TB):
            for k in range(self.kc):
                last = pe.matmul(self.pr_ps[:, i * D:(i + 1) * D], lhs(i, k), w(k),
                                 start=(k == 0), stop=(k == self.kc - 1))
        last.then_inc(self.s_proj, 1)

    def x_chunk(self, c):
        ts = self.tiles(c)
        return self.env.x[:, ts[0]:ts[-1] + 1:ts[1] - ts[0], :]

    def dve_sum(self, dve, c):
        dve.wait_ge(self.s_proj, c + 1)
        dve.wait_ge(self.s_xb, c + 1)
        if c >= 1:
            dve.wait_ge(self.s_xn, c)
        dve.tensor_tensor(self.r[:, :, :], self.pr_ps.rearrange("p (t n) -> p t n", t=TB),
                          self.x_chunk(c), ALU.add).then_inc(self.s_r, 1)

    def dve_norm(self, dve, c):
        dve.wait_ge(self.s_r, c + 1)
        for i in range(TB):
            dve.bn_stats(self.st[:, i, :], self.r[:, i, :]).then_inc(self.s_st, 1)
        dve.wait_ge(self.s_st, TB * (c + 1))
        for i in range(TB):
            last = dve.bn_aggr(self.mv[:, i, :], self.st[:, i, :])
        last.then_inc(self.s_mv, 1)
        dve.wait_ge(self.s_mv, c + 1)
        dve.tensor_scalar(self.ve[:, :], self.mv[:, :, 1], EPS, None, ALU.add).then_inc(self.s_ve, 1)
        dve.wait_ge(self.s_rstd, c + 1)
        if c >= 0:
            for i, t in enumerate(self.tiles(c)):
                last = dve.tensor_scalar(self.env.x[:, t, :], self.r[:, i, :], self.mv[:, i, 0:1],
                                         self.rstd[:, i:i + 1], ALU.subtract, ALU.mult)
            last.then_inc(self.s_xn, 1)

    def pool_rstd(self, pool, c):
        pool.wait_ge(self.s_ve, c + 1)
        pool.tensor_tensor(self.rstd[:, :], self.ve[:, :], self.env.mhalf, ALU.pow).then_inc(self.s_rstd, 1)

    def pe_out(self, pe, c):
        pe.wait_ge(self.s_xn, c + 1)
        if c >= 1:
            pe.wait_ge(self.s_xT, c)
        for i, t in enumerate(self.tiles(c)):
            for k in range(KD):
                last = pe.transpose(self.xT_ps[:, k * BANK + i * P:k * BANK + (i + 1) * P],
                                    self.env.x[:, t, k * P:(k + 1) * P], self.env.ident)
        last.then_inc(self.s_xT_ps, 1)

    def act_out(self, act, c):
        act.wait_ge(self.s_xT_ps, c + 1)
        ts = self.tiles(c)
        xT = self.env.xT[:, :, :].rearrange("p k (t n) -> p k t n", n=P)[:, :, ts[0]:ts[-1] + 1:ts[1] - ts[0], :]
        for k in range(KD):
            last = act.activation(xT[:, k], self.xT_ps[:, k * BANK:(k + 1) * BANK].rearrange("p (t n) -> p t n", n=P),
                                  ACT.Copy)
        last.then_inc(self.s_xT, 1)


class Split:

    def __init__(self, env, c, name, width, bias, dst, rope=None):
        self.env, self.width, self.bias, self.dst, self.rope = env, width, bias, dst, rope
        sb, sem = env.alloc(c)
        self.parts = sb(name + "_parts", [P, 2, 3, width], BF16)
        self.rest = sb(name + "_rest", [P, 2, width], F32)
        if rope:
            self.ta = sb(name + "_ta", [P, 2, width], F32)
            self.tb = sb(name + "_tb", [P, 2, width], F32)
            self.whole = sb(name + "_whole", [P, 2, width], F32)
        self.s_full = sem(name + "_full")
        self.s_rot = sem(name + "_rot")
        self.s_whole = sem(name + "_whole")
        self.s_hi = sem(name + "_hi")
        self.s_rest = sem(name + "_rest")
        self.s_mid = sem(name + "_mid")
        self.s_lo = sem(name + "_lo")
        self.s_out = [sem(f"{name}_out{u}") for u in range(2)]

    def freed(self, pe, n):
        pe.wait_ge(self.s_rot if self.rope else self.s_rest, n + 1)

    def act_hi(self, act, n, ps):
        u = n % 2
        if n >= 2:
            act.wait_ge(self.s_out[u], 48 * (n // 2))
        if self.rope:
            act.wait_ge(self.s_whole, n + 1)
            act.activation(self.parts[:, u, 0, :], self.whole[:, u, :], ACT.Copy).then_inc(self.s_hi, 1)
        else:
            act.wait_ge(self.s_full, n + 1)
            act.activation(self.parts[:, u, 0, :], ps, ACT.Identity, bias=self.bias(n)).then_inc(self.s_hi, 1)

    def act_mid(self, act, n):
        act.wait_ge(self.s_rest, n + 1)
        act.activation(self.parts[:, n % 2, 1, :], self.rest[:, n % 2, :], ACT.Copy).then_inc(self.s_mid, 1)

    def dve_rot(self, dve, n, ps_a, ps_b):
        u = n % 2
        ba, bb = self.bias(n)
        dve.wait_ge(self.s_full, n + 1)
        if n >= 2:
            dve.wait_ge(self.s_whole, n - 1)
        dve.scalar_tensor_tensor(self.ta[:, u, :], ps_a, ba, self.rope[0], ALU.add, ALU.mult)
        dve.scalar_tensor_tensor(self.tb[:, u, :], ps_b, bb, self.rope[1], ALU.add, ALU.mult).then_inc(self.s_rot, 1)

    def dve_rest(self, dve, n, ps=None):
        u = n % 2
        dve.wait_ge(self.s_hi, n + 1)
        if n >= 2:
            dve.wait_ge(self.s_lo, n - 1)
        if self.rope:
            dve.tensor_tensor(self.rest[:, u, :], self.whole[:, u, :], self.parts[:, u, 0, :],
                              ALU.subtract).then_inc(self.s_rest, 1)
        else:
            dve.scalar_tensor_tensor(self.rest[:, u, :], ps, self.bias(n), self.parts[:, u, 0, :],
                                     ALU.add, ALU.subtract).then_inc(self.s_rest, 1)

    def pool_whole(self, pool, n):
        u = n % 2
        pool.wait_ge(self.s_rot, n + 1)
        if n >= 2:
            pool.wait_ge(self.s_rest, n - 1)
        pool.tensor_tensor(self.whole[:, u, :], self.ta[:, u, :], self.tb[:, u, :], ALU.add).then_inc(self.s_whole, 1)

    def pool_lo(self, pool, n):
        u = n % 2
        pool.wait_ge(self.s_mid, n + 1)
        pool.tensor_tensor(self.parts[:, u, 2, :], self.rest[:, u, :], self.parts[:, u, 1, :],
                           ALU.subtract).then_inc(self.s_lo, 1)

    def sp_out(self, sp, n):
        sp.wait_ge(self.s_lo, n + 1)
        for j in range(3):
            sp.dma_start(self.dst(n, j), self.parts[:, n % 2, j, :]).then_inc(self.s_out[n % 2], 16)

    def sp_end(self, sp, blocks):
        for u in range(2):
            sp.wait_ge(self.s_out[u], 48 * ((blocks + 1 - u) // 2))


class Values:

    def __init__(self, env, c, name, items, bias, dst):
        self.env, self.items, self.bias, self.dst = env, items, bias, dst
        sb, sem = env.alloc(c)
        self.v = sb(name + "_v", [P, 2, 4, H * VW], F32)
        self.s_zero = sem(name + "_zero")
        self.s_ones = sem(name + "_ones")
        self.s_full = sem(name + "_vfull")
        self.s_v = sem(name + "_v")
        self.s_out = [sem(f"{name}_vout{u}") for u in range(2)]
        self.sent = [0, 0]
        self.sent_before = []
        for n, (b, kts, rows) in enumerate(items):
            self.sent_before.append(self.sent[n % 2])
            self.sent[n % 2] += 16 * len(kts)

    def pool_init(self, pool):
        v = self.v[:, :, :, :].rearrange("p u k n -> p (u k n)")
        pool.memset(v, 0.0).then_inc(self.s_zero, 1)
        pool.wait_ge(self.s_zero, 1)
        pool.memset(v.rearrange("p (h w) -> p h w", w=VW)[:, :, HD:HD + 1], 1.0).then_inc(self.s_ones, 1)

    def dve_copy(self, dve, n, ps):
        b, kts, rows = self.items[n]
        k = len(kts)
        if n == 0:
            dve.wait_ge(self.s_ones, 1)
        dve.wait_ge(self.s_full, n + 1)
        if n >= 2:
            dve.wait_ge(self.s_out[n % 2], self.sent_before[n])
        out = self.v[0:rows, n % 2, 0:k, :].rearrange("p k (h w) -> p (k h) w", w=VW)[:, :, 0:HD]
        src = ps[0:rows, 0:k * D].rearrange("p (k n) -> p k n", k=k)
        for i in range(k):
            last = dve.tensor_tensor(out[:, i * H:(i + 1) * H, :], src[:, i, :].rearrange("p (h d) -> p h d", d=HD),
                                     self.bias[0:rows, :].rearrange("p (h d) -> p h d", d=HD), ALU.add)
        last.then_inc(self.s_v, 1)

    def sp_out(self, sp, n):
        b, kts, rows = self.items[n]
        sp.wait_ge(self.s_v, n + 1)
        for i, kt in enumerate(kts):
            sp.dma_start(self.dst[b * G:(b + 1) * G, kt * P:kt * P + rows, :].rearrange("g p n -> p g n"),
                         self.v[0:rows, n % 2, i, :].rearrange("p (g n) -> p g n", g=G)).then_inc(self.s_out[n % 2], 16)

    def sp_end(self, sp):
        for u in range(2):
            sp.wait_ge(self.s_out[u], self.sent[u])


def ctx_prep(nc, env):
    w, PS = env.w, env.PS
    groups = [PS[:, 0:4 * BANK], PS[:, 4 * BANK:8 * BANK]]
    KB = B * KD
    vitems = [(b, kts, ctx_rows(kts[-1])) for b in range(B) for kts in ((0, 1, 2, 3), (4, 5, 6, 7), (8, 9, 10, 11), (12,))]
    with ExitStack() as c:
        sb, sem = env.alloc(c)
        sp_k = Split(env, c, "xk", CTX, lambda n: w["x_bk"][:, n % KD:n % KD + 1],
                     lambda n, j: env.kx[j, n * P:(n + 1) * P, :])
        val = Values(env, c, "xv", vitems, w["x_bv"], env.vx)
        s_c = [sem(f"ld_ctx{b}") for b in range(B)]
        s_x = sem("ld_x")
        s_const = sem("ld_const")
        s_w = sem("ld_w")
        s_xps = sem("x_ps")
        s_xT = sem("x_T")
        s_cps = sem("c_ps")
        s_cT = sem("c_T")
        s_zt = sem("zero_tile")
        s_zd = sem("zero_dram", keep=True)
        zt = sb("zt", [P, 8, D], F32)
        n_w = 0

        items = [("x", i) for i in range(B)] + [("c", b) for b in range(B)]
        for n in range(KB):
            items.append(("k", n))
            items += [("v", 2 * n), ("v", 2 * n + 1)]
        at = {it: groups[i % 2] for i, it in enumerate(items)}

        with nc.Block() as block:

            @block.sync
            def _(sp):
                sp.dma_start(env.cf[:, :], env.d["cf"]).then_inc(s_const, 16)
                sp.dma_start(env.x[:, :, :], env.d["x"].rearrange("(t p) n -> p t n", p=P)).then_inc(s_x, 16)
                for b in range(B):
                    sp.dma_start(env.ctx[:, b, 0:CT - 1, :],
                                 env.d["ctx"][b, 0:(CT - 1) * P, :].rearrange("(k p) n -> p k n", p=P)).then_inc(s_c[b], 16)
                    sp.dma_start(env.ctx[0:ctx_rows(CT - 1), b, CT - 1, :],
                                 env.d["ctx"][b, (CT - 1) * P:CTX, :]).then_inc(s_c[b], 16)
                for n in range(KB):
                    sp_k.sp_out(sp, n)
                    val.sp_out(sp, 2 * n)
                    val.sp_out(sp, 2 * n + 1)
                sp_k.sp_end(sp, KB)
                val.sp_end(sp)
                sp.wait_ge(s_zd, 16 * (ETILES // 8))

            @block.scalar
            def _(act):
                for dst, src in env.loads:
                    act.dma_start(dst, src).then_inc(s_w, 16)
                act.wait_ge(s_const, 16)
                act.activation(env.cb[:, :], env.cf[:, 0:3 * P], ACT.Copy)
                for i in range(B):
                    act.wait_ge(s_xps, i + 1)
                    act.activation(env.xT[:, :, i * L:(i + 1) * L],
                                   at["x", i][:, 0:KD * L].rearrange("p (k n) -> p k n", k=KD), ACT.Copy).then_inc(s_xT, 1)
                act.wait_ge(s_w, 16 * len(env.loads))
                for n in range(KB):
                    sp_k.act_hi(act, n, at["k", n][:, 0:CTX])
                    sp_k.act_mid(act, n)

            @block.gpsimd
            def _(pool):
                pool.memset(zt[:, :, :].rearrange("p a n -> p (a n)"), 0.0).then_inc(s_zt, 1)
                pool.memset(env.mhalf, -0.5)
                val.pool_init(pool)
                pool.wait_ge(s_zt, 1)
                for i in range(ETILES // 8):
                    pool.dma_start(env.xg[i * 8 * P:(i + 1) * 8 * P, :].rearrange("(a p) n -> p a n", p=P),
                                   zt[:, :, :]).then_inc(s_zd, 16)
                for n in range(KB):
                    sp_k.pool_lo(pool, n)

            @block.tensor
            def _(pe):
                def freed(it):
                    kind, n = it
                    if kind == "x":
                        pe.wait_ge(s_xT, n + 1)
                    elif kind == "c":
                        pe.wait_ge(s_cT, n + 1)
                    elif kind == "k":
                        sp_k.freed(pe, n)
                    else:
                        pe.wait_ge(val.s_v, n + 1)

                pe.wait_ge(s_const, 16)
                pe.wait_ge(s_x, 16)
                for i, it in enumerate(items):
                    kind, n = it
                    ps = at[it]
                    if i >= 2:
                        freed(items[i - 2])
                    if kind == "x":
                        for k in range(KD):
                            for j in range(TB):
                                last = pe.transpose(ps[:, k * L + j * P:k * L + (j + 1) * P],
                                                    env.x[:, n * TB + j, k * P:(k + 1) * P], env.ident)
                        last.then_inc(s_xps, 1)
                    elif kind == "c":
                        pe.wait_ge(s_c[n], 32)
                        for kt in range(CT):
                            r = ctx_rows(kt)
                            last = pe.transpose(ps[:, kt * P:kt * P + r], env.ctx[0:r, n, kt, :], env.ident[0:r, 0:r])
                        last.then_inc(s_cps, 1)
                    elif kind == "k":
                        if n == 0:
                            pe.wait_ge(s_w, 16 * len(env.loads))
                            pe.wait_ge(s_cT, B)
                        b, m = divmod(n, KD)
                        for q in range(0, CTX, BANK):
                            e = min(q + BANK, CTX)
                            last = pe.matmul(ps[:, q:e], w["x_wk"][:, m * P:(m + 1) * P],
                                             env.ctxT[:, b * CTX + q:b * CTX + e], start=True, stop=True)
                        last.then_inc(sp_k.s_full, 1)
                    else:
                        b, kts, rows = vitems[n]
                        for j, kt in enumerate(kts):
                            last = pe.matmul(ps[0:rows, j * D:(j + 1) * D],
                                             env.ctxT[:, b * CTX + kt * P:b * CTX + kt * P + rows], w["x_wv"],
                                             start=True, stop=True)
                        last.then_inc(val.s_full, 1)

            @block.vector
            def _(dve):
                for b in range(B):
                    dve.wait_ge(s_cps, b + 1)
                    dve.tensor_copy(env.ctxT[:, b * CTX:(b + 1) * CTX], at["c", b][:, 0:CTX]).then_inc(s_cT, 1)
                dve.wait_ge(s_w, 16 * len(env.loads))
                for n in range(KB):
                    sp_k.dve_rest(dve, n, at["k", n][:, 0:CTX])
                    for v in (2 * n, 2 * n + 1):
                        val.dve_copy(dve, v, at["v", v])


def l0_attn(nc, env):
    w, PS = env.w, env.PS
    W3 = 3 * D
    tiles = lambda c: [s * TB + c for s in range(B)]
    with ExitStack() as c_:
        sb, sem = env.alloc(c_)
        tail = Tail(env, c_, "t0", (2, 4, 6), tiles, KD)
        qkv = sb("qkv", [P, 2, B, W3], F32)
        prod = sb("prod", [P, 2, B, D], F32)
        half = sb("half", [P, 2, D], F32)
        sc = sb("sc", [P, B, B, H], F32)
        mx = sb("mx", [P, B, H], F32)
        ex = sb("ex", [P, B, B, H], F32)
        sm = sb("sm", [P, B, H], F32)
        rs = sb("rs", [P, B, H], F32)
        cx = sb("cx", [P, 2, B, D], F32)
        s_ps = sem("a0_ps")
        s_qkv = sem("a0_qkv")
        s_sh = sem("a0_shift")
        s_ex = sem("a0_exp")
        s_dve = sem("a0_dve")
        s_cx = sem("a0_cx")
        s_used = sem("a0_used")

        with nc.Block() as block:

            @block.tensor
            def _(pe):
                def project(c):
                    for s in range(B):
                        n = c * B + s
                        if n >= 1:
                            pe.wait_ge(s_qkv, n)
                        t = s * TB + c
                        for e in range(2):
                            o = PS[:, e * BANK:e * BANK + W3 // 2]
                            cols = slice(e * W3 // 2, (e + 1) * W3 // 2)
                            for k in range(KD):
                                pe.matmul(o, env.xT[:, k, t * P:(t + 1) * P], w["a0_in"][:, k, cols],
                                          start=(k == 0), stop=False)
                            last = pe.matmul(o, env.ones[0:1, :], w["a0_bin"][0:1, cols], start=False, stop=True)
                        last.then_inc(s_ps, 1)

                project(0)
                for c in range(TB):
                    if c + 1 < TB:
                        project(c + 1)
                    if c >= 1:
                        tail.pe_out(pe, c - 1)
                    tail.pe_in(pe, c, lambda i: cx[:, c % 2, i, :], lambda i: pe.wait_ge(s_cx, c + 1))
                    tail.pe_proj(pe, c, lambda k: w["a0_out"][:, k, :])
                tail.pe_out(pe, TB - 1)

            @block.scalar
            def _(act):
                def read(c):
                    for s in range(B):
                        act.wait_ge(s_ps, c * B + s + 1)
                        if c >= 2 and s == 0:
                            act.wait_ge(s_used, c - 1)
                        act.activation(qkv[:, c % 2, s, :].rearrange("p (e n) -> p e n", e=2),
                                       PS[:, 0:2 * BANK].rearrange("p (e n) -> p e n", e=2)[:, :, 0:W3 // 2],
                                       ACT.Copy).then_inc(s_qkv, 1)

                read(0)
                for c in range(TB):
                    if c + 1 < TB:
                        read(c + 1)
                    act.wait_ge(s_sh, c + 1)
                    act.activation(ex[:, :, :, :].rearrange("p a b h -> p (a b h)"),
                                   sc[:, :, :, :].rearrange("p a b h -> p (a b h)"), ACT.Exp,
                                   scale=SCALE).then_inc(s_ex, 1)
                    if c >= 1:
                        tail.act_out(act, c - 1)
                    tail.act_in(act, c)
                tail.act_out(act, TB - 1)

            @block.gpsimd
            def _(pool):
                for c in range(TB):
                    tail.pool_residual(pool, c, lambda t: w["a0_bout"])
                for c in range(TB):
                    tail.pool_rstd(pool, c)

            @block.vector
            def _(dve):
                steps = [0]

                def link(ins):
                    steps[0] += 1
                    ins.then_inc(s_dve, 1)
                    dve.wait_ge(s_dve, steps[0])

                def attend(c):
                    v5 = qkv[:, c % 2, :, :].rearrange("p s (h n) -> p s h n", n=3 * HD)
                    dve.wait_ge(s_qkv, B * (c + 1))
                    for s in range(B):
                        pr = prod[:, s % 2, :, :].rearrange("p t (h d) -> p t h d", d=HD)
                        link(dve.tensor_tensor(pr, v5[:, s, :, 0:HD].unsqueeze(1).to_broadcast([P, B, H, HD]),
                                               v5[:, :, :, HD:2 * HD], ALU.mult))
                        last = dve.tensor_reduce(sc[:, s, :, :].rearrange("p t h -> p (t h)"),
                                                 prod[:, s % 2, :, :].rearrange("p t (h d) -> p (t h) d", d=HD), AX, ALU.add)
                    link(last)
                    link(dve.tensor_reduce(mx[:, :, :], sc[:, :, :, :].rearrange("p s t h -> p s h t"), AX, ALU.max))
                    dve.tensor_tensor(sc[:, :, :, :], sc[:, :, :, :],
                                      mx[:, :, :].unsqueeze(2).to_broadcast([P, B, B, H]),
                                      ALU.subtract).then_inc(s_sh, 1)
                    if c >= 1:
                        tail.dve_sum(dve, c - 1)
                        tail.dve_norm(dve, c - 1)
                    dve.wait_ge(s_ex, c + 1)
                    link(dve.tensor_reduce(sm[:, :, :], ex[:, :, :, :].rearrange("p s t h -> p s h t"), AX, ALU.add))
                    link(dve.reciprocal(rs[:, :, :], sm[:, :, :]))
                    link(dve.tensor_tensor(ex[:, :, :, :], ex[:, :, :, :],
                                           rs[:, :, :].unsqueeze(2).to_broadcast([P, B, B, H]), ALU.mult))
                    if c >= 2:
                        dve.wait_ge(tail.s_cT_ps, c - 1)
                    for s in range(B):
                        pr = prod[:, s % 2, :, :].rearrange("p t (h d) -> p t h d", d=HD)
                        m = dve.tensor_tensor(pr, ex[:, s, :, :].unsqueeze(3).to_broadcast([P, B, H, HD]),
                                              v5[:, :, :, 2 * HD:3 * HD], ALU.mult)
                        if s == B - 1:
                            m.then_inc(s_used, 1)
                            dve.wait_ge(s_used, c + 1)
                        else:
                            link(m)
                        link(dve.tensor_tensor(half[:, :, :], prod[:, s % 2, 0:2, :], prod[:, s % 2, 2:4, :], ALU.add))
                        last = dve.tensor_tensor(cx[:, c % 2, s, :], half[:, 0, :], half[:, 1, :], ALU.add)
                    last.then_inc(s_cx, 1)

                for c in range(TB):
                    attend(c)
                tail.dve_sum(dve, TB - 1)
                tail.dve_norm(dve, TB - 1)


def l0_xattn(nc, env):
    w, PS = env.w, env.PS
    S_PS = PS[:, 0:4 * BANK]
    P_PS = PS[:, 4 * BANK:6 * BANK]
    M_PS = PS[:, 6 * BANK:7 * BANK]
    O_PS = PS[:, 7 * BANK:8 * BANK]
    with ExitStack() as c_:
        sb, sem = env.alloc(c_)
        qT = sb("qT", [P, KD, L], F32)
        qk = sb("qk", [P, L], F32)
        pr = sb("pr", [P, 2, CTX], F32)
        pT = sb("pT", [P, 2, CT, P], F32)
        zT = sb("zT", [P, 2, P], F32)
        mxs = sb("mxs", [P, T], F32)
        cq = sb("cq", [P, T], F32)
        top = sb("top", [P, T], F32)
        nb = sb("nb", [P, T], F32)
        rsum = sb("rsum", [P, T], F32)
        rinv = sb("rinv", [P, T], F32)
        r = sb("r0", [P, 2, D], F32)
        st = sb("st0", [P, 6], F32)
        mv = sb("mv0", [P, 2], F32)
        ve = sb("ve0", [P, 1], F32)
        rstd = sb("rstd0", [P, 1], F32)
        s_qps = sem("c0_qps")
        s_q = sem("c0_q")
        s_cps = sem("c0_cps")
        s_cq = sem("c0_cq")
        s_sps = sem("c0_sps")
        s_mx = sem("c0_mx")
        s_nb = sem("c0_nb")
        s_pr = sem("c0_pr")
        s_pps = sem("c0_pps")
        s_pTa = sem("c0_pTa")
        s_pTd = sem("c0_pTd")
        s_zps = sem("c0_zps")
        s_z = sem("c0_z")
        s_ops = sem("c0_ops")
        s_xb = sem("c0_xb")
        s_dve = sem("c0_dve")
        s_r = sem("c0_r")
        s_ve = sem("c0_ve")
        s_rstd = sem("c0_rstd")
        s_xn = sem("c0_xn")
        s_xps = sem("c0_xps")
        s_xT = sem("c0_xT")
        ROUNDS = ((0, 8), (8, CT))
        SPLIT = BANK // P

        with nc.Block() as block:

            @block.tensor
            def _(pe):
                def queries(b):
                    cols = slice(b * L, (b + 1) * L)
                    for m in range(KD):
                        if b or m:
                            pe.wait_ge(s_q, 3 * b + m)
                        if b and not m:
                            pe.wait_ge(s_z, TB * b)
                        for k in range(KD):
                            last = pe.matmul(M_PS, w["c0_wq"][:, k, m * P:(m + 1) * P], env.xT[:, k, cols],
                                             start=(k == 0), stop=(k == KD - 1))
                        last.then_inc(s_qps, 1)
                    pe.wait_ge(s_q, 3 * b + 2)
                    for m in range(KD):
                        last = pe.matmul(M_PS, w["c0_wkT"][:, m, :], qT[:, m, :], start=(m == 0), stop=(m == KD - 1))
                    last.then_inc(s_qps, 1)
                    if b:
                        pe.wait_ge(s_xT, TB * b)
                    for i in range(TB):
                        for m in range(KD):
                            last = pe.matmul(O_PS[:, i:i + 1], qT[:, m, i * P:(i + 1) * P], w["c0_bk"][:, m:m + 1],
                                             start=(m == 0), stop=(m == KD - 1))
                    last.then_inc(s_cps, 1)
                    pe.wait_ge(s_q, 3 * b + 3)

                def scores(t):
                    b, i = divmod(t, TB)
                    if t >= 1:
                        pe.wait_ge(s_pr, t)
                    for q in range(0, CTX, BANK):
                        e = min(q + BANK, CTX)
                        last = pe.matmul(S_PS[:, q:e], qk[:, i * P:(i + 1) * P],
                                         env.ctxT[:, b * CTX + q:b * CTX + e], start=True, stop=True)
                    last.then_inc(s_sps, 1)

                def rest(t):
                    b, i = divmod(t, TB)
                    pe.wait_ge(s_pr, t + 1)
                    for n, (k0, k1) in enumerate(ROUNDS):
                        if 2 * t + n >= 1:
                            pe.wait_ge(s_pTa, 2 * t + n)
                            pe.wait_ge(s_pTd, 2 * t + n)
                        for kt in range(k0, k1):
                            rows = ctx_rows(kt)
                            last = pe.transpose(P_PS[0:rows, (kt - k0) * P:(kt - k0 + 1) * P],
                                                pr[:, t % 2, kt * P:kt * P + rows], env.ident)
                        last.then_inc(s_pps, 1)
                    for n, (k0, k1) in enumerate(ROUNDS):
                        pe.wait_ge(s_pTa, 2 * t + n + 1)
                        pe.wait_ge(s_pTd, 2 * t + n + 1)
                        if n == 0 and t >= 1:
                            pe.wait_ge(s_z, t)
                        for kt in range(k0, k1):
                            rows = ctx_rows(kt)
                            last = pe.matmul(M_PS[:, 0:P], env.ctx[0:rows, b, kt, :], pT[0:rows, t % 2, kt, :],
                                             start=(kt == 0), stop=(kt == CT - 1))
                    last.then_inc(s_zps, 1)
                    if t % TB:
                        back(t - 1)
                    pe.wait_ge(s_z, t + 1)
                    if t == 0:
                        pe.wait_ge(s_cq, 1)
                    last = pe.matmul(O_PS[:, 0:D], zT[:, t % 2, :], w["c0_wv"], start=True, stop=True)
                    last.then_inc(s_ops, 1)

                def back(t):
                    pe.wait_ge(s_xn, t + 1)
                    for k in range(KD):
                        last = pe.transpose(O_PS[:, D + k * P:D + (k + 1) * P], env.x[:, t, k * P:(k + 1) * P], env.ident)
                    last.then_inc(s_xps, 1)
                    pe.wait_ge(s_xT, t + 1)

                for b in range(B):
                    queries(b)
                    scores(b * TB)
                    for t in range(b * TB, (b + 1) * TB):
                        if t % TB:
                            scores(t)
                            rest(t - 1)
                    rest((b + 1) * TB - 1)
                    back((b + 1) * TB - 1)

            @block.scalar
            def _(act):
                def tile_probs(t):
                    act.wait_ge(s_nb, t + 1)
                    if t >= 2:
                        act.wait_ge(s_pps, 2 * (t - 1))
                    act.activation(pr[:, t % 2, :], S_PS[:, 0:CTX], ACT.Exp, bias=nb[:, t:t + 1],
                                   accum_out=rsum[:, t:t + 1]).then_inc(s_pr, 1)

                def rest(t):
                    for n, (k0, k1) in enumerate(ROUNDS):
                        act.wait_ge(s_pps, 2 * t + n + 1)
                        if t >= 2 and n == 0:
                            act.wait_ge(s_zps, t - 1)
                        last = act.activation(pT[:, t % 2, k0:k0 + SPLIT, :].rearrange("p k n -> p (k n)"),
                                              P_PS[:, 0:BANK], ACT.Copy)
                        last.then_inc(s_pTa, 1)
                    act.wait_ge(s_zps, t + 1)
                    act.activation(zT[:, t % 2, :], M_PS[:, 0:P], ACT.Copy).then_inc(s_z, 1)

                def back(t):
                    act.wait_ge(s_xps, t + 1)
                    act.activation(env.xT[:, :, t * P:(t + 1) * P],
                                   O_PS[:, D:2 * D].rearrange("p (k n) -> p k n", k=KD), ACT.Copy).then_inc(s_xT, 1)

                for b in range(B):
                    for m in range(KD):
                        act.wait_ge(s_qps, 3 * b + m + 1)
                        act.activation(qT[:, m, :], M_PS, ACT.Identity, bias=w["c0_bq"][:, m:m + 1]).then_inc(s_q, 1)
                    act.wait_ge(s_qps, 3 * b + 3)
                    act.activation(qk[:, :], M_PS, ACT.Copy).then_inc(s_q, 1)
                    for t in range(b * TB, (b + 1) * TB):
                        tile_probs(t)
                        if t % TB:
                            rest_t = t - 1
                            rest(rest_t)
                            if rest_t >= 1 and rest_t % TB:
                                back(rest_t - 1)
                    rest((b + 1) * TB - 1)
                    back((b + 1) * TB - 2)
                    back((b + 1) * TB - 1)

            @block.gpsimd
            def _(pool):
                for t in range(T):
                    last = pool.tensor_tensor(env.x[:, t, :], env.x[:, t, :], w["c0_bv"], ALU.add)
                last.then_inc(s_xb, 1)
                for t in range(T):
                    pool.wait_ge(s_ve, t + 1)
                    pool.tensor_tensor(rstd[:, :], ve[:, :], env.mhalf[:, 0:1], ALU.pow).then_inc(s_rstd, 1)

            @block.vector
            def _(dve):
                steps = [0]

                def link(ins):
                    steps[0] += 1
                    ins.then_inc(s_dve, 1)
                    dve.wait_ge(s_dve, steps[0])

                def shift(t):
                    dve.wait_ge(s_sps, t + 1)
                    dve.tensor_reduce(mxs[:, t:t + 1], S_PS[:, 0:CTX], AX, ALU.max).then_inc(s_mx, 1)
                    dve.wait_ge(s_mx, t + 1)
                    link(dve.tensor_tensor(top[:, t:t + 1], mxs[:, t:t + 1], cq[:, t:t + 1], ALU.add))
                    dve.tensor_tensor(nb[:, t:t + 1], cq[:, t:t + 1], top[:, t:t + 1], ALU.subtract).then_inc(s_nb, 1)

                def probs_T(t):
                    for n, (k0, k1) in enumerate(ROUNDS):
                        dve.wait_ge(s_pps, 2 * t + n + 1)
                        if t >= 2 and n == 0:
                            dve.wait_ge(s_zps, t - 1)
                        rows = P if k1 < CT else ctx_rows(CT - 1)
                        last = dve.tensor_copy(pT[0:rows, t % 2, k0 + SPLIT:k1, :].rearrange("p k n -> p (k n)"),
                                               P_PS[0:rows, BANK:(k1 - k0) * P])
                        last.then_inc(s_pTd, 1)

                def norm(t):
                    link(dve.reciprocal(rinv[:, t:t + 1], rsum[:, t:t + 1]))
                    dve.wait_ge(s_ops, t + 1)
                    dve.scalar_tensor_tensor(r[:, t % 2, :], O_PS[:, 0:D], rinv[:, t:t + 1], env.x[:, t, :],
                                             ALU.mult, ALU.add).then_inc(s_r, 1)
                    dve.wait_ge(s_r, t + 1)
                    link(dve.bn_stats(st[:, :], r[:, t % 2, :]))
                    link(dve.bn_aggr(mv[:, :], st[:, :]))
                    dve.tensor_scalar(ve[:, :], mv[:, 1:2], EPS, None, ALU.add).then_inc(s_ve, 1)
                    dve.wait_ge(s_rstd, t + 1)
                    dve.tensor_scalar(env.x[:, t, :], r[:, t % 2, :], mv[:, 0:1], rstd[:, 0:1],
                                      ALU.subtract, ALU.mult).then_inc(s_xn, 1)

                dve.wait_ge(s_xb, 1)
                for b in range(B):
                    dve.wait_ge(s_cps, b + 1)
                    dve.tensor_copy(cq[:, b * TB:(b + 1) * TB], O_PS[:, 0:TB]).then_inc(s_cq, 1)
                    dve.wait_ge(s_cq, b + 1)
                    for t in range(b * TB, (b + 1) * TB):
                        shift(t)
                        if t % TB:
                            probs_T(t - 1)
                            norm(t - 1)
                    probs_T((b + 1) * TB - 1)
                    norm((b + 1) * TB - 1)


def l0_ffn(nc, env):
    w, PS = env.w, env.PS
    R = 3
    with ExitStack() as c_:
        sb, sem = env.alloc(c_)
        iota, thr, iota32 = env.iota16, env.thr16, env.iota32
        tiles = lambda c: list(range(c * TB, (c + 1) * TB))
        hT = sb("hT", [P, FC, N], F32)
        slot = sb("slot", [P, T], I32)
        xs = sb("xs", [P, T, D], F32)
        s_lps = sem("f_lps")
        s_dve = sem("f_dve")
        s_top = sem("f_top")
        s_ex = sem("f_exp")
        s_cnt = sem("f_cnt")
        s_rank = sem("f_rank")
        s_slot = sem("f_slot")
        s_tab = sem("f_tab")
        s_xs = sem("f_xs")
        s_scat = sem("f_scat", keep=True)
        s_sps = sem("f_sps")
        s_sg = sem("f_sg")
        s_sh = sem("f_sh")
        table = sb("table", [1, ETILES], I32)

        with ExitStack() as c2:
            sb2, _ = env.alloc(c2)
            lg = sb2("lg", [P, T, E], F32)
            top = sb2("top1", [P, T], F32)
            lt = sb2("lt", [P, T, E], F32)
            idx = sb2("idx", [P, T], F32)
            oh = sb2("oh", [P, T, E], F32)
            en = sb2("en", [P, T], F32)
            e1 = sb2("e1", [P, T], F32)
            sg = sb2("sgm", [P, T], F32)
            pre = sb2("pre", [P, T + 1, E], F32)
            nt3 = sb2("nt3", [P, E, E], F32)
            cs = sb2("cs", [P, 2, 2 * E], F32)
            nt = sb2("nt", [P, E], F32)
            st = sb2("st1", [P, E], F32)
            sbase = sb2("sbase", [P, E], F32)
            sf = sb2("sf", [P, T], F32)
            le = sb2("le", [1, ETILES, E], F32)
            tf = sb2("tf", [1, ETILES], F32)
            tf2 = sb2("tf2", [1, ETILES], F32)
            silu = sb2("silu", [P, 2, L], F32)
            items = [(c, f) for c in range(B) for f in range(FC)]

            with nc.Block() as block:

                @block.tensor
                def _(pe):
                    for t in range(T):
                        for k in range(KD):
                            last = pe.matmul(PS[:, t * E:(t + 1) * E], env.xT[:, k, t * P:(t + 1) * P],
                                             w["f_router"][:, k, :], start=(k == 0), stop=(k == KD - 1))
                    last.then_inc(s_lps, 1)

                    def shared(n):
                        c, f = items[n]
                        if n >= 2:
                            pe.wait_ge(s_sh, n - 1)
                        for e, name in enumerate(("f_wg", "f_wu")):
                            o = PS[:, (2 + 2 * (n % 2) + e) * BANK:(3 + 2 * (n % 2) + e) * BANK]
                            for k in range(KD):
                                last = pe.matmul(o, w[name][:, k, f * P:(f + 1) * P], env.xT[:, k, c * L:(c + 1) * L],
                                                 start=(k == 0), stop=(k == KD - 1))
                        last.then_inc(s_sps, 1)

                    for n in range(2):
                        shared(n)
                    pe.wait_ge(s_cnt, 1)
                    pe.matmul(PS[:, BANK:BANK + E], env.tri, pre[:, T, :], start=True, stop=True)
                    pe.matmul(PS[:, BANK + E:BANK + 2 * E], env.ones, pre[:, T, :], start=True,
                              stop=True).then_inc(s_rank, 1)
                    for n in range(2, len(items)):
                        shared(n)

                @block.scalar
                def _(act):
                    act.wait_ge(s_top, 1)
                    act.activation(en[:, :], top[:, :], ACT.Exp, scale=-1.0).then_inc(s_ex, 1)
                    for n in range(len(items)):
                        act.wait_ge(s_sps, n + 1)
                        if n >= 2:
                            act.wait_ge(s_sh, n - 1)
                        act.activation(silu[:, n % 2, :], PS[:, (2 + 2 * (n % 2)) * BANK:(3 + 2 * (n % 2)) * BANK],
                                       ACT.Silu).then_inc(s_sg, 1)

                @block.gpsimd
                def _(pool):
                    pool.wait_ge(s_slot, 1)
                    for t in range(T):
                        pool.wait_ge(s_xs, t + 1)
                        pool.indirect_dma_start(out=env.xg, out_offset=bass.IndirectOffsetOnAxis(ap=slot[:, t:t + 1], axis=0),
                                                in_=xs[:, t, :], in_offset=None).then_inc(s_scat, 16)
                    pool.wait_ge(s_scat, 16 * T)

                @block.vector
                def _(dve):
                    steps = [0]

                    def link(ins):
                        steps[0] += 1
                        ins.then_inc(s_dve, 1)
                        dve.wait_ge(s_dve, steps[0])

                    def shared(n):
                        c, f = items[n]
                        dve.wait_ge(s_sg, n + 1)
                        dve.tensor_tensor(hT[:, f, c * L:(c + 1) * L], silu[:, n % 2, :],
                                          PS[:, (3 + 2 * (n % 2)) * BANK:(4 + 2 * (n % 2)) * BANK],
                                          ALU.mult).then_inc(s_sh, 1)

                    te = lambda a: a.unsqueeze(2).to_broadcast([P, T, E])
                    ie = iota.unsqueeze(1).to_broadcast([P, T, E])
                    dve.wait_ge(s_lps, 1)
                    link(dve.tensor_copy(lg[:, :, :].rearrange("p t e -> p (t e)"), PS[:, 0:T * E]))
                    dve.tensor_reduce(top[:, :], lg[:, :, :], AX, ALU.max).then_inc(s_top, 1)
                    dve.wait_ge(s_top, 1)
                    link(dve.tensor_tensor(lt[:, :, :], lg[:, :, :], te(top[:, :]), ALU.is_lt))
                    link(dve.scalar_tensor_tensor(lg[:, :, :], lt[:, :, :], float(E), ie, ALU.mult, ALU.add))
                    link(dve.tensor_reduce(idx[:, :], lg[:, :, :], AX, ALU.min))
                    dve.memset(pre[:, 0, :], 0.0)
                    link(dve.tensor_tensor(oh[:, :, :], ie, te(idx[:, :]), ALU.is_equal))
                    for t in range(T):
                        ins = dve.tensor_tensor(pre[:, t + 1, :], pre[:, t, :], oh[:, t, :], ALU.add)
                        if t < T - 1:
                            link(ins)
                    ins.then_inc(s_cnt, 1)
                    dve.wait_ge(s_ex, 1)
                    link(dve.tensor_scalar(e1[:, :], en[:, :], 1.0, None, ALU.add))
                    link(dve.reciprocal(sg[:, :], e1[:, :]))
                    for t in range(T):
                        dve.tensor_scalar(xs[:, t, :], env.x[:, t, :], sg[:, t:t + 1], None, ALU.mult).then_inc(s_xs, 1)
                    link(dve.memset(cs[:, :, :], 0.0))
                    dve.wait_ge(s_rank, 1)
                    link(dve.tensor_tensor(nt3[:, :, :], PS[:, BANK + E:BANK + 2 * E].unsqueeze(2).to_broadcast([P, E, E]),
                                           thr.unsqueeze(1).to_broadcast([P, E, E]), ALU.is_gt))
                    link(dve.tensor_reduce(nt[:, :], nt3[:, :, :], AX, ALU.add))
                    link(dve.tensor_copy(cs[:, 0, E:2 * E], nt[:, :]))
                    for n in range(4):
                        a, b, d = n % 2, (n + 1) % 2, 1 << n
                        link(dve.tensor_tensor(cs[:, b, E:2 * E], cs[:, a, E:2 * E], cs[:, a, E - d:2 * E - d], ALU.add))
                    end = cs[:, 0, E:2 * E]
                    link(dve.tensor_tensor(st[:, :], end, nt[:, :], ALU.subtract))
                    link(dve.scalar_tensor_tensor(sbase[:, :], st[:, :], float(P), PS[:, BANK:BANK + E], ALU.mult, ALU.add))
                    link(dve.tensor_tensor(lt[:, :, :], pre[:, 0:T, :], sbase[:, :].unsqueeze(1).to_broadcast([P, T, E]), ALU.add))
                    link(dve.tensor_tensor(lg[:, :, :], lt[:, :, :], oh[:, :, :], ALU.mult))
                    link(dve.tensor_reduce(sf[:, :], lg[:, :, :], AX, ALU.add))
                    dve.tensor_copy(slot[:, :], sf[:, :]).then_inc(s_slot, 1)
                    link(dve.tensor_tensor(le[:, :, :], end[0:1, :].unsqueeze(1).to_broadcast([1, ETILES, E]),
                                           iota32[0:1, :].unsqueeze(2).to_broadcast([1, ETILES, E]), ALU.is_le))
                    link(dve.tensor_reduce(tf[:, :], le[:, :, :], AX, ALU.add))
                    link(dve.tensor_scalar(tf2[:, :], tf[:, :], float(E - 1), None, ALU.min))
                    dve.tensor_copy(table[:, :], tf2[:, :]).then_inc(s_tab, 1)
                    for n in range(len(items)):
                        shared(n)

        with ExitStack() as c2:
            sb2, sem2 = env.alloc(c2)
            wgu = sb2("wgu", [P, R, KD, 2 * F], F32)
            wdn = sb2("wdn", [P, R, FC, D], F32)
            xt = sb2("xt", [P, R, D], F32)
            xtT = sb2("xtT", [P, R, KD, P], F32)
            sgt = sb2("sgt", [P, R, F], F32)
            ht = sb2("ht", [P, R, FC, P], F32)
            yt = sb2("yt", [P, R, D], F32)
            s_ldx = [sem2(f"e_ldx{u}") for u in range(R)]
            s_ldw = [sem2(f"e_ldw{u}") for u in range(R)]
            s_tps = sem2("e_tps")
            s_t = sem2("e_t")
            s_gu = sem2("e_gu")
            s_g = sem2("e_g")
            s_h = sem2("e_h")
            s_yps = sem2("e_yps")
            s_y = sem2("e_y")
            s_yo = [sem2(f"e_yo{u}", keep=True) for u in range(R)]
            GU = lambda u: PS[:, 2 * u * BANK:2 * (u + 1) * BANK]
            T_PS, Y_PS = PS[:, 6 * BANK:7 * BANK], PS[:, 7 * BANK:8 * BANK]
            LAST = ETILES - 1
            ROUNDS = (ETILES - 2) // R

            with nc.Block() as block:

                @block.sync
                def _(sp):
                    def load(j, u):
                        e = sp.value_load(table[0:1, bass.ds(j, 1)], min_val=0, max_val=E - 1)
                        sp.dma_start(xt[:, u, :], env.xg_t[j]).then_inc(s_ldx[u], 16)
                        sp.dma_start(wgu[:, u, :, :], env.gu_t[e].rearrange("(k p) n -> p k n", p=P)).then_inc(s_ldw[u], 16)
                        sp.dma_start(wdn[:, u, :, :], env.dn_t[e].rearrange("(k p) n -> p k n", p=P)).then_inc(s_ldw[u], 16)

                    for j in range(R):
                        load(j, j)
                    with sp.Fori(0, (ETILES - R) // R) as i:
                        for u in range(R):
                            sp.wait_ge(s_yps, i * R + u + 1)
                            load(i * R + u + R, u)
                    for j in range(R + (ETILES - R) // R * R, ETILES):
                        sp.wait_ge(s_yps, j - R + 1)
                        load(j, j % R)

                @block.tensor
                def _(pe):
                    def turn(j, u, n):
                        pe.wait_ge(s_ldx[u], 16 * (n + 1))
                        pe.wait_ge(s_t, j + 1)
                        for k in range(KD):
                            last = pe.transpose(T_PS[:, k * P:(k + 1) * P], xt[:, u, k * P:(k + 1) * P], env.ident)
                        last.then_inc(s_tps, 1)

                    def gate_up(j, u, n):
                        pe.wait_ge(s_ldw[u], 32 * (n + 1))
                        pe.wait_ge(s_t, j + 2)
                        for f in range(2 * FC):
                            for k in range(KD):
                                last = pe.matmul(GU(u)[:, f * P:(f + 1) * P], wgu[:, u, k, f * P:(f + 1) * P],
                                                 xtT[:, u, k, :], start=(k == 0), stop=(k == KD - 1))
                        last.then_inc(s_gu, 1)

                    def down(j, u):
                        pe.wait_ge(s_h, j + 1)
                        pe.wait_ge(s_y, j + 1)
                        for f in range(FC):
                            last = pe.matmul(Y_PS[:, 0:D], ht[:, u, f, :], wdn[:, u, f, :],
                                             start=(f == 0), stop=(f == FC - 1))
                        last.then_inc(s_yps, 1)

                    turn(0, 0, 0)
                    gate_up(0, 0, 0)
                    turn(1, 1, 0)
                    with pe.Fori(0, ROUNDS) as i:
                        for m in range(R):
                            j = i * R + (m + 1)
                            gate_up(j, (m + 1) % R, i + (m + 1) // R)
                            turn(j + 1, (m + 2) % R, i + (m + 2) // R)
                            down(j - 1, m)
                    gate_up(LAST, LAST % R, LAST // R)
                    down(LAST - 1, (LAST - 1) % R)
                    down(LAST, LAST % R)

                @block.scalar
                def _(act):
                    def turn(j, u):
                        act.wait_ge(s_tps, j + 1)
                        act.activation(xtT[:, u, :, :].rearrange("p k n -> p (k n)"), T_PS[:, 0:D], ACT.Copy).then_inc(s_t, 1)

                    def gate(j, u):
                        act.wait_ge(s_gu, j + 1)
                        act.activation(sgt[:, u, :], GU(u)[:, 0:F], ACT.Silu).then_inc(s_g, 1)

                    act.sem_inc(s_t, 1)
                    turn(0, 0)
                    gate(0, 0)
                    turn(1, 1)
                    with act.Fori(0, ROUNDS) as i:
                        for m in range(R):
                            j = i * R + (m + 1)
                            gate(j, (m + 1) % R)
                            turn(j + 1, (m + 2) % R)
                    gate(LAST, LAST % R)

                @block.vector
                def _(dve):
                    def hidden(j, u):
                        dve.wait_ge(s_g, j + 1)
                        dve.tensor_tensor(ht[:, u, :, :].rearrange("p f n -> p (f n)"), sgt[:, u, :],
                                          GU(u)[:, F:2 * F], ALU.mult).then_inc(s_h, 1)

                    def out(j, u, n):
                        dve.wait_ge(s_yps, j + 1)
                        if n is not None:
                            dve.wait_ge(s_yo[u], 16 * n)
                        dve.tensor_copy(yt[:, u, :], Y_PS[:, 0:D]).then_inc(s_y, 1)

                    dve.sem_inc(s_y, 1)
                    hidden(0, 0)
                    for j in range(1, R + 1):
                        hidden(j, j % R)
                        out(j - 1, j - 1, None)
                    with dve.Fori(1, ROUNDS) as i:
                        for m in range(R):
                            j = i * R + (m + 1)
                            hidden(j, (m + 1) % R)
                            out(j - 1, m, i)
                    hidden(LAST, LAST % R)
                    out(LAST - 1, (LAST - 1) % R, (LAST - 1) // R)
                    out(LAST, LAST % R, LAST // R)

                @block.gpsimd
                def _(pool):
                    def out(j, u):
                        pool.wait_ge(s_y, j + 2)
                        pool.dma_start(env.yg_t[j], yt[:, u, :]).then_inc(s_yo[u], 16)

                    with pool.Fori(0, ETILES // R) as i:
                        for u in range(R):
                            out(i * R + u, u)
                    for j in range(ETILES // R * R, ETILES):
                        out(j, j % R)
                    for u in range(R):
                        pool.wait_ge(s_yo[u], 16 * ((ETILES - u + R - 1) // R))

        with ExitStack() as c2:
            _, sem2 = env.alloc(c2)
            tail = Tail(env, c2, "t2", (0, 2, 4), tiles, FC)
            s_ga = [sem2(f"f_ga{c}", keep=True) for c in range(B)]

            with nc.Block() as block:

                @block.gpsimd
                def _(pool):
                    for t in range(T):
                        pool.indirect_dma_start(out=xs[:, t, :], out_offset=None, in_=env.yg,
                                                in_offset=bass.IndirectOffsetOnAxis(ap=slot[:, t:t + 1], axis=0)
                                                ).then_inc(s_ga[t // TB], 16)
                    for c in range(B):
                        pool.wait_ge(s_ga[c], 16 * TB)
                        tail.pool_residual(pool, c, lambda t: xs[:, t, :])
                    for c in range(B):
                        tail.pool_rstd(pool, c)

                @block.tensor
                def _(pe):
                    for c in range(B):
                        tail.pe_proj(pe, c, lambda k: w["f_wd"][:, k, :],
                                     lambda i, k: hT[:, k, (c * TB + i) * P:(c * TB + i + 1) * P])
                        if c >= 1:
                            tail.pe_out(pe, c - 1)
                    tail.pe_out(pe, B - 1)

                @block.scalar
                def _(act):
                    for c in range(B):
                        tail.act_out(act, c)

                @block.vector
                def _(dve):
                    for c in range(B):
                        tail.dve_sum(dve, c)
                        tail.dve_norm(dve, c)


def l1_attn_prep(nc, env):
    w, PS = env.w, env.PS
    blocks = [(b, m, name) for b in range(B) for m in range(KD) for name in ("q", "k")]
    vitems = [(b, tuple(range(TB)), P) for b in range(B)]
    with ExitStack() as c:
        def bias(n):
            b, m, name = blocks[n]
            return w["s_b" + name][:, m:m + 1], w["s_b" + name + "s"][:, m:m + 1]

        def dst(n, j):
            b, m, name = blocks[n]
            return (env.qs if name == "q" else env.ks)[j, b * D + m * P:b * D + (m + 1) * P, :]

        sp_ = Split(env, c, "sqk", L, bias, dst, rope=(env.cos, env.sin))
        val = Values(env, c, "sv", vitems, w["s_bv"], env.vs)
        QK = lambda n: PS[:, 2 * (n % 3) * BANK:2 * (n % 3 + 1) * BANK]
        V = PS[:, 6 * BANK:8 * BANK]
        PER = len(blocks) // B

        with nc.Block() as block:

            @block.tensor
            def _(pe):
                for n, (b, m, name) in enumerate(blocks):
                    if n >= 3:
                        sp_.freed(pe, n - 3)
                    for e, wn in enumerate(("s_w" + name, "s_w" + name + "s")):
                        for k in range(KD):
                            last = pe.matmul(QK(n)[:, e * L:(e + 1) * L], w[wn][:, k, m * P:(m + 1) * P],
                                             env.xT[:, k, b * L:(b + 1) * L], start=(k == 0), stop=(k == KD - 1))
                    last.then_inc(sp_.s_full, 1)
                    if n % PER == PER - 1:
                        if b >= 1:
                            pe.wait_ge(val.s_v, b)
                        for j in range(TB):
                            t = b * TB + j
                            for k in range(KD):
                                last = pe.matmul(V[:, j * D:(j + 1) * D], env.xT[:, k, t * P:(t + 1) * P],
                                                 w["s_wv"][:, k, :], start=(k == 0), stop=(k == KD - 1))
                        last.then_inc(val.s_full, 1)

            @block.scalar
            def _(act):
                for n in range(len(blocks) + 1):
                    if n < len(blocks):
                        sp_.act_hi(act, n, None)
                    if n >= 1:
                        sp_.act_mid(act, n - 1)

            @block.vector
            def _(dve):
                for n in range(len(blocks) + 1):
                    if n < len(blocks):
                        sp_.dve_rot(dve, n, QK(n)[:, 0:L], QK(n)[:, L:2 * L])
                    if n >= 1:
                        sp_.dve_rest(dve, n - 1)
                        if (n - 1) % PER == PER - 1:
                            val.dve_copy(dve, (n - 1) // PER, V)

            @block.gpsimd
            def _(pool):
                val.pool_init(pool)
                for n in range(len(blocks) + 1):
                    if n < len(blocks):
                        sp_.pool_whole(pool, n)
                    if n >= 1:
                        sp_.pool_lo(pool, n - 1)

            @block.sync
            def _(sp):
                for n in range(len(blocks)):
                    sp_.sp_out(sp, n)
                    if n % PER == PER - 1:
                        val.sp_out(sp, n // PER)
                sp_.sp_end(sp, len(blocks))
                val.sp_end(sp)


def l1_xattn_prep(nc, env):
    w, PS = env.w, env.PS
    NB = B * KD
    with ExitStack() as c:
        sp_ = Split(env, c, "xq", L, lambda n: w["x_bq"][:, n % KD:n % KD + 1],
                    lambda n, j: env.qx[j, n * P:(n + 1) * P, :])
        Q = lambda n: PS[:, (n % 4) * BANK:(n % 4 + 1) * BANK]

        with nc.Block() as block:

            @block.tensor
            def _(pe):
                for n in range(NB):
                    b, m = divmod(n, KD)
                    if n >= 4:
                        sp_.freed(pe, n - 4)
                    for k in range(KD):
                        last = pe.matmul(Q(n), w["x_wq"][:, k, m * P:(m + 1) * P], env.xT[:, k, b * L:(b + 1) * L],
                                         start=(k == 0), stop=(k == KD - 1))
                    last.then_inc(sp_.s_full, 1)

            @block.scalar
            def _(act):
                for n in range(NB + 1):
                    if n < NB:
                        sp_.act_hi(act, n, Q(n))
                    if n >= 1:
                        sp_.act_mid(act, n - 1)

            @block.vector
            def _(dve):
                for n in range(NB):
                    sp_.dve_rest(dve, n, Q(n))

            @block.gpsimd
            def _(pool):
                for n in range(NB):
                    sp_.pool_lo(pool, n)

            @block.sync
            def _(sp):
                for n in range(NB):
                    sp_.sp_out(sp, n)
                sp_.sp_end(sp, NB)


def heads_loop(nc, env, name, NK, causal, qp, kp, vp, OT):
    PS = env.PS
    KT = -(-NK // P)
    R = 3
    STEPS = KT * G
    rows = lambda kt: min(P, NK - kt * P)
    q0 = lambda kt: kt * P if causal else 0
    HALF = 2 * BANK
    if causal:
        units = [(h, pair) for h in range(G) for pair in range(TB // 2)]
    else:
        units = [(h, qt, e) for h in range(G) for qt in range(TB) for e in range(2)]
    U = len(units)
    M_UNITS = 2
    LOADS = 2 * len(K_PARTS)
    VLOADS = 1 if NK % P == 0 else 2
    LASTG = GROUPS - 1
    ROUNDS = LASTG // R
    assert ROUNDS * R == LASTG and U % 2 == 0

    with ExitStack() as c:
        sb, sem = env.alloc(c)
        Kst = sb(name + "_K", [P, R, G, NK], BF16)
        Qst = sb(name + "_Q", [P, R, G, L], BF16)
        Vg = sb(name + "_V", [P, R, KT, G * VW], F32)
        Pr = sb(name + "_P", [P, R, G, L], F32)
        part = sb(name + "_part", [P, G * TB, 1 if causal else 2], F32)
        mx = sb(name + "_mx", [P, G * TB], F32)
        mh = sb(name + "_mh", [P, G * TB, 2], BF16)
        s_ones = sem(name + "_ones")
        s_kq = [sem(f"{name}_kq{u}") for u in range(R)]
        s_v = [sem(f"{name}_v{u}") for u in range(R)]
        s_1 = sem(name + "_1")
        s_1free = sem(name + "_1free")
        s_step = sem(name + "_step")
        s_mh = sem(name + "_mh")
        s_m = sem(name + "_m")
        s_mrow = sem(name + "_mrow")
        s_2 = sem(name + "_2")
        s_exp = sem(name + "_exp")
        s_pv = sem(name + "_pv")
        s_ot = sem(name + "_ot")
        ring1 = lambda n: PS[:, (n % 2) * HALF:(n % 2 + 1) * HALF]
        ring2 = lambda n: PS[:, (4 + n % R) * BANK:(5 + n % R) * BANK]
        O_PS = PS[:, 7 * BANK:8 * BANK]
        ONE = QK_ROWS

        with nc.Block() as block:

            @block.sync
            def _(sp):
                def load(g, u):
                    for j, (pk, pq) in enumerate(zip(K_PARTS, Q_PARTS)):
                        r = slice(j * HD, (j + 1) * HD)
                        sp.dma_start(Kst[r, u, :, :], kp[pk][g].rearrange("(h d) n -> d h n", d=HD)).then_inc(s_kq[u], 16)
                        sp.dma_start(Qst[r, u, :, :], qp[pq][g].rearrange("(h d) n -> d h n", d=HD)).then_inc(s_kq[u], 16)
                    full = NK // P
                    sp.dma_start(Vg[:, u, 0:full, :], vp[g][0:full * P, :].rearrange("(k p) n -> p k n", p=P)).then_inc(s_v[u], 16)
                    if full < KT:
                        sp.dma_start(Vg[0:rows(full), u, full, :], vp[g][full * P:NK, :]).then_inc(s_v[u], 16)

                for g in range(R):
                    load(g, g)
                n = (GROUPS - R) // R
                with sp.Fori(0, n) as i:
                    for u in range(R):
                        sp.wait_ge(s_pv, R + (i * R + (u + 1)) * KT)
                        load(i * R + (u + R), u)
                for g in range(R + n * R, GROUPS):
                    sp.wait_ge(s_pv, R + (g - R + 1) * KT)
                    load(g, g % R)

            @block.gpsimd
            def _(pool):
                for u in range(R):
                    last = pool.memset(Kst[ONE:P, u, :, :].rearrange("p h n -> p (h n)"), 1.0)
                last.then_inc(s_ones, 1)

            @block.tensor
            def _(pe):
                def unit(g, u, n, first):
                    if n == 0:
                        pe.wait_ge(s_kq[u], 16 * LOADS * (first + 1))
                    if n >= 2:
                        pe.wait_ge(s_1free, g * U + (n - 1))
                    o = ring1(n)
                    q = lambda h, qt: Qst[0:QK_ROWS, u, h, qt * P:(qt + 1) * P]
                    if causal:
                        h, pair = units[n]
                        for e in range(2):
                            qt = 2 * pair + e
                            w_ = (qt + 1) * P
                            pe.matmul(o[:, e * BANK:e * BANK + w_], q(h, qt), Kst[0:QK_ROWS, u, h, 0:w_], start=True, stop=False)
                            last = pe.matmul(o[:, e * BANK + w_ - P:e * BANK + w_], env.identb, env.mask_q, start=False, stop=True)
                    else:
                        h, qt, e = units[n]
                        for k in range(e * HALF, min((e + 1) * HALF, NK), BANK):
                            w_ = min(BANK, NK - k)
                            last = pe.matmul(o[:, k - e * HALF:k - e * HALF + w_], q(h, qt), Kst[0:QK_ROWS, u, h, k:k + w_],
                                             start=True, stop=True)
                    last.then_inc(s_1, 1)

                def rows_of_maxima(g, u):
                    pe.wait_ge(s_mh, g + 1)
                    for n in range(M_UNITS):
                        for h2 in range(G // M_UNITS):
                            for qt in range(TB):
                                col = (n * (G // M_UNITS) + h2) * TB + qt
                                last = pe.matmul(ring1(n)[ONE:ONE + 2, h2 * BANK + qt * P:h2 * BANK + (qt + 1) * P],
                                                 mh[:, col, :], env.identb, start=True, stop=True, tile_position=(0, ONE))
                        last.then_inc(s_m, 1)

                def score(g, u, kt, h):
                    n = kt * G + h
                    if n == 0:
                        pe.wait_ge(s_mrow, (g + 1) * M_UNITS)
                    if n >= R:
                        pe.wait_ge(s_exp, g * STEPS + (n - R + 1))
                    o = ring2(u * STEPS + n)
                    r = rows(kt)
                    w_ = L - q0(kt)
                    last = pe.matmul(o[0:r, 0:w_], Kst[0:ONE + 2, u, h, kt * P:kt * P + r], Qst[0:ONE + 2, u, h, q0(kt):L],
                                     start=True, stop=not causal)
                    if causal:
                        last = pe.matmul(o[0:r, 0:P], env.identb, env.mask_k, start=False, stop=True)
                    last.then_inc(s_2, 1)

                def values(g, u, kt, first):
                    r = rows(kt)
                    if kt == 0:
                        pe.wait_ge(s_v[u], 16 * VLOADS * (first + 1))
                        pe.wait_ge(s_ot, g + 1)
                    pe.wait_ge(s_exp, g * STEPS + (kt + 1) * G)
                    for h in range(G):
                        last = pe.matmul(O_PS[h * VW:(h + 1) * VW, q0(kt):L], Vg[0:r, u, kt, h * VW:(h + 1) * VW],
                                         Pr[0:r, (u * KT + kt) % R, h, 0:L - q0(kt)],
                                         start=(kt == 0), stop=(kt == KT - 1), tile_position=(0, h * VW))
                    last.then_inc(s_pv, 1)

                def group(g, u, first, nxt):
                    done = 0
                    for kt in range(KT):
                        for h in range(G):
                            score(g, u, kt, h)
                            want = min(U, -(-U * (kt * G + h + 1) // (STEPS - 3))) if nxt else 0
                            while done < want:
                                unit(g + 1, (u + 1) % R, done, first + (u + 1) // R)
                                done += 1
                        if kt >= 1:
                            values(g, u, kt - 1, first)
                    values(g, u, KT - 1, first)
                    if nxt:
                        rows_of_maxima(g + 1, (u + 1) % R)

                pe.wait_ge(s_ones, 1)
                for n in range(U):
                    unit(0, 0, n, 0)
                rows_of_maxima(0, 0)
                with pe.Fori(0, ROUNDS) as i:
                    for u in range(R):
                        group(i * R + u, u, i, True)
                group(LASTG, LASTG % R, LASTG // R, False)

            @block.scalar
            def _(act):
                def mrows(g, u):
                    for n in range(M_UNITS):
                        act.wait_ge(s_m, g * M_UNITS + (n + 1))
                        w_ = G // M_UNITS
                        act.activation(Qst[ONE:ONE + 2, u, n * w_:(n + 1) * w_, :].rearrange("p h n -> p (h n)"),
                                       ring1(n)[ONE:ONE + 2, :], ACT.Copy).then_inc(s_mrow, 1)

                def group(g, u, nxt):
                    for kt in range(KT):
                        act.wait_ge(s_pv, g * KT + (kt + 1))
                        r = rows(kt)
                        w_ = L - q0(kt)
                        for h in range(G):
                            n = kt * G + h
                            act.wait_ge(s_2, g * STEPS + (n + 1))
                            act.activation(Pr[0:r, (u * KT + kt) % R, h, 0:w_], ring2(u * STEPS + n)[0:r, 0:w_],
                                           ACT.Exp, scale=SCALE).then_inc(s_exp, 1)
                    act.wait_ge(s_pv, R + (g + 1) * KT)
                    act.activation(OT[:, bass.ds(g, 1), :].rearrange("p g n -> p (g n)"), O_PS, ACT.Copy).then_inc(s_ot, 1)
                    if nxt:
                        mrows(g + 1, (u + 1) % R)

                act.sem_inc(s_pv, R)
                act.sem_inc(s_ot, 1)
                mrows(0, 0)
                with act.Fori(0, ROUNDS) as i:
                    for u in range(R):
                        group(i * R + u, u, True)
                group(LASTG, LASTG % R, False)

            @block.vector
            def _(dve):
                def maxima(g):
                    for n in range(U):
                        dve.wait_ge(s_1, g * U + (n + 1))
                        o = ring1(n)
                        if causal:
                            h, pair = units[n]
                            for e in range(2):
                                qt = 2 * pair + e
                                last = dve.tensor_reduce(part[:, h * TB + qt, :], o[:, e * BANK:e * BANK + (qt + 1) * P], AX, ALU.max)
                        else:
                            h, qt, e = units[n]
                            w_ = min(HALF, NK - e * HALF)
                            last = dve.tensor_reduce(part[:, h * TB + qt, e:e + 1], o[:, 0:w_], AX, ALU.max)
                        last.then_inc(s_1free, 1)
                    dve.wait_ge(s_1free, g * U + U)
                    dve.tensor_reduce(mx[:, :], part[:, :, :], AX, ALU.max).then_inc(s_step, 1)
                    dve.wait_ge(s_step, g * 2 + 1)
                    dve.wait_ge(s_m, g * M_UNITS)
                    dve.tensor_scalar(mh[:, :, 0], mx[:, :], -1.0, None, ALU.mult).then_inc(s_step, 1)
                    dve.wait_ge(s_step, g * 2 + 2)
                    dve.scalar_tensor_tensor(mh[:, :, 1], mx[:, :], -1.0, mh[:, :, 0], ALU.mult, ALU.subtract).then_inc(s_mh, 1)

                maxima(0)
                with dve.Fori(1, GROUPS) as g:
                    maxima(g)


def heads_tail(nc, env, name, OT, wo, bo):
    w, PS = env.w, env.PS
    tiles = lambda c: list(range(c * TB, (c + 1) * TB))
    HW = G * VW
    with ExitStack() as c_:
        sb, sem = env.alloc(c_)
        tail = Tail(env, c_, name, (2, 4, 6), tiles, KD)
        rc = sb(name + "_rc", [P, 2, H], F32)
        cx = sb(name + "_cx", [P, 2, TB, D], F32)
        s_ops = sem(name + "_ops")
        s_rc = sem(name + "_rc")
        s_cx = sem(name + "_cx")

        with nc.Block() as block:

            @block.tensor
            def _(pe):
                def by_query(c):
                    for i in range(TB):
                        t = c * TB + i
                        if t >= 2:
                            pe.wait_ge(s_cx, t - 1)
                        for g in range(G):
                            last = pe.transpose(PS[:, (t % 2) * BANK + g * P:(t % 2) * BANK + (g + 1) * P],
                                                OT[:, c * G + g, i * P:(i + 1) * P], env.ident)
                        last.then_inc(s_ops, 1)

                for c in range(B):
                    by_query(c)
                    tail.pe_in(pe, c, lambda i: cx[:, c % 2, i, :], lambda i: pe.wait_ge(s_cx, c * TB + i + 1))
                    tail.pe_proj(pe, c, lambda k: wo[:, k, :])
                    if c >= 1:
                        tail.pe_out(pe, c - 1)
                tail.pe_out(pe, B - 1)

            @block.scalar
            def _(act):
                for c in range(B):
                    tail.act_in(act, c)
                    if c >= 1:
                        tail.act_out(act, c - 1)
                tail.act_out(act, B - 1)

            @block.gpsimd
            def _(pool):
                for c in range(B):
                    tail.pool_residual(pool, c, lambda t: bo)
                for c in range(B):
                    tail.pool_rstd(pool, c)

            @block.vector
            def _(dve):
                def context(c):
                    if c >= 2:
                        dve.wait_ge(tail.s_cT_ps, c - 1)
                    for i in range(TB):
                        t = c * TB + i
                        o = PS[:, (t % 2) * BANK:(t % 2 + 1) * BANK].rearrange("p (h n) -> p h n", n=VW)
                        dve.wait_ge(s_ops, t + 1)
                        dve.reciprocal(rc[:, t % 2, :], o[:, :, HD:HD + 1].rearrange("p h n -> p (h n)")).then_inc(s_rc, 1)
                        dve.wait_ge(s_rc, t + 1)
                        dve.tensor_tensor(cx[:, c % 2, i, :].rearrange("p (h d) -> p h d", d=HD), o[:, :, 0:HD],
                                          rc[:, t % 2, :].unsqueeze(2).to_broadcast([P, H, HD]), ALU.mult).then_inc(s_cx, 1)

                for c in range(B):
                    context(c)
                    if c >= 1:
                        tail.dve_sum(dve, c - 1)
                        tail.dve_norm(dve, c - 1)
                tail.dve_sum(dve, B - 1)
                tail.dve_norm(dve, B - 1)


def l1_tree(nc, env):
    w, PS = env.w, env.PS
    M = D
    NG = M - 1
    DEPTH = 8
    tiles = lambda c: list(range(c * TB, (c + 1) * TB))
    with ExitStack() as c_:
        sb, sem = env.alloc(c_)
        tail = Tail(env, c_, "t5", (2, 4, 6), tiles, KD)
        wr = sb("wr", [P, KD, M], F32)
        lw = sb("lw", [P, KD, D], F32)
        gx = sb("gx", [P, TB, M], F32)
        g1 = sb("g1", [P, TB, M], F32)
        gt = sb("gt", [P, TB, M], F32)
        om = sb("om", [P, TB, M], F32)
        lp = sb("lp", [P, 2, TB, M], F32)
        leaf = sb("leaf", [P, 2, TB, M], F32)
        s_wps = sem("d_wps")
        s_w = sem("d_w")
        s_gps = sem("d_gps")
        s_gx = sem("d_gx")
        s_dve = sem("d_dve")
        s_leaf = sem("d_leaf")
        s_out = sem("d_out")

        with nc.Block() as block:

            @block.tensor
            def _(pe):
                for n, (a, b_, width) in enumerate((("d_wq", "d_rT", NG), ("d_lvT", "d_woT", D))):
                    for m in range(KD):
                        for k in range(KD):
                            last = pe.matmul(PS[:, n * BANK + m * M:n * BANK + m * M + width], w[a][:, k, m * P:(m + 1) * P],
                                             w[b_][:, k, 0:width], start=(k == 0), stop=(k == KD - 1))
                    last.then_inc(s_wps, 1)
                pe.wait_ge(s_w, 2)

                def gates(c):
                    if c >= 1:
                        pe.wait_ge(s_gx, c)
                    for i in range(TB):
                        t = c * TB + i
                        for k in range(KD):
                            last = pe.matmul(PS[:, i * M:i * M + NG], env.xT[:, k, t * P:(t + 1) * P], wr[:, k, 0:NG],
                                             start=(k == 0), stop=(k == KD - 1))
                    last.then_inc(s_gps, 1)

                gates(0)
                for c in range(B):
                    if c + 1 < B:
                        gates(c + 1)
                    tail.pe_in(pe, c, lambda i: leaf[:, c % 2, i, :], lambda i: pe.wait_ge(s_leaf, c + 1))
                    tail.pe_proj(pe, c, lambda k: lw[:, k, :])

            @block.scalar
            def _(act):
                act.wait_ge(s_wps, 1)
                act.activation(wr[:, :, 0:NG], PS[:, 0:KD * M].rearrange("p (k n) -> p k n", k=KD)[:, :, 0:NG],
                               ACT.Copy).then_inc(s_w, 1)
                act.wait_ge(s_wps, 2)
                act.activation(lw[:, :, :], PS[:, BANK:BANK + KD * D].rearrange("p (k n) -> p k n", k=KD),
                               ACT.Copy).then_inc(s_w, 1)

                def gates(c):
                    act.wait_ge(s_gps, c + 1)
                    if c >= 1:
                        act.wait_ge(s_leaf, c)
                    act.activation(gx[:, :, 0:NG], PS[:, 0:TB * M].rearrange("p (t n) -> p t n", t=TB)[:, :, 0:NG],
                                   ACT.Exp, scale=-1.0).then_inc(s_gx, 1)

                gates(0)
                for c in range(B):
                    if c + 1 < B:
                        gates(c + 1)
                    tail.act_in(act, c)

            @block.gpsimd
            def _(pool):
                for c in range(B):
                    tail.pool_residual(pool, c, lambda t: w["d_bout"])
                for c in range(B):
                    tail.pool_rstd(pool, c)

            @block.vector
            def _(dve):
                steps = [0]

                def link(ins):
                    steps[0] += 1
                    ins.then_inc(s_dve, 1)
                    dve.wait_ge(s_dve, steps[0])

                def leaves(c):
                    dve.wait_ge(s_gx, c + 1)
                    if c >= 2:
                        dve.wait_ge(tail.s_cT_ps, c - 1)
                    link(dve.tensor_scalar(g1[:, :, 0:NG], gx[:, :, 0:NG], 1.0, None, ALU.add))
                    link(dve.reciprocal(gt[:, :, 0:NG], g1[:, :, 0:NG]))
                    link(dve.tensor_scalar(om[:, :, 0:NG], gt[:, :, 0:NG], -1.0, 1.0, ALU.mult, ALU.add))
                    for level in range(DEPTH):
                        n = 1 << level
                        dst = leaf[:, c % 2, :, :] if level == DEPTH - 1 else lp[:, level % 2, :, 0:2 * n]
                        dst = dst.rearrange("p t (n e) -> p t n e", e=2)
                        for e, g in enumerate((om, gt)):
                            gg = g[:, :, n - 1:2 * n - 1]
                            if level == 0:
                                last = dve.tensor_copy(dst[:, :, :, e], gg)
                            else:
                                last = dve.tensor_tensor(dst[:, :, :, e], lp[:, (level - 1) % 2, :, 0:n], gg, ALU.mult)
                        if level < DEPTH - 1:
                            link(last)
                    last.then_inc(s_leaf, 1)

                for c in range(B):
                    leaves(c)
                    if c >= 1:
                        tail.dve_sum(dve, c - 1)
                        tail.dve_norm(dve, c - 1)
                tail.dve_sum(dve, B - 1)
                tail.dve_norm(dve, B - 1)

            @block.sync
            def _(sp):
                for c in range(B):
                    sp.wait_ge(tail.s_xn, c + 1)
                    sp.dma_start(env.d["out"][c * L:(c + 1) * L, :].rearrange("(t p) n -> p t n", p=P),
                                 env.x[:, c * TB:(c + 1) * TB, :]).then_inc(s_out, 16)
                sp.wait_ge(s_out, 16 * B)


CF = 5 * P + 2 * E + ETILES + 2 * L

MATS = {
    "a0_in": (D, 3 * D, 0), "a0_out": (D, D, 0), "c0_wq": (D, D, 0), "c0_wkT": (D, CD, 0), "c0_wv": (CD, D, 0),
    "f_router": (D, E, 0), "f_wg": (D, F, 0), "f_wu": (D, F, 0), "f_wd": (F, D, 0),
    "s_wq": (D, D, 1), "s_wqs": (D, D, 1), "s_wk": (D, D, 1), "s_wks": (D, D, 1), "s_wv": (D, D, 1), "s_wo": (D, D, 1),
    "x_wq": (D, D, 1), "x_wk": (CD, D, 1), "x_wv": (CD, D, 1), "x_wo": (D, D, 1),
    "d_wq": (D, D, 1), "d_rT": (D, D - 1, 1), "d_lvT": (D, D, 1), "d_woT": (D, D, 1),
}
ROWS = {"a0_bout": 0, "c0_bv": 0, "s_bv": 1, "s_bo": 1, "x_bv": 1, "x_bo": 1, "d_bout": 1}
COLS = {"c0_bq": 0, "c0_bk": 0, "s_bq": 1, "s_bqs": 1, "s_bk": 1, "s_bks": 1, "x_bq": 1, "x_bk": 1}


def build(nc, d):
    env = Env()
    env.d = d
    with ExitStack() as ctx:
        layer_sems = []

        def alloc(c):
            def sb(name, shape, dt):
                return c.enter_context(nc.sbuf_tensor(name, shape, dt))

            def sem(name, keep=False):
                handle = nc.alloc_semaphore(name)
                if not keep:
                    layer_sems.append(handle)
                return handle

            return sb, sem

        env.alloc = alloc
        sb, sem = alloc(ctx)
        scratch = lambda name, shape, dt: nc.dram_tensor(name, shape, dt, kind="Internal").ap()
        env.kx = scratch("kx", (3, B * D, CTX), BF16)
        env.qx = scratch("qx", (3, B * D, L), BF16)
        env.vx = scratch("vx", (GROUPS, CTX, G * VW), F32)
        env.ks = scratch("ks", (3, B * D, L), BF16)
        env.qs = scratch("qs", (3, B * D, L), BF16)
        env.vs = scratch("vs", (GROUPS, L, G * VW), F32)
        env.xg = scratch("xg", (ETILES * P, D), F32)
        env.yg = scratch("yg", (ETILES * P, D), F32)
        env.xg_t = env.xg.rearrange("(j p) n -> j p n", p=P)
        env.yg_t = env.yg.rearrange("(j p) n -> j p n", p=P)
        env.gu_t, env.dn_t = d["f_gu"], d["f_dn"]

        psum = ctx.enter_context(nc.psum_tensor("psum", [P, 8 * BANK], F32))
        env.PS = psum[:, :]
        env.x = sb("x_sb", [P, T, D], F32)
        env.xT = sb("xT_sb", [P, KD, N], F32)
        env.cf = sb("cf_sb", [P, CF], F32)
        env.cb = sb("cb_sb", [P, 3 * P], BF16)
        mh = sb("mhalf", [P, TB], F32)
        env.mhalf = mh[:, :]
        at = 0
        parts = []
        for n in (P, P, P, P, P, E, E, ETILES, L, L):
            parts.append(env.cf[:, at:at + n])
            at += n
        env.ident, _, _, env.tri, env.ones, env.iota16, env.thr16, env.iota32, env.cos, env.sin = parts
        env.identb, env.mask_q, env.mask_k = (env.cb[:, i * P:(i + 1) * P] for i in range(3))

        env.w, env.loads = {}, []

        def weights(layer, c):
            sbw, _ = alloc(c)
            for name, (k, n, l) in MATS.items():
                if l == layer:
                    if k == P:
                        t = sbw(name + "_sb", [P, n], F32)
                        env.w[name] = t[:, :]
                        env.loads.append((t[:, :], d[name]))
                    else:
                        t = sbw(name + "_sb", [P, k // P, n], F32)
                        env.w[name] = t
                        env.loads.append((t[:, :, :], d[name].rearrange("(k p) n -> p k n", p=P)))
            for name, l in ROWS.items():
                if l == layer:
                    t = sbw(name + "_sb", [P, D], F32)
                    env.w[name] = t[:, :]
                    env.loads.append((t[:, :], d[name].partition_broadcast(P)))
            for name, l in COLS.items():
                if l == layer:
                    t = sbw(name + "_sb", [P, KD], F32)
                    env.w[name] = t[:, :]
                    env.loads.append((t[:, :], d[name]))
            if layer == 0:
                t = sbw("a0_bin_sb", [1, 3 * D], F32)
                env.w["a0_bin"] = t[:, :]
                env.loads.append((t[:, :], d["a0_bin"]))

        weights(1, ctx)
        with ExitStack() as c0:
            weights(0, c0)
            with ExitStack() as c1:
                sbc, _ = alloc(c1)
                ctx_sb = sbc("ctx_sb", [P, B, CT, CD], F32)
                ctxT_sb = sbc("ctxT_sb", [CD, B * CTX], F32)
                env.ctx, env.ctxT = ctx_sb, ctxT_sb
                ctx_prep(nc, env)
                l0_attn(nc, env)
                l0_xattn(nc, env)
            l0_ffn(nc, env)
        with nc.Block() as block:

            @block.sync
            def _(sp):
                for handle in layer_sems:
                    sp.sem_clear(handle)

        for handle in layer_sems:
            nc.release_semaphore(handle)
        layer_sems.clear()
        grouped = lambda a: [a[j].rearrange("(g r) n -> g r n", g=GROUPS) for j in range(3)]
        with ExitStack() as c1:
            l1_attn_prep(nc, env)
            sbc, _ = alloc(c1)
            OT = sbc("OT", [P, GROUPS, L], F32)
            heads_loop(nc, env, "sa", L, True, grouped(env.qs), grouped(env.ks), env.vs, OT)
            heads_tail(nc, env, "t3", OT, env.w["s_wo"], env.w["s_bo"])
            l1_xattn_prep(nc, env)
            heads_loop(nc, env, "xa", CTX, False, grouped(env.qx), grouped(env.kx), env.vx, OT)
            heads_tail(nc, env, "t4", OT, env.w["x_wo"], env.w["x_bo"])
        l1_tree(nc, env)


def constants():
    f = np.zeros((P, CF), np.float32)
    i = np.arange(P)
    at = 0

    def put(a):
        nonlocal at
        f[:, at:at + a.shape[1]] = a
        at += a.shape[1]

    put(np.eye(P, dtype=np.float32))
    hide = np.where(i[:, None] >= i[None, :], 0.0, -1e30).astype(np.float32)
    put(hide)
    put(hide.T)
    put((i[:, None] < i[None, :]).astype(np.float32))
    put(np.ones((P, P), np.float32))
    put(np.tile(np.arange(E, dtype=np.float32), (P, 1)))
    put(np.tile(P * np.arange(E, dtype=np.float32), (P, 1)))
    put(np.tile(np.arange(ETILES, dtype=np.float32), (P, 1)))
    frac = (2 * np.arange(HD // 2) / HD).astype(np.float32)
    scale = np.power(np.float32(2500), frac).astype(np.float32)
    angle = np.arange(L).astype(np.float32)[None, :] / scale[:, None]
    cos, sin = np.cos(angle).astype(np.float32), np.sin(angle).astype(np.float32)
    put(np.tile(np.concatenate([cos, cos]), (P // HD, 1)))
    put(np.tile(np.concatenate([-sin, sin]), (P // HD, 1)))
    return f


def kernel(**inputs):
    import concourse.bacc as bacc
    from concourse.bass_utils import run_bass_kernel_spmd

    a = {k: np.asarray(v) for k, v in inputs.items()}
    c = np.ascontiguousarray
    cols = lambda v: c(v.reshape(KD, P).T)
    swap = np.arange(D).reshape(H, 2, HD // 2)[:, ::-1, :].reshape(-1)
    cf = constants()
    arrays = {
        "x": c(a["x"].reshape(N, D)), "ctx": c(a["ctx_512"]), "cf": cf,
        "a0_in": c(a["L0_attn_in_proj_weight"].T), "a0_bin": c(a["L0_attn_in_proj_bias"][None, :]),
        "a0_out": c(a["L0_attn_out_proj_weight"].T), "a0_bout": c(a["L0_attn_out_proj_bias"]),
        "c0_wq": c(a["L0_xattn_Wq"]), "c0_bq": cols(a["L0_xattn_bq"]), "c0_wkT": c(a["L0_xattn_Wk"].T),
        "c0_bk": cols(a["L0_xattn_bk"]), "c0_wv": c(a["L0_xattn_Wv"]), "c0_bv": c(a["L0_xattn_bv"]),
        "f_router": c(a["L0_ffn_w_router"].T), "f_gu": c(a["L0_ffn_gate_up_proj"]), "f_dn": c(a["L0_ffn_down_proj"]),
        "f_wg": c(a["L0_ffn_w_gate"].T), "f_wu": c(a["L0_ffn_w_up"].T), "f_wd": c(a["L0_ffn_w_down"].T),
        "s_wq": c(a["L1_attn_wq_w"]), "s_wqs": c(a["L1_attn_wq_w"][:, swap]), "s_bq": cols(a["L1_attn_wq_b"]),
        "s_bqs": cols(a["L1_attn_wq_b"][swap]), "s_wk": c(a["L1_attn_wk_w"]), "s_wks": c(a["L1_attn_wk_w"][:, swap]),
        "s_bk": cols(a["L1_attn_wk_b"]), "s_bks": cols(a["L1_attn_wk_b"][swap]), "s_wv": c(a["L1_attn_wv_w"]),
        "s_bv": c(a["L1_attn_wv_b"]), "s_wo": c(a["L1_attn_wo_w"]), "s_bo": c(a["L1_attn_wo_b"]),
        "x_wq": c(a["L1_xattn_Wq"]), "x_bq": cols(a["L1_xattn_bq"]), "x_wk": c(a["L1_xattn_Wk"]),
        "x_bk": cols(a["L1_xattn_bk"]), "x_wv": c(a["L1_xattn_Wv"]), "x_bv": c(a["L1_xattn_bv"]),
        "x_wo": c(a["L1_xattn_Wo"]), "x_bo": c(a["L1_xattn_bo"]),
        "d_wq": c(a["L1_ffn_Wq"]), "d_rT": c(a["L1_ffn_routers"].T), "d_lvT": c(a["L1_ffn_leaf_values"].T),
        "d_woT": c(a["L1_ffn_Wout_w"].T), "d_bout": c(a["L1_ffn_Wout_b"]),
    }
    nc = bacc.Bacc("TRN2", target_bir_lowering=False, num_devices=1)
    d = {}
    for name, arr in arrays.items():
        d[name] = nc.dram_tensor("in_" + name, arr.shape, mybir.dt.from_np(arr.dtype), kind="ExternalInput").ap()
    d["out"] = nc.dram_tensor("out_0", (N, D), F32, kind="ExternalOutput").ap()
    build(nc, d)
    r = run_bass_kernel_spmd(nc, [{"in_" + k: v for k, v in arrays.items()}], core_ids=[0])
    return r.results[0]["out_0"].reshape(B, L, D)
```

```python
from contextlib import ExitStack

import numpy as np

import concourse.bass as bass
from concourse import mybir

F32 = mybir.dt.float32
BF16 = mybir.dt.bfloat16
I32 = mybir.dt.int32
ALU = mybir.AluOpType
ACT = mybir.ActivationFunctionType
AX = mybir.AxisListType.X

P = 128
B, L, D = 4, 512, 256
N = B * L
T = N // P
TB = L // P
KD = D // P
H, HD = 16, 16
CTX, CD = 1601, 128
CT = -(-CTX // P)
E, F = 16, 512
FC = F // P
BANK = 512
EPS = 1e-5
SCALE = HD ** -0.5
G = 4
GROUPS = B * H // G
VW = 32
K_PARTS = (0, 1, 2, 0, 1, 0)
Q_PARTS = (0, 0, 0, 1, 1, 2)
QK_ROWS = HD * len(K_PARTS)
ETILES = N // P + E


def ctx_rows(kt):
    return min(P, CTX - kt * P)


class Env:
    pass


class Tail:
    def __init__(self, env, c, name, banks, tiles, kc, last=False):
        self.env, self.tiles, self.kc, self.last = env, tiles, kc, last
        self.cT_ps, self.pr_ps, self.xT_ps = (env.PS[:, b * BANK:(b + 2) * BANK] for b in banks)
        sb, sem = env.alloc(c)
        self.cT = sb(name + "_cT", [P, KD, TB * P], F32)
        self.r = sb(name + "_r", [P, TB, D], F32)
        self.st = sb(name + "_st", [P, TB, 6], F32)
        self.mv = sb(name + "_mv", [P, TB, 2], F32)
        self.ve = sb(name + "_ve", [P, TB], F32)
        self.rstd = sb(name + "_rstd", [P, TB], F32)
        self.s_cT_ps = sem(name + "_cT_ps")
        self.s_cT = sem(name + "_cT")
        self.s_proj = sem(name + "_proj")
        self.s_xb = sem(name + "_xb")
        self.s_r = sem(name + "_r")
        self.s_st = sem(name + "_st")
        self.s_mv = sem(name + "_mv")
        self.s_ve = sem(name + "_ve")
        self.s_rstd = sem(name + "_rstd")
        self.s_xn = sem(name + "_xn")
        self.s_xT_ps = sem(name + "_xT_ps")
        self.s_xT = sem(name + "_xT")

    def pool_residual(self, pool, c, add):
        x = self.env.x
        for t in self.tiles(c):
            last = pool.tensor_tensor(x[:, t, :], x[:, t, :], add(t), ALU.add)
        last.then_inc(self.s_xb, 1)

    def pe_in(self, pe, c, nat, ready):
        if c >= 1:
            pe.wait_ge(self.s_cT, c)
        for i in range(TB):
            ready(i)
            for k in range(KD):
                last = pe.transpose(self.cT_ps[:, k * BANK + i * P:k * BANK + (i + 1) * P],
                                    nat(i)[:, k * P:(k + 1) * P], self.env.ident)
        last.then_inc(self.s_cT_ps, 1)

    def act_in(self, act, c):
        act.wait_ge(self.s_cT_ps, c + 1)
        if c >= 1:
            act.wait_ge(self.s_proj, c)
        act.activation(self.cT[:, :, :].rearrange("p k n -> p (k n)"), self.cT_ps,
                       ACT.Copy).then_inc(self.s_cT, 1)

    def pe_proj(self, pe, c, w, lhs=None):
        if lhs is None:
            pe.wait_ge(self.s_cT, c + 1)
            lhs = lambda i, k: self.cT[:, k, i * P:(i + 1) * P]
        if c >= 1:
            pe.wait_ge(self.s_r, c)
        for i in range(TB):
            for k in range(self.kc):
                last = pe.matmul(self.pr_ps[:, i * D:(i + 1) * D], lhs(i, k), w(k),
                                 start=(k == 0), stop=(k == self.kc - 1))
        last.then_inc(self.s_proj, 1)

    def x_chunk(self, c):
        ts = self.tiles(c)
        return self.env.x[:, ts[0]:ts[-1] + 1:ts[1] - ts[0], :]

    def dve_sum(self, dve, c):
        dve.wait_ge(self.s_proj, c + 1)
        dve.wait_ge(self.s_xb, c + 1)
        if c >= 1:
            dve.wait_ge(self.s_xn, c)
        dve.tensor_tensor(self.r[:, :, :], self.pr_ps.rearrange("p (t n) -> p t n", t=TB),
                          self.x_chunk(c), ALU.add).then_inc(self.s_r, 1)

    def dve_norm(self, dve, c):
        dve.wait_ge(self.s_r, c + 1)
        for i in range(TB):
            dve.bn_stats(self.st[:, i, :], self.r[:, i, :]).then_inc(self.s_st, 1)
        dve.wait_ge(self.s_st, TB * (c + 1))
        for i in range(TB):
            last = dve.bn_aggr(self.mv[:, i, :], self.st[:, i, :])
        last.then_inc(self.s_mv, 1)
        dve.wait_ge(self.s_mv, c + 1)
        dve.tensor_scalar(self.ve[:, :], self.mv[:, :, 1], EPS, None, ALU.add).then_inc(self.s_ve, 1)
        dve.wait_ge(self.s_rstd, c + 1)
        if c >= 0:
            for i, t in enumerate(self.tiles(c)):
                last = dve.tensor_scalar(self.env.x[:, t, :], self.r[:, i, :], self.mv[:, i, 0:1],
                                         self.rstd[:, i:i + 1], ALU.subtract, ALU.mult)
            last.then_inc(self.s_xn, 1)

    def pool_rstd(self, pool, c):
        pool.wait_ge(self.s_ve, c + 1)
        pool.tensor_tensor(self.rstd[:, :], self.ve[:, :], self.env.mhalf, ALU.pow).then_inc(self.s_rstd, 1)

    def pe_out(self, pe, c):
        pe.wait_ge(self.s_xn, c + 1)
        if c >= 1:
            pe.wait_ge(self.s_xT, c)
        for i, t in enumerate(self.tiles(c)):
            for k in range(KD):
                last = pe.transpose(self.xT_ps[:, k * BANK + i * P:k * BANK + (i + 1) * P],
                                    self.env.x[:, t, k * P:(k + 1) * P], self.env.ident)
        last.then_inc(self.s_xT_ps, 1)

    def act_out(self, act, c):
        act.wait_ge(self.s_xT_ps, c + 1)
        ts = self.tiles(c)
        xT = self.env.xT[:, :, :].rearrange("p k (t n) -> p k t n", n=P)[:, :, ts[0]:ts[-1] + 1:ts[1] - ts[0], :]
        for k in range(KD):
            last = act.activation(xT[:, k], self.xT_ps[:, k * BANK:(k + 1) * BANK].rearrange("p (t n) -> p t n", n=P),
                                  ACT.Copy)
        last.then_inc(self.s_xT, 1)


def slot_runs(slots):
    runs = []
    for i, j in enumerate(slots):
        if runs:
            s0, n, j0, same = runs[-1]
            if j == j0 and (same or n == 1) or j == j0 + n and not same:
                runs[-1] = (s0, n + 1, j0, j == j0)
                continue
        runs.append((i, 1, j, False))
    return runs


class Split:

    def __init__(self, env, c, name, width, bias, dst, slots, ring, rope=None):
        self.env, self.width, self.bias, self.dst, self.rope, self.ring = env, width, bias, dst, rope, ring
        self.slots, self.per = slots, len(slot_runs(slots(0)))
        sb, sem = env.alloc(c)
        self.parts = sb(name + "_parts", [P, ring, 3, width], BF16)
        self.rest = sb(name + "_rest", [P, ring, width], F32)
        if rope:
            self.ta = sb(name + "_ta", [P, ring, width], F32)
            self.tb = sb(name + "_tb", [P, ring, width], F32)
            self.whole = sb(name + "_whole", [P, ring, width], F32)
        self.s_full = sem(name + "_full")
        self.s_rot = sem(name + "_rot")
        self.s_whole = sem(name + "_whole")
        self.s_hi = sem(name + "_hi")
        self.s_rest = sem(name + "_rest")
        self.s_mid = sem(name + "_mid")
        self.s_lo = sem(name + "_lo")
        self.s_out = [sem(f"{name}_out{u}") for u in range(ring)]

    def freed(self, pe, n):
        pe.wait_ge(self.s_rot if self.rope else self.s_rest, n + 1)

    def act_hi(self, act, n, ps):
        u = n % self.ring
        if n >= self.ring:
            act.wait_ge(self.s_out[u], 16 * self.per * (n // self.ring))
        if self.rope:
            act.wait_ge(self.s_whole, n + 1)
            act.activation(self.parts[:, u, 0, :], self.whole[:, u, :], ACT.Copy).then_inc(self.s_hi, 1)
        else:
            act.wait_ge(self.s_full, n + 1)
            act.activation(self.parts[:, u, 0, :], ps, ACT.Identity, bias=self.bias(n)).then_inc(self.s_hi, 1)

    def act_mid(self, act, n):
        act.wait_ge(self.s_rest, n + 1)
        act.activation(self.parts[:, n % self.ring, 1, :], self.rest[:, n % self.ring, :], ACT.Copy).then_inc(self.s_mid, 1)

    def dve_rot(self, dve, n, full, ps_a, ps_b):
        u = n % self.ring
        ba, bb = self.bias(n)
        dve.wait_ge(self.s_full, full)
        if n >= self.ring:
            dve.wait_ge(self.s_whole, n - self.ring + 1)
        dve.scalar_tensor_tensor(self.ta[:, u, :], ps_a, ba, self.rope(n)[0], ALU.add, ALU.mult)
        dve.scalar_tensor_tensor(self.tb[:, u, :], ps_b, bb, self.rope(n)[1], ALU.add, ALU.mult).then_inc(self.s_rot, 1)

    def dve_rest(self, dve, n, ps=None):
        u = n % self.ring
        dve.wait_ge(self.s_hi, n + 1)
        if n >= self.ring:
            dve.wait_ge(self.s_lo, n - self.ring + 1)
        if self.rope:
            dve.tensor_tensor(self.rest[:, u, :], self.whole[:, u, :], self.parts[:, u, 0, :],
                              ALU.subtract).then_inc(self.s_rest, 1)
        else:
            dve.scalar_tensor_tensor(self.rest[:, u, :], ps, self.bias(n), self.parts[:, u, 0, :],
                                     ALU.add, ALU.subtract).then_inc(self.s_rest, 1)

    def pool_whole(self, pool, n):
        u = n % self.ring
        pool.wait_ge(self.s_rot, n + 1)
        if n >= self.ring:
            pool.wait_ge(self.s_rest, n - self.ring + 1)
        pool.tensor_tensor(self.whole[:, u, :], self.ta[:, u, :], self.tb[:, u, :], ALU.add).then_inc(self.s_whole, 1)

    def pool_lo(self, pool, n):
        u = n % self.ring
        pool.wait_ge(self.s_mid, n + 1)
        pool.tensor_tensor(self.parts[:, u, 2, :], self.rest[:, u, :], self.parts[:, u, 1, :],
                           ALU.subtract).then_inc(self.s_lo, 1)

    def sp_out(self, sp, n):
        sp.wait_ge(self.s_lo, n + 1)
        dst = self.dst(n)
        for s0, slots, j, same in slot_runs(self.slots(n)):
            src = self.parts[:, n % self.ring, j:j + (1 if same else slots), :]
            if same:
                src = src.to_broadcast([P, slots, self.width])
            sp.dma_start(dst[:, s0:s0 + slots, :], src).then_inc(self.s_out[n % self.ring], 16)

    def sp_end(self, sp, blocks):
        for u in range(self.ring):
            sp.wait_ge(self.s_out[u], 16 * self.per * ((blocks - u + self.ring - 1) // self.ring))


class Values:

    def __init__(self, env, c, name, items, bias, dst):
        self.env, self.items, self.bias, self.dst = env, items, bias, dst
        sb, sem = env.alloc(c)
        self.v = sb(name + "_v", [P, 2, 4, H * VW], F32)
        self.s_zero = sem(name + "_zero")
        self.s_ones = sem(name + "_ones")
        self.s_full = sem(name + "_vfull")
        self.s_v = sem(name + "_v")
        self.s_out = [sem(f"{name}_vout{u}") for u in range(2)]
        self.sent = [0, 0]
        self.sent_before = []
        for n, (b, kts, rows) in enumerate(items):
            self.sent_before.append(self.sent[n % 2])
            self.sent[n % 2] += 16 * len(kts)

    def pool_init(self, pool):
        v = self.v[:, :, :, :].rearrange("p u k n -> p (u k n)")
        pool.memset(v, 0.0).then_inc(self.s_zero, 1)
        pool.wait_ge(self.s_zero, 1)
        pool.memset(v.rearrange("p (h w) -> p h w", w=VW)[:, :, HD:HD + 1], 1.0).then_inc(self.s_ones, 1)

    def dve_copy(self, dve, n, ps):
        b, kts, rows = self.items[n]
        k = len(kts)
        if n == 0:
            dve.wait_ge(self.s_ones, 1)
        dve.wait_ge(self.s_full, n + 1)
        if n >= 2:
            dve.wait_ge(self.s_out[n % 2], self.sent_before[n])
        out = self.v[0:rows, n % 2, 0:k, :].rearrange("p k (h w) -> p (k h) w", w=VW)[:, :, 0:HD]
        src = ps[0:rows, 0:k * D].rearrange("p (k n) -> p k n", k=k)
        for i in range(k):
            last = dve.tensor_tensor(out[:, i * H:(i + 1) * H, :], src[:, i, :].rearrange("p (h d) -> p h d", d=HD),
                                     self.bias[0:rows, :].rearrange("p (h d) -> p h d", d=HD), ALU.add)
        last.then_inc(self.s_v, 1)

    def sp_out(self, sp, n):
        b, kts, rows = self.items[n]
        sp.wait_ge(self.s_v, n + 1)
        for i, kt in enumerate(kts):
            sp.dma_start(self.dst[b * G:(b + 1) * G, kt * P:kt * P + rows, :].rearrange("g p n -> p g n"),
                         self.v[0:rows, n % 2, i, :].rearrange("p (g n) -> p g n", g=G)).then_inc(self.s_out[n % 2], 16)

    def sp_end(self, sp):
        for u in range(2):
            sp.wait_ge(self.s_out[u], self.sent[u])


def ctx_prep(nc, env):
    w, PS = env.w, env.PS
    groups = [PS[:, 0:4 * BANK], PS[:, 4 * BANK:8 * BANK]]
    KB = B * KD
    vitems = [(b, kts, ctx_rows(kts[-1])) for b in range(B) for kts in ((0, 1, 2, 3), (4, 5, 6, 7), (8, 9, 10, 11), (12,))]
    with ExitStack() as c:
        sb, sem = env.alloc(c)
        sp_k = Split(env, c, "xk", CTX, lambda n: w["x_bk"][:, n % KD:n % KD + 1],
                     lambda n: env.kx[n * P:(n + 1) * P, :, :], lambda n: range(3), 2)
        val = Values(env, c, "xv", vitems, w["x_bv"], env.vx)
        s_c = [sem(f"ld_ctx{b}") for b in range(B)]
        s_x = sem("ld_x")
        s_const = sem("ld_const")
        s_w = sem("ld_w")
        s_xps = sem("x_ps")
        s_xT = sem("x_T")
        s_cps = sem("c_ps")
        s_cT = sem("c_T")
        s_zt = sem("zero_tile")
        s_zd = sem("zero_dram", keep=True)
        zt = sb("zt", [P, 8, D], F32)
        n_w = 0

        items = [("x", i) for i in range(B)] + [("c", b) for b in range(B)]
        for n in range(KB):
            items.append(("k", n))
            items += [("v", 2 * n), ("v", 2 * n + 1)]
        at = {it: groups[i % 2] for i, it in enumerate(items)}

        with nc.Block() as block:

            @block.sync
            def _(sp):
                sp.dma_start(env.cf[:, :], env.d["cf"]).then_inc(s_const, 16)
                sp.dma_start(env.x[:, :, :], env.d["x"].rearrange("(t p) n -> p t n", p=P)).then_inc(s_x, 16)
                for b in range(B):
                    sp.dma_start(env.ctx[:, b, 0:CT - 1, :],
                                 env.d["ctx"][b, 0:(CT - 1) * P, :].rearrange("(k p) n -> p k n", p=P)).then_inc(s_c[b], 16)
                    sp.dma_start(env.ctx[0:ctx_rows(CT - 1), b, CT - 1, :],
                                 env.d["ctx"][b, (CT - 1) * P:CTX, :]).then_inc(s_c[b], 16)
                for n in range(KB):
                    sp_k.sp_out(sp, n)
                    val.sp_out(sp, 2 * n)
                    val.sp_out(sp, 2 * n + 1)
                sp_k.sp_end(sp, KB)
                val.sp_end(sp)
                sp.wait_ge(s_zd, 16 * (ETILES // 8))

            @block.scalar
            def _(act):
                for dst, src in env.loads:
                    act.dma_start(dst, src).then_inc(s_w, 16)
                act.wait_ge(s_const, 16)
                act.activation(env.cb[:, :], env.cf[:, 0:3 * P], ACT.Copy)
                for i in range(B):
                    act.wait_ge(s_xps, i + 1)
                    act.activation(env.xT[:, :, i * L:(i + 1) * L],
                                   at["x", i][:, 0:KD * L].rearrange("p (k n) -> p k n", k=KD), ACT.Copy).then_inc(s_xT, 1)
                act.wait_ge(s_w, 16 * len(env.loads))
                for n in range(KB):
                    sp_k.act_hi(act, n, at["k", n][:, 0:CTX])
                    sp_k.act_mid(act, n)

            @block.gpsimd
            def _(pool):
                pool.memset(zt[:, :, :].rearrange("p a n -> p (a n)"), 0.0).then_inc(s_zt, 1)
                pool.memset(env.mhalf, -0.5)
                val.pool_init(pool)
                pool.wait_ge(s_zt, 1)
                for i in range(ETILES // 8):
                    pool.dma_start(env.xg[i * 8 * P:(i + 1) * 8 * P, :].rearrange("(a p) n -> p a n", p=P),
                                   zt[:, :, :]).then_inc(s_zd, 16)
                for n in range(KB):
                    sp_k.pool_lo(pool, n)

            @block.tensor
            def _(pe):
                def freed(it):
                    kind, n = it
                    if kind == "x":
                        pe.wait_ge(s_xT, n + 1)
                    elif kind == "c":
                        pe.wait_ge(s_cT, n + 1)
                    elif kind == "k":
                        sp_k.freed(pe, n)
                    else:
                        pe.wait_ge(val.s_v, n + 1)

                pe.wait_ge(s_const, 16)
                pe.wait_ge(s_x, 16)
                for i, it in enumerate(items):
                    kind, n = it
                    ps = at[it]
                    if i >= 2:
                        freed(items[i - 2])
                    if kind == "x":
                        for k in range(KD):
                            for j in range(TB):
                                last = pe.transpose(ps[:, k * L + j * P:k * L + (j + 1) * P],
                                                    env.x[:, n * TB + j, k * P:(k + 1) * P], env.ident)
                        last.then_inc(s_xps, 1)
                    elif kind == "c":
                        pe.wait_ge(s_c[n], 32)
                        for kt in range(CT):
                            r = ctx_rows(kt)
                            last = pe.transpose(ps[:, kt * P:kt * P + r], env.ctx[0:r, n, kt, :], env.ident[0:r, 0:r])
                        last.then_inc(s_cps, 1)
                    elif kind == "k":
                        if n == 0:
                            pe.wait_ge(s_w, 16 * len(env.loads))
                            pe.wait_ge(s_cT, B)
                        b, m = divmod(n, KD)
                        for q in range(0, CTX, BANK):
                            e = min(q + BANK, CTX)
                            last = pe.matmul(ps[:, q:e], w["x_wk"][:, m * P:(m + 1) * P],
                                             env.ctxT[:, b * CTX + q:b * CTX + e], start=True, stop=True)
                        last.then_inc(sp_k.s_full, 1)
                    else:
                        b, kts, rows = vitems[n]
                        for j, kt in enumerate(kts):
                            last = pe.matmul(ps[0:rows, j * D:(j + 1) * D],
                                             env.ctxT[:, b * CTX + kt * P:b * CTX + kt * P + rows], w["x_wv"],
                                             start=True, stop=True)
                        last.then_inc(val.s_full, 1)

            @block.vector
            def _(dve):
                for b in range(B):
                    dve.wait_ge(s_cps, b + 1)
                    dve.tensor_copy(env.ctxT[:, b * CTX:(b + 1) * CTX], at["c", b][:, 0:CTX]).then_inc(s_cT, 1)
                dve.wait_ge(s_w, 16 * len(env.loads))
                for n in range(KB):
                    sp_k.dve_rest(dve, n, at["k", n][:, 0:CTX])
                    for v in (2 * n, 2 * n + 1):
                        val.dve_copy(dve, v, at["v", v])


def l0_attn(nc, env):
    w, PS = env.w, env.PS
    W3 = 3 * D
    tiles = lambda c: [s * TB + c for s in range(B)]
    with ExitStack() as c_:
        sb, sem = env.alloc(c_)
        tail = Tail(env, c_, "t0", (2, 4, 6), tiles, KD)
        qkv = sb("qkv", [P, 2, B, W3], F32)
        prod = sb("prod", [P, 2, B, D], F32)
        half = sb("half", [P, 2, D], F32)
        sc = sb("sc", [P, B, B, H], F32)
        mx = sb("mx", [P, B, H], F32)
        ex = sb("ex", [P, B, B, H], F32)
        sm = sb("sm", [P, B, H], F32)
        rs = sb("rs", [P, B, H], F32)
        cx = sb("cx", [P, 2, B, D], F32)
        s_ps = sem("a0_ps")
        s_qkv = sem("a0_qkv")
        s_sh = sem("a0_shift")
        s_ex = sem("a0_exp")
        s_dve = sem("a0_dve")
        s_cx = sem("a0_cx")
        s_used = sem("a0_used")

        with nc.Block() as block:

            @block.tensor
            def _(pe):
                def project(c):
                    for s in range(B):
                        n = c * B + s
                        if n >= 1:
                            pe.wait_ge(s_qkv, n)
                        t = s * TB + c
                        for e in range(2):
                            o = PS[:, e * BANK:e * BANK + W3 // 2]
                            cols = slice(e * W3 // 2, (e + 1) * W3 // 2)
                            for k in range(KD):
                                pe.matmul(o, env.xT[:, k, t * P:(t + 1) * P], w["a0_in"][:, k, cols],
                                          start=(k == 0), stop=False)
                            last = pe.matmul(o, env.ones[0:1, :], w["a0_bin"][0:1, cols], start=False, stop=True)
                        last.then_inc(s_ps, 1)

                project(0)
                for c in range(TB):
                    if c + 1 < TB:
                        project(c + 1)
                    if c >= 1:
                        tail.pe_out(pe, c - 1)
                    tail.pe_in(pe, c, lambda i: cx[:, c % 2, i, :], lambda i: pe.wait_ge(s_cx, c + 1))
                    tail.pe_proj(pe, c, lambda k: w["a0_out"][:, k, :])
                tail.pe_out(pe, TB - 1)

            @block.scalar
            def _(act):
                def read(c):
                    for s in range(B):
                        act.wait_ge(s_ps, c * B + s + 1)
                        if c >= 2 and s == 0:
                            act.wait_ge(s_used, c - 1)
                        act.activation(qkv[:, c % 2, s, :].rearrange("p (e n) -> p e n", e=2),
                                       PS[:, 0:2 * BANK].rearrange("p (e n) -> p e n", e=2)[:, :, 0:W3 // 2],
                                       ACT.Copy).then_inc(s_qkv, 1)

                read(0)
                for c in range(TB):
                    if c + 1 < TB:
                        read(c + 1)
                    act.wait_ge(s_sh, c + 1)
                    act.activation(ex[:, :, :, :].rearrange("p a b h -> p (a b h)"),
                                   sc[:, :, :, :].rearrange("p a b h -> p (a b h)"), ACT.Exp,
                                   scale=SCALE).then_inc(s_ex, 1)
                    if c >= 1:
                        tail.act_out(act, c - 1)
                    tail.act_in(act, c)
                tail.act_out(act, TB - 1)

            @block.gpsimd
            def _(pool):
                for c in range(TB):
                    tail.pool_residual(pool, c, lambda t: w["a0_bout"])
                for c in range(TB):
                    tail.pool_rstd(pool, c)

            @block.vector
            def _(dve):
                steps = [0]

                def link(ins):
                    steps[0] += 1
                    ins.then_inc(s_dve, 1)
                    dve.wait_ge(s_dve, steps[0])

                def attend(c):
                    v5 = qkv[:, c % 2, :, :].rearrange("p s (h n) -> p s h n", n=3 * HD)
                    dve.wait_ge(s_qkv, B * (c + 1))
                    for s in range(B):
                        pr = prod[:, s % 2, :, :].rearrange("p t (h d) -> p t h d", d=HD)
                        link(dve.tensor_tensor(pr, v5[:, s, :, 0:HD].unsqueeze(1).to_broadcast([P, B, H, HD]),
                                               v5[:, :, :, HD:2 * HD], ALU.mult))
                        last = dve.tensor_reduce(sc[:, s, :, :].rearrange("p t h -> p (t h)"),
                                                 prod[:, s % 2, :, :].rearrange("p t (h d) -> p (t h) d", d=HD), AX, ALU.add)
                    link(last)
                    link(dve.tensor_reduce(mx[:, :, :], sc[:, :, :, :].rearrange("p s t h -> p s h t"), AX, ALU.max))
                    dve.tensor_tensor(sc[:, :, :, :], sc[:, :, :, :],
                                      mx[:, :, :].unsqueeze(2).to_broadcast([P, B, B, H]),
                                      ALU.subtract).then_inc(s_sh, 1)
                    if c >= 1:
                        tail.dve_sum(dve, c - 1)
                        tail.dve_norm(dve, c - 1)
                    dve.wait_ge(s_ex, c + 1)
                    link(dve.tensor_reduce(sm[:, :, :], ex[:, :, :, :].rearrange("p s t h -> p s h t"), AX, ALU.add))
                    link(dve.reciprocal(rs[:, :, :], sm[:, :, :]))
                    link(dve.tensor_tensor(ex[:, :, :, :], ex[:, :, :, :],
                                           rs[:, :, :].unsqueeze(2).to_broadcast([P, B, B, H]), ALU.mult))
                    if c >= 2:
                        dve.wait_ge(tail.s_cT_ps, c - 1)
                    for s in range(B):
                        pr = prod[:, s % 2, :, :].rearrange("p t (h d) -> p t h d", d=HD)
                        m = dve.tensor_tensor(pr, ex[:, s, :, :].unsqueeze(3).to_broadcast([P, B, H, HD]),
                                              v5[:, :, :, 2 * HD:3 * HD], ALU.mult)
                        if s == B - 1:
                            m.then_inc(s_used, 1)
                            dve.wait_ge(s_used, c + 1)
                        else:
                            link(m)
                        link(dve.tensor_tensor(half[:, :, :], prod[:, s % 2, 0:2, :], prod[:, s % 2, 2:4, :], ALU.add))
                        last = dve.tensor_tensor(cx[:, c % 2, s, :], half[:, 0, :], half[:, 1, :], ALU.add)
                    last.then_inc(s_cx, 1)

                for c in range(TB):
                    attend(c)
                tail.dve_sum(dve, TB - 1)
                tail.dve_norm(dve, TB - 1)


def l0_xattn(nc, env):
    w, PS = env.w, env.PS
    S_PS = PS[:, 0:4 * BANK]
    P_PS = PS[:, 4 * BANK:6 * BANK]
    M_PS = PS[:, 6 * BANK:7 * BANK]
    O_PS = PS[:, 7 * BANK:8 * BANK]
    NQ = B * KD
    with ExitStack() as c_:
        sb, sem = env.alloc(c_)
        qT = sb("qT", [P, KD, N], F32)
        qk = sb("qk", [P, N], F32)
        pr = sb("pr", [P, 2, CTX], F32)
        pT = sb("pT", [P, 2, CT, P], F32)
        zT = sb("zT", [P, 2, P], F32)
        mxs = sb("mxs", [P, T], F32)
        cq = sb("cq", [P, T], F32)
        top = sb("top", [P, T], F32)
        nb = sb("nb", [P, T], F32)
        rsum = sb("rsum", [P, T], F32)
        rinv = sb("rinv", [P, T], F32)
        r = sb("r0", [P, 2, D], F32)
        st = sb("st0", [P, 6], F32)
        mv = sb("mv0", [P, 2], F32)
        ve = sb("ve0", [P, 1], F32)
        rstd = sb("rstd0", [P, 1], F32)
        s_qps = sem("c0_qps")
        s_q = sem("c0_q")
        s_fps = sem("c0_fps")
        s_f = sem("c0_f")
        s_cps = sem("c0_cps")
        s_cq = sem("c0_cq")
        s_sps = sem("c0_sps")
        s_mx = sem("c0_mx")
        s_nb = sem("c0_nb")
        s_pr = sem("c0_pr")
        s_pps = sem("c0_pps")
        s_pTa = sem("c0_pTa")
        s_pTd = sem("c0_pTd")
        s_zps = sem("c0_zps")
        s_z = sem("c0_z")
        s_ops = sem("c0_ops")
        s_xb = sem("c0_xb")
        s_dve = sem("c0_dve")
        s_r = sem("c0_r")
        s_ve = sem("c0_ve")
        s_rstd = sem("c0_rstd")
        s_xn = sem("c0_xn")
        s_xps = sem("c0_xps")
        s_xT = sem("c0_xT")
        ROUNDS = ((0, 8), (8, CT))
        SPLIT = BANK // P
        bank = lambda n: PS[:, n * BANK:(n + 1) * BANK]

        with nc.Block() as block:

            @block.tensor
            def _(pe):
                def half(n):
                    b, m = divmod(n, KD)
                    if n >= 4:
                        pe.wait_ge(s_q, n - 3)
                    for k in range(KD):
                        last = pe.matmul(bank(n % 4), w["c0_wq"][:, k, m * P:(m + 1) * P], env.xT[:, k, b * L:(b + 1) * L],
                                         start=(k == 0), stop=(k == KD - 1))
                    last.then_inc(s_qps, 1)

                def fold(b):
                    pe.wait_ge(s_q, KD * (b + 1))
                    if b >= 2:
                        pe.wait_ge(s_f, b - 1)
                    for m in range(KD):
                        last = pe.matmul(bank(4 + b % 2), w["c0_wkT"][:, m, :], qT[:, m, b * L:(b + 1) * L],
                                         start=(m == 0), stop=(m == KD - 1))
                    last.then_inc(s_fps, 1)

                def scores(t):
                    b = t // TB
                    pe.wait_ge(s_pr, t) if t >= 1 else pe.wait_ge(s_q, NQ)
                    if t % TB == 0:
                        pe.wait_ge(s_f, b + 1)
                    for q in range(0, CTX, BANK):
                        e = min(q + BANK, CTX)
                        last = pe.matmul(S_PS[:, q:e], qk[:, t * P:(t + 1) * P],
                                         env.ctxT[:, b * CTX + q:b * CTX + e], start=True, stop=True)
                    last.then_inc(s_sps, 1)

                def turn(t, n):
                    k0, k1 = ROUNDS[n]
                    if n == 0:
                        pe.wait_ge(s_pr, t + 1)
                        if t == 0:
                            pe.wait_ge(s_f, B)
                    else:
                        pe.wait_ge(s_pTd, t + 1)
                    if 2 * t + n >= 1:
                        pe.wait_ge(s_pTa, 2 * t + n)
                    for kt in range(k0, k1):
                        rows = ctx_rows(kt)
                        last = pe.transpose(P_PS[0:rows, (kt - k0) * P:(kt - k0 + 1) * P],
                                            pr[:, t % 2, kt * P:kt * P + rows], env.ident)
                    last.then_inc(s_pps, 1)

                def values(t):
                    b = t // TB
                    if t >= 1:
                        pe.wait_ge(s_z, t)
                    for n, (k0, k1) in enumerate(ROUNDS):
                        pe.wait_ge(s_pTa, 2 * t + n + 1)
                        for kt in range(k0, k1):
                            rows = ctx_rows(kt)
                            last = pe.matmul(M_PS[:, 0:P], env.ctx[0:rows, b, kt, :], pT[0:rows, t % 2, kt, :],
                                             start=(kt == 0), stop=(kt == CT - 1))
                    last.then_inc(s_zps, 1)

                def project(t):
                    pe.wait_ge(s_z, t + 1)
                    if t >= 1:
                        pe.wait_ge(s_xT, t)
                    else:
                        pe.wait_ge(s_cq, 1)
                    pe.matmul(O_PS[:, 0:D], zT[:, t % 2, :], w["c0_wv"], start=True, stop=True).then_inc(s_ops, 1)

                def back(t):
                    pe.wait_ge(s_xn, t + 1)
                    for k in range(KD):
                        last = pe.transpose(O_PS[:, D + k * P:D + (k + 1) * P], env.x[:, t, k * P:(k + 1) * P], env.ident)
                    last.then_inc(s_xps, 1)

                for n in range(NQ):
                    half(n)
                    if n % KD and n >= 3:
                        fold(n // KD - 1)
                fold(B - 1)
                for t in range(T):
                    for m in range(KD):
                        last = pe.matmul(O_PS[:, t:t + 1], qT[:, m, t * P:(t + 1) * P], w["c0_bk"][:, m:m + 1],
                                         start=(m == 0), stop=(m == KD - 1))
                last.then_inc(s_cps, 1)
                for t in range(T + 3):
                    if 1 <= t <= T:
                        turn(t - 1, 0)
                    if t >= 3:
                        back(t - 3)
                    if t < T:
                        scores(t)
                    if 2 <= t <= T + 1:
                        project(t - 2)
                    if 1 <= t <= T:
                        turn(t - 1, 1)
                        values(t - 1)

            @block.scalar
            def _(act):
                for n in range(NQ):
                    b, m = divmod(n, KD)
                    act.wait_ge(s_qps, n + 1)
                    act.activation(qT[:, m, b * L:(b + 1) * L], bank(n % 4), ACT.Identity,
                                   bias=w["c0_bq"][:, m:m + 1]).then_inc(s_q, 1)

                def turned(t, n):
                    act.wait_ge(s_pps, 2 * t + n + 1)
                    if t >= 2 and n == 0:
                        act.wait_ge(s_zps, t - 1)
                    k0, k1 = ROUNDS[n]
                    last = act.activation(pT[:, t % 2, k0:k0 + SPLIT, :].rearrange("p k n -> p (k n)"),
                                          P_PS[:, 0:BANK], ACT.Copy)
                    if n == 1:
                        rows = ctx_rows(CT - 1)
                        last = act.activation(pT[0:rows, t % 2, CT - 1, :], P_PS[0:rows, BANK:BANK + P], ACT.Copy)
                    last.then_inc(s_pTa, 1)

                for t in range(T + 3):
                    if 1 <= t <= T:
                        turned(t - 1, 0)
                    if t >= 3:
                        act.wait_ge(s_xps, t - 2)
                        act.activation(env.xT[:, :, (t - 3) * P:(t - 2) * P],
                                       O_PS[:, D:2 * D].rearrange("p (k n) -> p k n", k=KD), ACT.Copy).then_inc(s_xT, 1)
                    if 1 <= t <= T:
                        turned(t - 1, 1)
                    if t < T:
                        act.wait_ge(s_nb, t + 1)
                        act.activation(pr[:, t % 2, :], S_PS[:, 0:CTX], ACT.Exp, bias=nb[:, t:t + 1],
                                       accum_out=rsum[:, t:t + 1]).then_inc(s_pr, 1)
                    if 1 <= t <= T:
                        act.wait_ge(s_zps, t)
                        act.activation(zT[:, (t - 1) % 2, :], M_PS[:, 0:P], ACT.Copy).then_inc(s_z, 1)

            @block.gpsimd
            def _(pool):
                for t in range(T):
                    last = pool.tensor_tensor(env.x[:, t, :], env.x[:, t, :], w["c0_bv"], ALU.add)
                last.then_inc(s_xb, 1)
                for t in range(T):
                    pool.wait_ge(s_ve, t + 1)
                    pool.tensor_tensor(rstd[:, :], ve[:, :], env.mhalf[:, 0:1], ALU.pow).then_inc(s_rstd, 1)

            @block.vector
            def _(dve):
                steps = [0]

                def link(ins):
                    steps[0] += 1
                    ins.then_inc(s_dve, 1)
                    dve.wait_ge(s_dve, steps[0])

                def turned(t):
                    dve.wait_ge(s_pps, 2 * t + 1)
                    if t >= 2:
                        dve.wait_ge(s_zps, t - 1)
                    dve.tensor_copy(pT[:, t % 2, SPLIT:2 * SPLIT, :].rearrange("p k n -> p (k n)"),
                                    P_PS[:, BANK:2 * BANK]).then_inc(s_pTd, 1)

                def shift(t):
                    dve.wait_ge(s_sps, t + 1)
                    dve.tensor_reduce(mxs[:, t:t + 1], S_PS[:, 0:CTX], AX, ALU.max).then_inc(s_mx, 1)
                    dve.wait_ge(s_mx, t + 1)
                    link(dve.tensor_tensor(top[:, t:t + 1], mxs[:, t:t + 1], cq[:, t:t + 1], ALU.add))
                    dve.tensor_tensor(nb[:, t:t + 1], cq[:, t:t + 1], top[:, t:t + 1], ALU.subtract).then_inc(s_nb, 1)

                def norm(t):
                    dve.wait_ge(s_pr, t + 1)
                    link(dve.reciprocal(rinv[:, t:t + 1], rsum[:, t:t + 1]))
                    if t == 0:
                        dve.wait_ge(s_xb, 1)
                    dve.wait_ge(s_ops, t + 1)
                    dve.scalar_tensor_tensor(r[:, t % 2, :], O_PS[:, 0:D], rinv[:, t:t + 1], env.x[:, t, :],
                                             ALU.mult, ALU.add).then_inc(s_r, 1)
                    dve.wait_ge(s_r, t + 1)
                    link(dve.bn_stats(st[:, :], r[:, t % 2, :]))
                    link(dve.bn_aggr(mv[:, :], st[:, :]))
                    dve.tensor_scalar(ve[:, :], mv[:, 1:2], EPS, None, ALU.add).then_inc(s_ve, 1)
                    dve.wait_ge(s_rstd, t + 1)
                    dve.tensor_scalar(env.x[:, t, :], r[:, t % 2, :], mv[:, 0:1], rstd[:, 0:1],
                                      ALU.subtract, ALU.mult).then_inc(s_xn, 1)

                for b in range(B):
                    dve.wait_ge(s_fps, b + 1)
                    dve.tensor_copy(qk[:, b * L:(b + 1) * L], bank(4 + b % 2)).then_inc(s_f, 1)
                dve.wait_ge(s_cps, 1)
                dve.tensor_copy(cq[:, :], O_PS[:, 0:T]).then_inc(s_cq, 1)
                dve.wait_ge(s_cq, 1)
                for t in range(T + 2):
                    if 1 <= t <= T:
                        turned(t - 1)
                    if t < T:
                        shift(t)
                    if t >= 2:
                        norm(t - 2)


def l0_ffn(nc, env):
    w, PS = env.w, env.PS
    R = 3
    with ExitStack() as c_:
        sb, sem = env.alloc(c_)
        iota, thr, iota32 = env.iota16, env.thr16, env.iota32
        tiles = lambda c: list(range(c * TB, (c + 1) * TB))
        hT = sb("hT", [P, FC, N], F32)
        slot = sb("slot", [P, T], I32)
        xs = sb("xs", [P, T, D], F32)
        s_lps = sem("f_lps")
        s_dve = sem("f_dve")
        s_top = sem("f_top")
        s_ex = sem("f_exp")
        s_cnt = sem("f_cnt")
        s_rank = sem("f_rank")
        s_slot = sem("f_slot")
        s_tab = sem("f_tab")
        s_xs = sem("f_xs")
        s_scat = sem("f_scat", keep=True)
        s_sps = sem("f_sps")
        s_sg = sem("f_sg")
        s_sh = sem("f_sh")
        table = sb("table", [1, ETILES], I32)

        with ExitStack() as c2:
            sb2, _ = env.alloc(c2)
            lg = sb2("lg", [P, T, E], F32)
            top = sb2("top1", [P, T], F32)
            lt = sb2("lt", [P, T, E], F32)
            idx = sb2("idx", [P, T], F32)
            oh = sb2("oh", [P, T, E], F32)
            en = sb2("en", [P, T], F32)
            e1 = sb2("e1", [P, T], F32)
            sg = sb2("sgm", [P, T], F32)
            pre = sb2("pre", [P, T + 1, E], F32)
            nt3 = sb2("nt3", [P, E, E], F32)
            cs = sb2("cs", [P, 2, 2 * E], F32)
            nt = sb2("nt", [P, E], F32)
            st = sb2("st1", [P, E], F32)
            sbase = sb2("sbase", [P, E], F32)
            sf = sb2("sf", [P, T], F32)
            le = sb2("le", [1, ETILES, E], F32)
            tf = sb2("tf", [1, ETILES], F32)
            tf2 = sb2("tf2", [1, ETILES], F32)
            silu = sb2("silu", [P, 2, L], F32)
            items = [(c, f) for c in range(B) for f in range(FC)]

            with nc.Block() as block:

                @block.tensor
                def _(pe):
                    for t in range(T):
                        for k in range(KD):
                            last = pe.matmul(PS[:, t * E:(t + 1) * E], env.xT[:, k, t * P:(t + 1) * P],
                                             w["f_router"][:, k, :], start=(k == 0), stop=(k == KD - 1))
                    last.then_inc(s_lps, 1)

                    def shared(n):
                        c, f = items[n]
                        if n >= 2:
                            pe.wait_ge(s_sh, n - 1)
                        for e, name in enumerate(("f_wg", "f_wu")):
                            o = PS[:, (2 + 2 * (n % 2) + e) * BANK:(3 + 2 * (n % 2) + e) * BANK]
                            for k in range(KD):
                                last = pe.matmul(o, w[name][:, k, f * P:(f + 1) * P], env.xT[:, k, c * L:(c + 1) * L],
                                                 start=(k == 0), stop=(k == KD - 1))
                        last.then_inc(s_sps, 1)

                    for n in range(2):
                        shared(n)
                    pe.wait_ge(s_cnt, 1)
                    pe.matmul(PS[:, BANK:BANK + E], env.tri, pre[:, T, :], start=True, stop=True)
                    pe.matmul(PS[:, BANK + E:BANK + 2 * E], env.ones, pre[:, T, :], start=True,
                              stop=True).then_inc(s_rank, 1)
                    for n in range(2, len(items)):
                        shared(n)

                @block.scalar
                def _(act):
                    act.wait_ge(s_top, 1)
                    act.activation(en[:, :], top[:, :], ACT.Exp, scale=-1.0).then_inc(s_ex, 1)
                    for n in range(len(items)):
                        act.wait_ge(s_sps, n + 1)
                        if n >= 2:
                            act.wait_ge(s_sh, n - 1)
                        act.activation(silu[:, n % 2, :], PS[:, (2 + 2 * (n % 2)) * BANK:(3 + 2 * (n % 2)) * BANK],
                                       ACT.Silu).then_inc(s_sg, 1)

                @block.gpsimd
                def _(pool):
                    pool.wait_ge(s_slot, 1)
                    for t in range(T):
                        pool.wait_ge(s_xs, t + 1)
                        pool.indirect_dma_start(out=env.xg, out_offset=bass.IndirectOffsetOnAxis(ap=slot[:, t:t + 1], axis=0),
                                                in_=xs[:, t, :], in_offset=None).then_inc(s_scat, 16)
                    pool.wait_ge(s_scat, 16 * T)

                @block.vector
                def _(dve):
                    steps = [0]

                    def link(ins):
                        steps[0] += 1
                        ins.then_inc(s_dve, 1)
                        dve.wait_ge(s_dve, steps[0])

                    def shared(n):
                        c, f = items[n]
                        dve.wait_ge(s_sg, n + 1)
                        dve.tensor_tensor(hT[:, f, c * L:(c + 1) * L], silu[:, n % 2, :],
                                          PS[:, (3 + 2 * (n % 2)) * BANK:(4 + 2 * (n % 2)) * BANK],
                                          ALU.mult).then_inc(s_sh, 1)

                    te = lambda a: a.unsqueeze(2).to_broadcast([P, T, E])
                    ie = iota.unsqueeze(1).to_broadcast([P, T, E])
                    dve.wait_ge(s_lps, 1)
                    link(dve.tensor_copy(lg[:, :, :].rearrange("p t e -> p (t e)"), PS[:, 0:T * E]))
                    dve.tensor_reduce(top[:, :], lg[:, :, :], AX, ALU.max).then_inc(s_top, 1)
                    dve.wait_ge(s_top, 1)
                    link(dve.tensor_tensor(lt[:, :, :], lg[:, :, :], te(top[:, :]), ALU.is_lt))
                    link(dve.scalar_tensor_tensor(lg[:, :, :], lt[:, :, :], float(E), ie, ALU.mult, ALU.add))
                    link(dve.tensor_reduce(idx[:, :], lg[:, :, :], AX, ALU.min))
                    dve.memset(pre[:, 0, :], 0.0)
                    link(dve.tensor_tensor(oh[:, :, :], ie, te(idx[:, :]), ALU.is_equal))
                    for t in range(T):
                        ins = dve.tensor_tensor(pre[:, t + 1, :], pre[:, t, :], oh[:, t, :], ALU.add)
                        if t < T - 1:
                            link(ins)
                    ins.then_inc(s_cnt, 1)
                    dve.wait_ge(s_ex, 1)
                    link(dve.tensor_scalar(e1[:, :], en[:, :], 1.0, None, ALU.add))
                    link(dve.reciprocal(sg[:, :], e1[:, :]))
                    for t in range(T):
                        dve.tensor_scalar(xs[:, t, :], env.x[:, t, :], sg[:, t:t + 1], None, ALU.mult).then_inc(s_xs, 1)
                    link(dve.memset(cs[:, :, :], 0.0))
                    dve.wait_ge(s_rank, 1)
                    link(dve.tensor_tensor(nt3[:, :, :], PS[:, BANK + E:BANK + 2 * E].unsqueeze(2).to_broadcast([P, E, E]),
                                           thr.unsqueeze(1).to_broadcast([P, E, E]), ALU.is_gt))
                    link(dve.tensor_reduce(nt[:, :], nt3[:, :, :], AX, ALU.add))
                    link(dve.tensor_copy(cs[:, 0, E:2 * E], nt[:, :]))
                    for n in range(4):
                        a, b, d = n % 2, (n + 1) % 2, 1 << n
                        link(dve.tensor_tensor(cs[:, b, E:2 * E], cs[:, a, E:2 * E], cs[:, a, E - d:2 * E - d], ALU.add))
                    end = cs[:, 0, E:2 * E]
                    link(dve.tensor_tensor(st[:, :], end, nt[:, :], ALU.subtract))
                    link(dve.scalar_tensor_tensor(sbase[:, :], st[:, :], float(P), PS[:, BANK:BANK + E], ALU.mult, ALU.add))
                    link(dve.tensor_tensor(lt[:, :, :], pre[:, 0:T, :], sbase[:, :].unsqueeze(1).to_broadcast([P, T, E]), ALU.add))
                    link(dve.tensor_tensor(lg[:, :, :], lt[:, :, :], oh[:, :, :], ALU.mult))
                    link(dve.tensor_reduce(sf[:, :], lg[:, :, :], AX, ALU.add))
                    dve.tensor_copy(slot[:, :], sf[:, :]).then_inc(s_slot, 1)
                    link(dve.tensor_tensor(le[:, :, :], end[0:1, :].unsqueeze(1).to_broadcast([1, ETILES, E]),
                                           iota32[0:1, :].unsqueeze(2).to_broadcast([1, ETILES, E]), ALU.is_le))
                    link(dve.tensor_reduce(tf[:, :], le[:, :, :], AX, ALU.add))
                    link(dve.tensor_scalar(tf2[:, :], tf[:, :], float(E - 1), None, ALU.min))
                    dve.tensor_copy(table[:, :], tf2[:, :]).then_inc(s_tab, 1)
                    for n in range(len(items)):
                        shared(n)

        with ExitStack() as c2:
            sb2, sem2 = env.alloc(c2)
            wgu = sb2("wgu", [P, R, KD, 2 * F], F32)
            wdn = sb2("wdn", [P, R, FC, D], F32)
            xt = sb2("xt", [P, R, D], F32)
            xtT = sb2("xtT", [P, R, KD, P], F32)
            sgt = sb2("sgt", [P, R, F], F32)
            ht = sb2("ht", [P, R, FC, P], F32)
            yt = sb2("yt", [P, R, D], F32)
            s_ldx = [sem2(f"e_ldx{u}") for u in range(R)]
            s_ldw = [sem2(f"e_ldw{u}") for u in range(R)]
            s_tps = sem2("e_tps")
            s_t = sem2("e_t")
            s_gu = sem2("e_gu")
            s_g = sem2("e_g")
            s_h = sem2("e_h")
            s_yps = sem2("e_yps")
            s_y = sem2("e_y")
            s_yo = [sem2(f"e_yo{u}", keep=True) for u in range(R)]
            GU = lambda u: PS[:, 2 * u * BANK:2 * (u + 1) * BANK]
            T_PS, Y_PS = PS[:, 6 * BANK:7 * BANK], PS[:, 7 * BANK:8 * BANK]
            LAST = ETILES - 1
            ROUNDS = (ETILES - 2) // R

            with nc.Block() as block:

                @block.sync
                def _(sp):
                    def load(j, u):
                        e = sp.value_load(table[0:1, bass.ds(j, 1)], min_val=0, max_val=E - 1)
                        sp.dma_start(xt[:, u, :], env.xg_t[j]).then_inc(s_ldx[u], 16)
                        sp.dma_start(wgu[:, u, :, :], env.gu_t[e].rearrange("(k p) n -> p k n", p=P)).then_inc(s_ldw[u], 16)
                        sp.dma_start(wdn[:, u, :, :], env.dn_t[e].rearrange("(k p) n -> p k n", p=P)).then_inc(s_ldw[u], 16)

                    for j in range(R):
                        load(j, j)
                    with sp.Fori(0, (ETILES - R) // R) as i:
                        for u in range(R):
                            sp.wait_ge(s_yps, i * R + u + 1)
                            load(i * R + u + R, u)
                    for j in range(R + (ETILES - R) // R * R, ETILES):
                        sp.wait_ge(s_yps, j - R + 1)
                        load(j, j % R)

                @block.tensor
                def _(pe):
                    def turn(j, u, n):
                        pe.wait_ge(s_ldx[u], 16 * (n + 1))
                        pe.wait_ge(s_t, j + 1)
                        for k in range(KD):
                            last = pe.transpose(T_PS[:, k * P:(k + 1) * P], xt[:, u, k * P:(k + 1) * P], env.ident)
                        last.then_inc(s_tps, 1)

                    def gate_up(j, u, n):
                        pe.wait_ge(s_ldw[u], 32 * (n + 1))
                        pe.wait_ge(s_t, j + 2)
                        for f in range(2 * FC):
                            for k in range(KD):
                                last = pe.matmul(GU(u)[:, f * P:(f + 1) * P], wgu[:, u, k, f * P:(f + 1) * P],
                                                 xtT[:, u, k, :], start=(k == 0), stop=(k == KD - 1))
                        last.then_inc(s_gu, 1)

                    def down(j, u):
                        pe.wait_ge(s_h, j + 1)
                        pe.wait_ge(s_y, j + 1)
                        for f in range(FC):
                            last = pe.matmul(Y_PS[:, 0:D], ht[:, u, f, :], wdn[:, u, f, :],
                                             start=(f == 0), stop=(f == FC - 1))
                        last.then_inc(s_yps, 1)

                    turn(0, 0, 0)
                    gate_up(0, 0, 0)
                    turn(1, 1, 0)
                    with pe.Fori(0, ROUNDS) as i:
                        for m in range(R):
                            j = i * R + (m + 1)
                            gate_up(j, (m + 1) % R, i + (m + 1) // R)
                            turn(j + 1, (m + 2) % R, i + (m + 2) // R)
                            down(j - 1, m)
                    gate_up(LAST, LAST % R, LAST // R)
                    down(LAST - 1, (LAST - 1) % R)
                    down(LAST, LAST % R)

                @block.scalar
                def _(act):
                    def turn(j, u):
                        act.wait_ge(s_tps, j + 1)
                        act.activation(xtT[:, u, :, :].rearrange("p k n -> p (k n)"), T_PS[:, 0:D], ACT.Copy).then_inc(s_t, 1)

                    def gate(j, u):
                        act.wait_ge(s_gu, j + 1)
                        act.activation(sgt[:, u, :], GU(u)[:, 0:F], ACT.Silu).then_inc(s_g, 1)

                    act.sem_inc(s_t, 1)
                    turn(0, 0)
                    gate(0, 0)
                    turn(1, 1)
                    with act.Fori(0, ROUNDS) as i:
                        for m in range(R):
                            j = i * R + (m + 1)
                            gate(j, (m + 1) % R)
                            turn(j + 1, (m + 2) % R)
                    gate(LAST, LAST % R)

                @block.vector
                def _(dve):
                    def hidden(j, u):
                        dve.wait_ge(s_g, j + 1)
                        dve.tensor_tensor(ht[:, u, :, :].rearrange("p f n -> p (f n)"), sgt[:, u, :],
                                          GU(u)[:, F:2 * F], ALU.mult).then_inc(s_h, 1)

                    def out(j, u, n):
                        dve.wait_ge(s_yps, j + 1)
                        if n is not None:
                            dve.wait_ge(s_yo[u], 16 * n)
                        dve.tensor_copy(yt[:, u, :], Y_PS[:, 0:D]).then_inc(s_y, 1)

                    dve.sem_inc(s_y, 1)
                    hidden(0, 0)
                    for j in range(1, R + 1):
                        hidden(j, j % R)
                        out(j - 1, j - 1, None)
                    with dve.Fori(1, ROUNDS) as i:
                        for m in range(R):
                            j = i * R + (m + 1)
                            hidden(j, (m + 1) % R)
                            out(j - 1, m, i)
                    hidden(LAST, LAST % R)
                    out(LAST - 1, (LAST - 1) % R, (LAST - 1) // R)
                    out(LAST, LAST % R, LAST // R)

                @block.gpsimd
                def _(pool):
                    def out(j, u):
                        pool.wait_ge(s_y, j + 2)
                        pool.dma_start(env.yg_t[j], yt[:, u, :]).then_inc(s_yo[u], 16)

                    with pool.Fori(0, ETILES // R) as i:
                        for u in range(R):
                            out(i * R + u, u)
                    for j in range(ETILES // R * R, ETILES):
                        out(j, j % R)
                    for u in range(R):
                        pool.wait_ge(s_yo[u], 16 * ((ETILES - u + R - 1) // R))

        with ExitStack() as c2:
            _, sem2 = env.alloc(c2)
            tail = Tail(env, c2, "t2", (0, 2, 4), tiles, FC)
            s_ga = [sem2(f"f_ga{c}", keep=True) for c in range(B)]

            with nc.Block() as block:

                @block.gpsimd
                def _(pool):
                    for t in range(T):
                        pool.indirect_dma_start(out=xs[:, t, :], out_offset=None, in_=env.yg,
                                                in_offset=bass.IndirectOffsetOnAxis(ap=slot[:, t:t + 1], axis=0)
                                                ).then_inc(s_ga[t // TB], 16)
                    for c in range(B):
                        pool.wait_ge(s_ga[c], 16 * TB)
                        tail.pool_residual(pool, c, lambda t: xs[:, t, :])
                    for c in range(B):
                        tail.pool_rstd(pool, c)

                @block.tensor
                def _(pe):
                    for c in range(B):
                        tail.pe_proj(pe, c, lambda k: w["f_wd"][:, k, :],
                                     lambda i, k: hT[:, k, (c * TB + i) * P:(c * TB + i + 1) * P])
                        if c >= 1:
                            tail.pe_out(pe, c - 1)
                    tail.pe_out(pe, B - 1)

                @block.scalar
                def _(act):
                    for c in range(B):
                        tail.act_out(act, c)

                @block.vector
                def _(dve):
                    for c in range(B):
                        tail.dve_sum(dve, c)
                        tail.dve_norm(dve, c)


def l1_attn_prep(nc, env):
    w, PS = env.w, env.PS
    blocks = [(b, name, m) for b in range(B) for name in ("q", "k") for m in range(KD)]
    vitems = [(b, tuple(range(TB)), P) for b in range(B)]
    with ExitStack() as c:
        def bias(n):
            b, name, m = blocks[n]
            return w["s_b" + name][:, m:m + 1], w["s_b" + name][:, 1 - m:2 - m]

        def dst(n):
            b, name, m = blocks[n]
            return (env.qs if name == "q" else env.ks).rearrange("(b p m s) l -> b m p s l", b=B, p=P, m=KD)[b][m]

        slots = lambda name: Q_PARTS if name == "q" else K_PARTS
        sp_ = Split(env, c, "sqk", L, bias, dst, lambda n: slots(blocks[n][1]), 4,
                        rope=lambda n: (env.cos, env.sin_neg if blocks[n][2] == 0 else env.sin))
        val = Values(env, c, "sv", vitems, w["s_bv"], env.vs)
        QK = lambda n: PS[:, 2 * (n // 2 % 3) * BANK:2 * (n // 2 % 3 + 1) * BANK]
        V = PS[:, 6 * BANK:8 * BANK]
        PER = len(blocks) // B

        with nc.Block() as block:

            @block.tensor
            def _(pe):
                for n, (b, name, m) in enumerate(blocks):
                    if m == 0 and n >= 6:
                        sp_.freed(pe, n - 5)
                    for k in range(KD):
                        last = pe.matmul(QK(n)[:, m * L:(m + 1) * L], w["s_w" + name][:, k, m * P:(m + 1) * P],
                                         env.xT[:, k, b * L:(b + 1) * L], start=(k == 0), stop=(k == KD - 1))
                    last.then_inc(sp_.s_full, 1)
                    if n % PER == PER - 1:
                        if b >= 1:
                            pe.wait_ge(val.s_v, b)
                        for j in range(TB):
                            t = b * TB + j
                            for k in range(KD):
                                last = pe.matmul(V[:, j * D:(j + 1) * D], env.xT[:, k, t * P:(t + 1) * P],
                                                 w["s_wv"][:, k, :], start=(k == 0), stop=(k == KD - 1))
                        last.then_inc(val.s_full, 1)

            @block.scalar
            def _(act):
                for n in range(len(blocks) + 1):
                    if n < len(blocks):
                        sp_.act_hi(act, n, None)
                    if n >= 1:
                        sp_.act_mid(act, n - 1)

            @block.vector
            def _(dve):
                for n in range(len(blocks) + 1):
                    if n < len(blocks):
                        m = n % KD
                        sp_.dve_rot(dve, n, n - m + KD, QK(n)[:, m * L:(m + 1) * L], QK(n)[:, (1 - m) * L:(2 - m) * L])
                    if n >= 1:
                        sp_.dve_rest(dve, n - 1)
                        if (n - 1) % PER == PER - 1:
                            val.dve_copy(dve, (n - 1) // PER, V)

            @block.gpsimd
            def _(pool):
                val.pool_init(pool)
                for n in range(len(blocks) + 1):
                    if n < len(blocks):
                        sp_.pool_whole(pool, n)
                    if n >= 1:
                        sp_.pool_lo(pool, n - 1)

            @block.sync
            def _(sp):
                for n in range(len(blocks)):
                    sp_.sp_out(sp, n)
                    if n % PER == PER - 1:
                        val.sp_out(sp, n // PER)
                sp_.sp_end(sp, len(blocks))
                val.sp_end(sp)


def l1_xattn_prep(nc, env):
    w, PS = env.w, env.PS
    NB = B * KD
    with ExitStack() as c:
        sp_ = Split(env, c, "xq", L, lambda n: w["x_bq"][:, n % KD:n % KD + 1],
                    lambda n: env.qx.rearrange("(n p s) l -> n p s l", p=P, s=len(Q_PARTS))[n], lambda n: Q_PARTS, 4)
        Q = lambda n: PS[:, (n % 4) * BANK:(n % 4 + 1) * BANK]

        with nc.Block() as block:

            @block.tensor
            def _(pe):
                for n in range(NB):
                    b, m = divmod(n, KD)
                    if n >= 4:
                        sp_.freed(pe, n - 4)
                    for k in range(KD):
                        last = pe.matmul(Q(n), w["x_wq"][:, k, m * P:(m + 1) * P], env.xT[:, k, b * L:(b + 1) * L],
                                         start=(k == 0), stop=(k == KD - 1))
                    last.then_inc(sp_.s_full, 1)

            @block.scalar
            def _(act):
                for n in range(NB + 1):
                    if n < NB:
                        sp_.act_hi(act, n, Q(n))
                    if n >= 1:
                        sp_.act_mid(act, n - 1)

            @block.vector
            def _(dve):
                for n in range(NB):
                    sp_.dve_rest(dve, n, Q(n))

            @block.gpsimd
            def _(pool):
                for n in range(NB):
                    sp_.pool_lo(pool, n)

            @block.sync
            def _(sp):
                for n in range(NB):
                    sp_.sp_out(sp, n)
                sp_.sp_end(sp, NB)


def heads_loop(nc, env, name, NK, causal, qp, kp, vp, OT):
    PS = env.PS
    KT = -(-NK // P)
    R = 3
    STEPS = KT * G
    rows = lambda kt: min(P, NK - kt * P)
    q0 = lambda kt: kt * P if causal else 0
    HALF = 2 * BANK
    if causal:
        units = [(h, pair) for h in range(G) for pair in range(TB // 2)]
    else:
        units = [(h, qt, e) for h in range(G) for qt in range(TB) for e in range(2)]
    U = len(units)
    EARLY = U // 2 + causal
    M_STEP = (U - EARLY) * STEPS // U + 3
    S1 = STEPS + 1
    def pos(g, n):
        return n + (n > M_STEP and not (type(g) is int and g == GROUPS - 1))

    M_POS = M_STEP + 1
    COLS = G * TB
    KLOADS = 1 if causal else len(K_PARTS)
    LEAD = 4
    VLOADS = 1 if NK % P == 0 else 2
    ROUNDS = (GROUPS - R - 1) // R
    assert U % 2 == 0 and GROUPS == R * ROUNDS + R + 1

    with ExitStack() as c:
        sb, sem = env.alloc(c)
        Kst = sb(name + "_K", [P, R, G, NK], BF16)
        Qst = sb(name + "_Q", [P, R, G, L], BF16)
        Vg = sb(name + "_V", [P, R, KT, G * VW], F32)
        Pr = sb(name + "_P", [P, R, G, L], F32)
        part = sb(name + "_part", [P, COLS, 1 if causal else 2], F32)
        mx = sb(name + "_mx", [P, COLS], F32)
        mh = sb(name + "_mh", [P, 2, COLS], BF16)
        mrow = sb(name + "_mrow", [2 * COLS, P], BF16)
        s_ones = sem(name + "_ones")
        s_k = [sem(f"{name}_k{u}") for u in range(R)]
        s_q = [sem(f"{name}_q{u}") for u in range(R)]
        s_v = [sem(f"{name}_v{u}") for u in range(R)]
        s_mq = [sem(f"{name}_mq{u}") for u in range(R)]
        s_1 = sem(name + "_1")
        s_1free = sem(name + "_1free")
        s_step = sem(name + "_step")
        s_mh = sem(name + "_mh")
        s_2 = sem(name + "_2")
        s_exp = sem(name + "_exp")
        s_pv = sem(name + "_pv")
        s_ot = sem(name + "_ot")
        ring1 = lambda n: PS[:, (n % 2) * HALF:(n % 2 + 1) * HALF]
        ring2 = lambda n: PS[:, (4 + n % R) * BANK:(5 + n % R) * BANK]
        O_PS = PS[:, 7 * BANK:8 * BANK]
        ONE = QK_ROWS


        with nc.Block() as block:

            @block.sync
            def _(sp):
                def load_kq(g, u):
                    sp.dma_start(Qst[0:QK_ROWS, u, :, :], qp(g)).then_inc(s_q[u], 16)
                    if causal:
                        sp.dma_start(Kst[0:QK_ROWS, u, :, :], kp(g)).then_inc(s_k[u], 16)
                    else:
                        for j, part in enumerate(K_PARTS):
                            sp.dma_start(Kst[j:QK_ROWS:len(K_PARTS), u, :, :], kp(g, part)).then_inc(s_k[u], 16)

                def load_v(g, u):
                    full = NK // P
                    sp.dma_start(Vg[:, u, 0:full, :], vp[g][0:full * P, :].rearrange("(k p) n -> p k n", p=P)).then_inc(s_v[u], 16)
                    if full < KT:
                        sp.dma_start(Vg[0:rows(full), u, full, :], vp[g][full * P:NK, :]).then_inc(s_v[u], 16)

                def maxima(items_before, u):
                    sp.wait_ge(s_exp, items_before + 1)
                    for e in range(2):
                        sp.dma_start(Qst[ONE + e:ONE + e + 1, u, :, :].rearrange("p h (t n) -> p (h t) n", n=P),
                                     mrow[e * COLS:(e + 1) * COLS, :]).then_inc(s_mq[u], 16)

                def reload(g, u):
                    sp.wait_ge(s_2, g * S1 + (1 + S1))
                    load_kq(g + R, u)
                    sp.wait_ge(s_pv, g * KT + (R + KT))
                    load_v(g + R, u)

                for g in range(R):
                    load_kq(g, g)
                    load_v(g, g)
                maxima(0, 0)
                with sp.Fori(0, ROUNDS) as i:
                    for u in range(R):
                        g = i * R + u
                        maxima(g * S1 + (1 + M_POS), (u + 1) % R)
                        reload(g, u)
                for g in range(ROUNDS * R, GROUPS - 1):
                    maxima(g * S1 + (1 + M_POS), (g + 1) % R)
                    if g + R < GROUPS:
                        reload(g, g % R)

            @block.gpsimd
            def _(pool):
                for u in range(R):
                    pool.memset(Kst[ONE:ONE + 2, u, :, :].rearrange("p h n -> p (h n)"), 1.0).then_inc(s_ones, 1)

            @block.tensor
            def _(pe):
                def unit(g, u, n, first):
                    if n == 0:
                        pe.wait_ge(s_k[u], 16 * KLOADS * (first + 1))
                        pe.wait_ge(s_q[u], 16 * (first + 1))
                    if n >= 2 or type(g) is not int or g:
                        pe.wait_ge(s_1free, g * U + (n - 1))
                    o = ring1(n)
                    q = lambda h, qt: Qst[0:QK_ROWS, u, h, qt * P:(qt + 1) * P]
                    if causal:
                        h, pair = units[n]
                        for e in range(2):
                            qt = 2 * pair + e
                            w_ = (qt + 1) * P
                            pe.matmul(o[:, e * BANK:e * BANK + w_], q(h, qt), Kst[0:QK_ROWS, u, h, 0:w_], start=True, stop=False)
                            last = pe.matmul(o[:, e * BANK + w_ - P:e * BANK + w_], env.identb, env.mask_q, start=False, stop=True)
                    else:
                        h, qt, e = units[n]
                        for k in range(e * HALF, min((e + 1) * HALF, NK), BANK):
                            w_ = min(BANK, NK - k)
                            last = pe.matmul(o[:, k - e * HALF:k - e * HALF + w_], q(h, qt), Kst[0:QK_ROWS, u, h, k:k + w_],
                                             start=True, stop=True)
                    last.then_inc(s_1, 1)

                def maxima(g, item):
                    pe.wait_ge(s_mh, g + 1)
                    pe.matmul(ring2(item)[0:2 * COLS, 0:P], mh[:, :, :].rearrange("p e c -> p (e c)"), env.identb,
                              start=True, stop=True).then_inc(s_2, 1)

                def bank_free(g, p):
                    if type(g) is not int or g or p >= 2:
                        pe.wait_ge(s_exp, g * S1 + (p - 1))

                def score(g, u, kt, h, first):
                    n = kt * G + h
                    if n == 0:
                        pe.wait_ge(s_ones, R)
                        pe.wait_ge(s_mq[u], 32 * (first + 1))
                    bank_free(g, pos(g, n))
                    o = ring2(1 + u * S1 + pos(g, n))
                    r = rows(kt)
                    w_ = L - q0(kt)
                    last = pe.matmul(o[0:r, 0:w_], Kst[0:ONE + 2, u, h, kt * P:kt * P + r], Qst[0:ONE + 2, u, h, q0(kt):L],
                                     start=True, stop=not causal)
                    if causal:
                        last = pe.matmul(o[0:r, 0:P], env.identb, env.mask_k, start=False, stop=True)
                    last.then_inc(s_2, 1)

                def values(g, u, kt, first):
                    r = rows(kt)
                    if kt == 0:
                        pe.wait_ge(s_v[u], 16 * VLOADS * (first + 1))
                        pe.wait_ge(s_ot, g + 1)
                    pe.wait_ge(s_exp, g * S1 + (2 + pos(g, kt * G + G - 1)))
                    for h in range(G):
                        last = pe.matmul(O_PS[h * VW:(h + 1) * VW, q0(kt):L], Vg[0:r, u, kt, h * VW:(h + 1) * VW],
                                         Pr[0:r, (u * KT + kt) % R, h, 0:L - q0(kt)],
                                         start=(kt == 0), stop=(kt == KT - 1), tile_position=(0, h * VW))
                    last.then_inc(s_pv, 1)

                def group(g, u, first, before, ahead):
                    after = [(1, n) for n in range(EARLY if before else LEAD, U)] * (ahead >= 1)
                    due = [min(len(after), -(-len(after) * (n + 1) // (M_STEP - 3))) for n in range(STEPS)]
                    if ahead >= 2:
                        late = STEPS - (M_STEP - 3)
                        due = [d + max(0, -(-EARLY * (n + 1 - (M_STEP - 3)) // late)) for n, d in enumerate(due)]
                        after += [(2, n) for n in range(EARLY)]
                    done = 0
                    for kt in range(KT):
                        for h in range(G):
                            n = kt * G + h
                            score(g, u, kt, h, first)
                            while done < due[n]:
                                a, m = after[done]
                                unit(g + a, (u + a) % R, m, first + (u + a) // R)
                                done += 1
                            if n == M_STEP and ahead:
                                bank_free(g, M_POS)
                                maxima(g + 1, 1 + u * S1 + M_POS)
                        if kt >= 1:
                            values(g, u, kt - 1, first)
                        elif before:
                            values(g - 1, (u + R - 1) % R, KT - 1, None)

                for n in range(U):
                    unit(0, 0, n, 0)
                for n in range(LEAD):
                    if n == 2:
                        maxima(0, 0)
                    unit(1, 1, n, 0)
                group(0, 0, 0, False, 2)
                with pe.Fori(0, ROUNDS) as i:
                    for v in range(1, R + 1):
                        group(i * R + v, v % R, i + v // R, True, 2)
                for g in range(ROUNDS * R + 1, GROUPS):
                    group(g, g % R, g // R, True, GROUPS - 1 - g)
                values(GROUPS - 1, (GROUPS - 1) % R, KT - 1, None)

            @block.scalar
            def _(act):
                def maxima(item, bank):
                    act.wait_ge(s_2, item + 1)
                    act.activation(mrow[:, :], ring2(bank)[0:2 * COLS, 0:P], ACT.Copy).then_inc(s_exp, 1)

                def output(g):
                    act.wait_ge(s_pv, g * KT + (R + KT))
                    act.activation(OT[:, bass.ds(g, 1), :].rearrange("p g n -> p (g n)"), O_PS, ACT.Copy).then_inc(s_ot, 1)

                def group(g, u, before, ahead):
                    for kt in range(KT):
                        act.wait_ge(s_pv, g * KT + (kt + 1))
                        r = rows(kt)
                        w_ = L - q0(kt)
                        for h in range(G):
                            n = kt * G + h
                            act.wait_ge(s_2, g * S1 + (2 + pos(g, n)))
                            act.activation(Pr[0:r, (u * KT + kt) % R, h, 0:w_], ring2(1 + u * S1 + pos(g, n))[0:r, 0:w_],
                                           ACT.Exp, scale=SCALE).then_inc(s_exp, 1)
                            if n == M_STEP and ahead:
                                maxima(g * S1 + (1 + M_POS), 1 + u * S1 + M_POS)
                        if kt == 0 and before:
                            output(g - 1)

                act.sem_inc(s_pv, R)
                act.sem_inc(s_ot, 1)
                maxima(0, 0)
                group(0, 0, False, 2)
                with act.Fori(0, ROUNDS) as i:
                    for v in range(1, R + 1):
                        group(i * R + v, v % R, True, 2)
                for g in range(ROUNDS * R + 1, GROUPS):
                    group(g, g % R, True, GROUPS - 1 - g)
                output(GROUPS - 1)

            @block.vector
            def _(dve):
                def maxima(g):
                    for n in range(U):
                        dve.wait_ge(s_1, g * U + (n + 1))
                        o = ring1(n)
                        if causal:
                            h, pair = units[n]
                            for e in range(2):
                                qt = 2 * pair + e
                                last = dve.tensor_reduce(part[:, h * TB + qt, :], o[:, e * BANK:e * BANK + (qt + 1) * P], AX, ALU.max)
                        else:
                            h, qt, e = units[n]
                            w_ = min(HALF, NK - e * HALF)
                            last = dve.tensor_reduce(part[:, h * TB + qt, e:e + 1], o[:, 0:w_], AX, ALU.max)
                        last.then_inc(s_1free, 1)
                    dve.wait_ge(s_1free, g * U + U)
                    dve.tensor_reduce(mx[:, :], part[:, :, :], AX, ALU.max).then_inc(s_step, 1)
                    dve.wait_ge(s_step, g * 2 + 1)
                    dve.tensor_scalar(mh[:, 0, :], mx[:, :], -1.0, None, ALU.mult).then_inc(s_step, 1)
                    dve.wait_ge(s_step, g * 2 + 2)
                    dve.scalar_tensor_tensor(mh[:, 1, :], mx[:, :], -1.0, mh[:, 0, :], ALU.mult, ALU.subtract).then_inc(s_mh, 1)

                maxima(0)
                with dve.Fori(1, GROUPS) as g:
                    maxima(g)


def heads_tail(nc, env, name, OT, wo, bo):
    w, PS = env.w, env.PS
    tiles = lambda c: list(range(c * TB, (c + 1) * TB))
    HW = G * VW
    with ExitStack() as c_:
        sb, sem = env.alloc(c_)
        tail = Tail(env, c_, name, (2, 4, 6), tiles, KD)
        rc = sb(name + "_rc", [P, 2, H], F32)
        cx = sb(name + "_cx", [P, 2, TB, D], F32)
        s_ops = sem(name + "_ops")
        s_rc = sem(name + "_rc")
        s_cx = sem(name + "_cx")

        with nc.Block() as block:

            @block.tensor
            def _(pe):
                def by_query(c):
                    for i in range(TB):
                        t = c * TB + i
                        if t >= 2:
                            pe.wait_ge(s_cx, t - 1)
                        for g in range(G):
                            last = pe.transpose(PS[:, (t % 2) * BANK + g * P:(t % 2) * BANK + (g + 1) * P],
                                                OT[:, c * G + g, i * P:(i + 1) * P], env.ident)
                        last.then_inc(s_ops, 1)

                for c in range(B):
                    by_query(c)
                    tail.pe_in(pe, c, lambda i: cx[:, c % 2, i, :], lambda i: pe.wait_ge(s_cx, c * TB + i + 1))
                    tail.pe_proj(pe, c, lambda k: wo[:, k, :])
                    if c >= 1:
                        tail.pe_out(pe, c - 1)
                tail.pe_out(pe, B - 1)

            @block.scalar
            def _(act):
                for c in range(B):
                    tail.act_in(act, c)
                    if c >= 1:
                        tail.act_out(act, c - 1)
                tail.act_out(act, B - 1)

            @block.gpsimd
            def _(pool):
                for c in range(B):
                    tail.pool_residual(pool, c, lambda t: bo)
                for c in range(B):
                    tail.pool_rstd(pool, c)

            @block.vector
            def _(dve):
                def context(c):
                    if c >= 2:
                        dve.wait_ge(tail.s_cT_ps, c - 1)
                    for i in range(TB):
                        t = c * TB + i
                        o = PS[:, (t % 2) * BANK:(t % 2 + 1) * BANK].rearrange("p (h n) -> p h n", n=VW)
                        dve.wait_ge(s_ops, t + 1)
                        dve.reciprocal(rc[:, t % 2, :], o[:, :, HD:HD + 1].rearrange("p h n -> p (h n)")).then_inc(s_rc, 1)
                        dve.wait_ge(s_rc, t + 1)
                        dve.tensor_tensor(cx[:, c % 2, i, :].rearrange("p (h d) -> p h d", d=HD), o[:, :, 0:HD],
                                          rc[:, t % 2, :].unsqueeze(2).to_broadcast([P, H, HD]), ALU.mult).then_inc(s_cx, 1)

                for c in range(B):
                    context(c)
                    if c >= 1:
                        tail.dve_sum(dve, c - 1)
                        tail.dve_norm(dve, c - 1)
                tail.dve_sum(dve, B - 1)
                tail.dve_norm(dve, B - 1)


def l1_tree(nc, env):
    w, PS = env.w, env.PS
    M = D
    NG = M - 1
    DEPTH = 8
    tiles = lambda c: list(range(c * TB, (c + 1) * TB))
    with ExitStack() as c_:
        sb, sem = env.alloc(c_)
        tail = Tail(env, c_, "t5", (2, 4, 6), tiles, KD)
        wr = sb("wr", [P, KD, M], F32)
        lw = sb("lw", [P, KD, D], F32)
        gx = sb("gx", [P, TB, M], F32)
        g1 = sb("g1", [P, TB, M], F32)
        gt = sb("gt", [P, TB, M], F32)
        om = sb("om", [P, TB, M], F32)
        lp = sb("lp", [P, 2, TB, M], F32)
        leaf = sb("leaf", [P, 2, TB, M], F32)
        s_wps = sem("d_wps")
        s_w = sem("d_w")
        s_gps = sem("d_gps")
        s_gx = sem("d_gx")
        s_dve = sem("d_dve")
        s_leaf = sem("d_leaf")
        s_out = sem("d_out")

        with nc.Block() as block:

            @block.tensor
            def _(pe):
                for n, (a, b_, width) in enumerate((("d_wq", "d_rT", NG), ("d_lvT", "d_woT", D))):
                    for m in range(KD):
                        for k in range(KD):
                            last = pe.matmul(PS[:, n * BANK + m * M:n * BANK + m * M + width], w[a][:, k, m * P:(m + 1) * P],
                                             w[b_][:, k, 0:width], start=(k == 0), stop=(k == KD - 1))
                    last.then_inc(s_wps, 1)
                pe.wait_ge(s_w, 2)

                def gates(c):
                    if c >= 1:
                        pe.wait_ge(s_gx, c)
                    for i in range(TB):
                        t = c * TB + i
                        for k in range(KD):
                            last = pe.matmul(PS[:, i * M:i * M + NG], env.xT[:, k, t * P:(t + 1) * P], wr[:, k, 0:NG],
                                             start=(k == 0), stop=(k == KD - 1))
                    last.then_inc(s_gps, 1)

                gates(0)
                for c in range(B):
                    if c + 1 < B:
                        gates(c + 1)
                    tail.pe_in(pe, c, lambda i: leaf[:, c % 2, i, :], lambda i: pe.wait_ge(s_leaf, c + 1))
                    tail.pe_proj(pe, c, lambda k: lw[:, k, :])

            @block.scalar
            def _(act):
                act.wait_ge(s_wps, 1)
                act.activation(wr[:, :, 0:NG], PS[:, 0:KD * M].rearrange("p (k n) -> p k n", k=KD)[:, :, 0:NG],
                               ACT.Copy).then_inc(s_w, 1)
                act.wait_ge(s_wps, 2)
                act.activation(lw[:, :, :], PS[:, BANK:BANK + KD * D].rearrange("p (k n) -> p k n", k=KD),
                               ACT.Copy).then_inc(s_w, 1)

                def gates(c):
                    act.wait_ge(s_gps, c + 1)
                    if c >= 1:
                        act.wait_ge(s_leaf, c)
                    act.activation(gx[:, :, 0:NG], PS[:, 0:TB * M].rearrange("p (t n) -> p t n", t=TB)[:, :, 0:NG],
                                   ACT.Exp, scale=-1.0).then_inc(s_gx, 1)

                gates(0)
                for c in range(B):
                    if c + 1 < B:
                        gates(c + 1)
                    tail.act_in(act, c)

            @block.gpsimd
            def _(pool):
                for c in range(B):
                    tail.pool_residual(pool, c, lambda t: w["d_bout"])
                for c in range(B):
                    tail.pool_rstd(pool, c)

            @block.vector
            def _(dve):
                steps = [0]

                def link(ins):
                    steps[0] += 1
                    ins.then_inc(s_dve, 1)
                    dve.wait_ge(s_dve, steps[0])

                def leaves(c):
                    dve.wait_ge(s_gx, c + 1)
                    if c >= 2:
                        dve.wait_ge(tail.s_cT_ps, c - 1)
                    link(dve.tensor_scalar(g1[:, :, 0:NG], gx[:, :, 0:NG], 1.0, None, ALU.add))
                    link(dve.reciprocal(gt[:, :, 0:NG], g1[:, :, 0:NG]))
                    link(dve.tensor_scalar(om[:, :, 0:NG], gt[:, :, 0:NG], -1.0, 1.0, ALU.mult, ALU.add))
                    for level in range(DEPTH):
                        n = 1 << level
                        dst = leaf[:, c % 2, :, :] if level == DEPTH - 1 else lp[:, level % 2, :, 0:2 * n]
                        dst = dst.rearrange("p t (n e) -> p t n e", e=2)
                        for e, g in enumerate((om, gt)):
                            gg = g[:, :, n - 1:2 * n - 1]
                            if level == 0:
                                last = dve.tensor_copy(dst[:, :, :, e], gg)
                            else:
                                last = dve.tensor_tensor(dst[:, :, :, e], lp[:, (level - 1) % 2, :, 0:n], gg, ALU.mult)
                        if level < DEPTH - 1:
                            link(last)
                    last.then_inc(s_leaf, 1)

                for c in range(B):
                    leaves(c)
                    if c >= 1:
                        tail.dve_sum(dve, c - 1)
                        tail.dve_norm(dve, c - 1)
                tail.dve_sum(dve, B - 1)
                tail.dve_norm(dve, B - 1)

            @block.sync
            def _(sp):
                for c in range(B):
                    sp.wait_ge(tail.s_xn, c + 1)
                    sp.dma_start(env.d["out"][c * L:(c + 1) * L, :].rearrange("(t p) n -> p t n", p=P),
                                 env.x[:, c * TB:(c + 1) * TB, :]).then_inc(s_out, 16)
                sp.wait_ge(s_out, 16 * B)


CF = 5 * P + 2 * E + ETILES + 3 * L

MATS = {
    "a0_in": (D, 3 * D, 0), "a0_out": (D, D, 0), "c0_wq": (D, D, 0), "c0_wkT": (D, CD, 0), "c0_wv": (CD, D, 0),
    "f_router": (D, E, 0), "f_wg": (D, F, 0), "f_wu": (D, F, 0), "f_wd": (F, D, 0),
    "s_wq": (D, D, 1), "s_wk": (D, D, 1), "s_wv": (D, D, 1), "s_wo": (D, D, 1),
    "x_wq": (D, D, 1), "x_wk": (CD, D, 1), "x_wv": (CD, D, 1), "x_wo": (D, D, 1),
    "d_wq": (D, D, 1), "d_rT": (D, D - 1, 1), "d_lvT": (D, D, 1), "d_woT": (D, D, 1),
}
ROWS = {"a0_bout": 0, "c0_bv": 0, "s_bv": 1, "s_bo": 1, "x_bv": 1, "x_bo": 1, "d_bout": 1}
COLS = {"c0_bq": 0, "c0_bk": 0, "s_bq": 1, "s_bk": 1, "x_bq": 1, "x_bk": 1}


def build(nc, d):
    env = Env()
    env.d = d
    with ExitStack() as ctx:
        layer_sems = []

        def alloc(c):
            def sb(name, shape, dt):
                return c.enter_context(nc.sbuf_tensor(name, shape, dt))

            def sem(name, keep=False):
                handle = nc.alloc_semaphore(name)
                if not keep:
                    layer_sems.append(handle)
                return handle

            return sb, sem

        env.alloc = alloc
        sb, sem = alloc(ctx)
        scratch = lambda name, shape, dt: nc.dram_tensor(name, shape, dt, kind="Internal").ap()
        env.kx = scratch("kx", (B * D, 3, CTX), BF16)
        env.qx = scratch("qx", (B * H * QK_ROWS, L), BF16)
        env.vx = scratch("vx", (GROUPS, CTX, G * VW), F32)
        env.ks = scratch("ks", (B * H * QK_ROWS, L), BF16)
        env.qs = scratch("qs", (B * H * QK_ROWS, L), BF16)
        env.vs = scratch("vs", (GROUPS, L, G * VW), F32)
        env.xg = scratch("xg", (ETILES * P, D), F32)
        env.yg = scratch("yg", (ETILES * P, D), F32)
        env.xg_t = env.xg.rearrange("(j p) n -> j p n", p=P)
        env.yg_t = env.yg.rearrange("(j p) n -> j p n", p=P)
        env.gu_t, env.dn_t = d["f_gu"], d["f_dn"]

        psum = ctx.enter_context(nc.psum_tensor("psum", [P, 8 * BANK], F32))
        env.PS = psum[:, :]
        env.x = sb("x_sb", [P, T, D], F32)
        env.xT = sb("xT_sb", [P, KD, N], F32)
        env.cf = sb("cf_sb", [P, CF], F32)
        env.cb = sb("cb_sb", [P, 3 * P], BF16)
        mh = sb("mhalf", [P, TB], F32)
        env.mhalf = mh[:, :]
        at = 0
        parts = []
        for n in (P, P, P, P, P, E, E, ETILES, L, L, L):
            parts.append(env.cf[:, at:at + n])
            at += n
        env.ident, _, _, env.tri, env.ones, env.iota16, env.thr16, env.iota32, env.cos, env.sin, env.sin_neg = parts
        env.identb, env.mask_q, env.mask_k = (env.cb[:, i * P:(i + 1) * P] for i in range(3))

        env.w, env.loads = {}, []

        def weights(layer, c):
            sbw, _ = alloc(c)
            for name, (k, n, l) in MATS.items():
                if l == layer:
                    if k == P:
                        t = sbw(name + "_sb", [P, n], F32)
                        env.w[name] = t[:, :]
                        env.loads.append((t[:, :], d[name]))
                    else:
                        t = sbw(name + "_sb", [P, k // P, n], F32)
                        env.w[name] = t
                        env.loads.append((t[:, :, :], d[name].rearrange("(k p) n -> p k n", p=P)))
            for name, l in ROWS.items():
                if l == layer:
                    t = sbw(name + "_sb", [P, D], F32)
                    env.w[name] = t[:, :]
                    env.loads.append((t[:, :], d[name].partition_broadcast(P)))
            for name, l in COLS.items():
                if l == layer:
                    t = sbw(name + "_sb", [P, KD], F32)
                    env.w[name] = t[:, :]
                    env.loads.append((t[:, :], d[name]))
            if layer == 0:
                t = sbw("a0_bin_sb", [1, 3 * D], F32)
                env.w["a0_bin"] = t[:, :]
                env.loads.append((t[:, :], d["a0_bin"]))

        weights(1, ctx)
        with ExitStack() as c0:
            weights(0, c0)
            with ExitStack() as c1:
                sbc, _ = alloc(c1)
                ctx_sb = sbc("ctx_sb", [P, B, CT, CD], F32)
                ctxT_sb = sbc("ctxT_sb", [CD, B * CTX], F32)
                env.ctx, env.ctxT = ctx_sb, ctxT_sb
                ctx_prep(nc, env)
                l0_attn(nc, env)
                l0_xattn(nc, env)
            l0_ffn(nc, env)
        with nc.Block() as block:

            @block.sync
            def _(sp):
                for handle in layer_sems:
                    sp.sem_clear(handle)

        for handle in layer_sems:
            nc.release_semaphore(handle)
        layer_sems.clear()
        stacks = lambda a: lambda g: a.rearrange("(g h r) n -> g r h n", g=GROUPS, r=QK_ROWS)[g]
        kx_part = lambda g, j: env.kx.rearrange("(g h d) j n -> j g d h n", g=GROUPS, d=HD)[j][g]
        with ExitStack() as c1:
            l1_attn_prep(nc, env)
            sbc, _ = alloc(c1)
            OT = sbc("OT", [P, GROUPS, L], F32)
            heads_loop(nc, env, "sa", L, True, stacks(env.qs), stacks(env.ks), env.vs, OT)
            heads_tail(nc, env, "t3", OT, env.w["s_wo"], env.w["s_bo"])
            l1_xattn_prep(nc, env)
            heads_loop(nc, env, "xa", CTX, False, stacks(env.qx), kx_part, env.vx, OT)
            heads_tail(nc, env, "t4", OT, env.w["x_wo"], env.w["x_bo"])
        l1_tree(nc, env)


def constants():
    f = np.zeros((P, CF), np.float32)
    i = np.arange(P)
    at = 0

    def put(a):
        nonlocal at
        f[:, at:at + a.shape[1]] = a
        at += a.shape[1]

    put(np.eye(P, dtype=np.float32))
    hide = np.where(i[:, None] >= i[None, :], 0.0, -1e30).astype(np.float32)
    put(hide)
    put(hide.T)
    put((i[:, None] < i[None, :]).astype(np.float32))
    put(np.ones((P, P), np.float32))
    put(np.tile(np.arange(E, dtype=np.float32), (P, 1)))
    put(np.tile(P * np.arange(E, dtype=np.float32), (P, 1)))
    put(np.tile(np.arange(ETILES, dtype=np.float32), (P, 1)))
    frac = (2 * np.arange(HD // 2) / HD).astype(np.float32)
    scale = np.power(np.float32(2500), frac).astype(np.float32)
    angle = np.arange(L).astype(np.float32)[None, :] / scale[:, None]
    cos, sin = np.cos(angle).astype(np.float32), np.sin(angle).astype(np.float32)
    for table in (cos, sin, -sin):
        put(np.tile(table, (2 * P // HD, 1)))
    return f


def kernel(**inputs):
    import concourse.bacc as bacc
    from concourse.bass_utils import run_bass_kernel_spmd

    a = {k: np.asarray(v) for k, v in inputs.items()}
    c = np.ascontiguousarray
    cols = lambda v: c(v.reshape(KD, P).T)
    halves = np.arange(D).reshape(H, 2, HD // 2).transpose(1, 0, 2).reshape(-1)
    cf = constants()
    arrays = {
        "x": c(a["x"].reshape(N, D)), "ctx": c(a["ctx_512"]), "cf": cf,
        "a0_in": c(a["L0_attn_in_proj_weight"].T), "a0_bin": c(a["L0_attn_in_proj_bias"][None, :]),
        "a0_out": c(a["L0_attn_out_proj_weight"].T), "a0_bout": c(a["L0_attn_out_proj_bias"]),
        "c0_wq": c(a["L0_xattn_Wq"]), "c0_bq": cols(a["L0_xattn_bq"]), "c0_wkT": c(a["L0_xattn_Wk"].T),
        "c0_bk": cols(a["L0_xattn_bk"]), "c0_wv": c(a["L0_xattn_Wv"]), "c0_bv": c(a["L0_xattn_bv"]),
        "f_router": c(a["L0_ffn_w_router"].T), "f_gu": c(a["L0_ffn_gate_up_proj"]), "f_dn": c(a["L0_ffn_down_proj"]),
        "f_wg": c(a["L0_ffn_w_gate"].T), "f_wu": c(a["L0_ffn_w_up"].T), "f_wd": c(a["L0_ffn_w_down"].T),
        "s_wq": c(a["L1_attn_wq_w"][:, halves]), "s_bq": cols(a["L1_attn_wq_b"][halves]),
        "s_wk": c(a["L1_attn_wk_w"][:, halves]), "s_bk": cols(a["L1_attn_wk_b"][halves]), "s_wv": c(a["L1_attn_wv_w"]),
        "s_bv": c(a["L1_attn_wv_b"]), "s_wo": c(a["L1_attn_wo_w"]), "s_bo": c(a["L1_attn_wo_b"]),
        "x_wq": c(a["L1_xattn_Wq"]), "x_bq": cols(a["L1_xattn_bq"]), "x_wk": c(a["L1_xattn_Wk"]),
        "x_bk": cols(a["L1_xattn_bk"]), "x_wv": c(a["L1_xattn_Wv"]), "x_bv": c(a["L1_xattn_bv"]),
        "x_wo": c(a["L1_xattn_Wo"]), "x_bo": c(a["L1_xattn_bo"]),
        "d_wq": c(a["L1_ffn_Wq"]), "d_rT": c(a["L1_ffn_routers"].T), "d_lvT": c(a["L1_ffn_leaf_values"].T),
        "d_woT": c(a["L1_ffn_Wout_w"].T), "d_bout": c(a["L1_ffn_Wout_b"]),
    }
    nc = bacc.Bacc("TRN2", target_bir_lowering=False, num_devices=1)
    d = {}
    for name, arr in arrays.items():
        d[name] = nc.dram_tensor("in_" + name, arr.shape, mybir.dt.from_np(arr.dtype), kind="ExternalInput").ap()
    d["out"] = nc.dram_tensor("out_0", (N, D), F32, kind="ExternalOutput").ap()
    build(nc, d)
    r = run_bass_kernel_spmd(nc, [{"in_" + k: v for k, v in arrays.items()}], core_ids=[0])
    return r.results[0]["out_0"].reshape(B, L, D)
```

```python
from contextlib import ExitStack

import numpy as np

import concourse.bass as bass
from concourse import mybir

F32 = mybir.dt.float32
BF16 = mybir.dt.bfloat16
I32 = mybir.dt.int32
ALU = mybir.AluOpType
ACT = mybir.ActivationFunctionType
AX = mybir.AxisListType.X

P = 128
B, L, D = 4, 512, 256
N = B * L
T = N // P
TB = L // P
KD = D // P
H, HD = 16, 16
CTX, CD = 1601, 128
CT = -(-CTX // P)
E, F = 16, 512
FC = F // P
BANK = 512
EPS = 1e-5
SCALE = HD ** -0.5
G = 4
GROUPS = B * H // G
VW = 32
K_PARTS = (0, 1, 2, 0, 1, 0)
Q_PARTS = (0, 0, 0, 1, 1, 2)
QK_ROWS = HD * len(K_PARTS)
ETILES = (N - E) // P + E


CHUNKS = T // 2
PAIR_TILES = lambda c: [2 * c, 2 * c + 1]


def ctx_rows(kt):
    return min(P, CTX - kt * P)


class Env:
    pass


class Tail:

    def __init__(self, env, c, name, banks, tiles, kc, behind=0, inputs=True):
        self.env, self.tiles, self.kc, self.banks, self.behind = env, tiles, kc, banks, behind
        self.tc = tc = len(tiles(0))
        self.ring = ring = TB // tc
        self.shared = banks[0] == banks[2]
        sb, sem = env.alloc(c)
        self.cT = sb(name + "_cT", [P, ring, KD, tc * P], F32) if inputs else None
        self.r = sb(name + "_r", [P, ring, tc, D], F32)
        self.st = sb(name + "_st", [P, ring, tc, 6], F32)
        self.mv = sb(name + "_mv", [P, ring, tc, 2], F32)
        self.ve = sb(name + "_ve", [P, ring, tc], F32)
        self.rstd = sb(name + "_rstd", [P, ring, tc], F32)
        self.s_cT_ps = sem(name + "_cT_ps")
        self.s_cT = sem(name + "_cT")
        self.s_proj = sem(name + "_proj")
        self.s_xb = sem(name + "_xb")
        self.s_r = sem(name + "_r")
        self.s_st = sem(name + "_st")
        self.s_mv = sem(name + "_mv")
        self.s_ve = sem(name + "_ve")
        self.s_rstd = sem(name + "_rstd")
        self.s_xn = sem(name + "_xn")
        self.s_xT_ps = sem(name + "_xT_ps")
        self.s_xT = sem(name + "_xT")

    def ps(self, which, c):
        width = 2 * BANK // self.ring
        at = self.banks[which] * BANK + c % self.ring * width
        return self.env.PS[:, at:at + width]

    def free(self, engine, sem, c):
        if c >= self.ring:
            engine.wait_ge(sem, c - self.ring + 1)

    def pool_residual(self, pool, c, add):
        x = self.env.x
        for t in self.tiles(c):
            last = pool.tensor_tensor(x[:, t, :], x[:, t, :], add(t), ALU.add)
        last.then_inc(self.s_xb, 1)

    def turn(self, pe, ps, i, src):
        for k in range(KD):
            at = (k * self.tc + i) * P
            last = pe.transpose(ps[:, at:at + P], src[:, k * P:(k + 1) * P], self.env.ident)
        return last

    def pe_in(self, pe, c, nat, ready):
        self.free(pe, self.s_cT, c)
        if self.shared and c > self.behind:
            pe.wait_ge(self.s_xT, c - self.behind)
        for i in range(self.tc):
            ready(i)
            last = self.turn(pe, self.ps(0, c), i, nat(i))
        last.then_inc(self.s_cT_ps, 1)

    def act_in(self, act, c):
        act.wait_ge(self.s_cT_ps, c + 1)
        self.free(act, self.s_proj, c)
        act.activation(self.cT[:, c % self.ring, :, :].rearrange("p k n -> p (k n)"), self.ps(0, c),
                       ACT.Copy).then_inc(self.s_cT, 1)

    def pe_proj(self, pe, c, w, lhs=None):
        if lhs is None:
            pe.wait_ge(self.s_cT, c + 1)
            lhs = lambda i, k: self.cT[:, c % self.ring, k, i * P:(i + 1) * P]
        self.free(pe, self.s_r, c)
        for i in range(self.tc):
            for k in range(self.kc):
                last = pe.matmul(self.ps(1, c)[:, i * D:(i + 1) * D], lhs(i, k), w(k),
                                 start=(k == 0), stop=(k == self.kc - 1))
        last.then_inc(self.s_proj, 1)

    def x_chunk(self, c):
        ts = self.tiles(c)
        return self.env.x[:, ts[0]:ts[-1] + 1:ts[1] - ts[0], :]

    def dve_sum(self, dve, c, biased=True):
        dve.wait_ge(self.s_proj, c + 1)
        if biased:
            dve.wait_ge(self.s_xb, c + 1)
        self.free(dve, self.s_xn, c)
        dve.tensor_tensor(self.r[:, c % self.ring, :, :], self.ps(1, c).rearrange("p (t n) -> p t n", t=self.tc),
                          self.x_chunk(c), ALU.add).then_inc(self.s_r, 1)

    def dve_stats(self, dve, c, ready=None):
        u = c % self.ring
        dve.wait_ge(ready or self.s_r, c + 1)
        for i in range(self.tc):
            dve.bn_stats(self.st[:, u, i, :], self.r[:, u, i, :]).then_inc(self.s_st, 1)
        dve.wait_ge(self.s_st, self.tc * (c + 1))
        for i in range(self.tc):
            last = dve.bn_aggr(self.mv[:, u, i, :], self.st[:, u, i, :])
        last.then_inc(self.s_mv, 1)
        dve.wait_ge(self.s_mv, c + 1)
        dve.tensor_scalar(self.ve[:, u, :], self.mv[:, u, :, 1], EPS, None, ALU.add).then_inc(self.s_ve, 1)

    def pool_rstd(self, pool, c):
        u = c % self.ring
        pool.wait_ge(self.s_ve, c + 1)
        pool.tensor_tensor(self.rstd[:, u, :], self.ve[:, u, :], self.env.mhalf[:, 0:self.tc], ALU.pow).then_inc(self.s_rstd, 1)

    def dve_apply(self, dve, c):
        u = c % self.ring
        dve.wait_ge(self.s_rstd, c + 1)
        for i, t in enumerate(self.tiles(c)):
            last = dve.tensor_scalar(self.env.x[:, t, :], self.r[:, u, i, :], self.mv[:, u, i, 0:1],
                                     self.rstd[:, u, i:i + 1], ALU.subtract, ALU.mult)
        last.then_inc(self.s_xn, 1)

    def dve_norm(self, dve, c):
        self.dve_stats(dve, c)
        self.dve_apply(dve, c)

    def pe_out(self, pe, c):
        pe.wait_ge(self.s_xn, c + 1)
        self.free(pe, self.s_xT, c)
        for i, t in enumerate(self.tiles(c)):
            last = self.turn(pe, self.ps(2, c), i, self.env.x[:, t, :])
        last.then_inc(self.s_xT_ps, 1)

    def act_out(self, act, c):
        act.wait_ge(self.s_xT_ps, c + 1)
        ts = self.tiles(c)
        xT = self.env.xT[:, :, :].rearrange("p k (t n) -> p k t n", n=P)[:, :, ts[0]:ts[-1] + 1:ts[1] - ts[0], :]
        width = self.tc * P
        for k in range(KD):
            last = act.activation(xT[:, k], self.ps(2, c)[:, k * width:(k + 1) * width].rearrange("p (t n) -> p t n", n=P),
                                  ACT.Copy)
        last.then_inc(self.s_xT, 1)


def slot_runs(slots):
    runs = []
    for i, j in enumerate(slots):
        if runs:
            s0, n, j0, same = runs[-1]
            if j == j0 and (same or n == 1) or j == j0 + n and not same:
                runs[-1] = (s0, n + 1, j0, j == j0)
                continue
        runs.append((i, 1, j, False))
    return runs


class Split:

    def __init__(self, env, c, name, width, bias, dst, slots, ring, rope=None, width_of=None):
        self.env, self.width, self.bias, self.dst, self.rope, self.ring = env, width, bias, dst, rope, ring
        self.width_of = width_of or (lambda n: width)
        self.slots, self.per = slots, len(slot_runs(slots(0)))
        sb, sem = env.alloc(c)
        self.rest = sb(name + "_rest", [P, ring, width], F32)
        if rope:
            self.ta = sb(name + "_ta", [P, 2, width], F32)
            self.tb = sb(name + "_tb", [P, 2, width], F32)
            self.whole = sb(name + "_whole", [P, ring, width], F32)
        self.parts = sb(name + "_parts", [P, ring, 3, width], BF16)
        self.s_full = sem(name + "_full")
        self.s_rot = sem(name + "_rot")
        self.s_whole = sem(name + "_whole")
        self.s_hi = sem(name + "_hi")
        self.s_rest = sem(name + "_rest")
        self.s_mid = sem(name + "_mid")
        self.s_lo = sem(name + "_lo")
        self.s_out = [sem(f"{name}_out{u}") for u in range(ring)]

    def freed(self, pe, n):
        pe.wait_ge(self.s_rot if self.rope else self.s_rest, n + 1)

    def act_hi(self, act, n, ps):
        u = n % self.ring
        if n >= self.ring:
            act.wait_ge(self.s_out[u], 16 * self.per * (n // self.ring))
        if self.rope:
            act.wait_ge(self.s_whole, n + 1)
            act.activation(self.parts[:, u, 0, 0:self.width_of(n)], self.whole[:, u, :], ACT.Copy).then_inc(self.s_hi, 1)
        else:
            act.wait_ge(self.s_full, n + 1)
            act.activation(self.parts[:, u, 0, 0:self.width_of(n)], ps, ACT.Identity, bias=self.bias(n)).then_inc(self.s_hi, 1)

    def act_mid(self, act, n):
        act.wait_ge(self.s_rest, n + 1)
        act.activation(self.parts[:, n % self.ring, 1, 0:self.width_of(n)], self.rest[:, n % self.ring, 0:self.width_of(n)], ACT.Copy).then_inc(self.s_mid, 1)

    def dve_rot(self, dve, n, full, ps_a, ps_b):
        u = n % 2
        ba, bb = self.bias(n)
        dve.wait_ge(self.s_full, full)
        if n >= 2:
            dve.wait_ge(self.s_whole, n - 1)
        dve.scalar_tensor_tensor(self.ta[:, u, :], ps_a, ba, self.rope(n)[0], ALU.add, ALU.mult)
        dve.scalar_tensor_tensor(self.tb[:, u, :], ps_b, bb, self.rope(n)[1], ALU.add, ALU.mult).then_inc(self.s_rot, 1)

    def dve_rest(self, dve, n, ps=None):
        u = n % self.ring
        dve.wait_ge(self.s_hi, n + 1)
        if n >= self.ring:
            dve.wait_ge(self.s_lo, n - self.ring + 1)
        if self.rope:
            dve.tensor_tensor(self.rest[:, u, 0:self.width_of(n)], self.whole[:, u, :], self.parts[:, u, 0, 0:self.width_of(n)],
                              ALU.subtract).then_inc(self.s_rest, 1)
        else:
            dve.scalar_tensor_tensor(self.rest[:, u, 0:self.width_of(n)], ps, self.bias(n), self.parts[:, u, 0, 0:self.width_of(n)],
                                     ALU.add, ALU.subtract).then_inc(self.s_rest, 1)

    def pool_whole(self, pool, n):
        u = n % self.ring
        pool.wait_ge(self.s_rot, n + 1)
        if n >= self.ring:
            pool.wait_ge(self.s_rest, n - self.ring + 1)
        pool.tensor_tensor(self.whole[:, u, :], self.ta[:, n % 2, :], self.tb[:, n % 2, :], ALU.add).then_inc(self.s_whole, 1)

    def pool_lo(self, pool, n):
        u = n % self.ring
        pool.wait_ge(self.s_mid, n + 1)
        pool.tensor_tensor(self.parts[:, u, 2, 0:self.width_of(n)], self.rest[:, u, 0:self.width_of(n)], self.parts[:, u, 1, 0:self.width_of(n)],
                           ALU.subtract).then_inc(self.s_lo, 1)

    def sp_out(self, sp, n):
        sp.wait_ge(self.s_lo, n + 1)
        dst = self.dst(n)
        for s0, slots, j, same in slot_runs(self.slots(n)):
            src = self.parts[:, n % self.ring, j:j + (1 if same else slots), 0:self.width_of(n)]
            if same:
                src = src.to_broadcast([P, slots, self.width_of(n)])
            sp.dma_start(dst[:, s0:s0 + slots, :], src).then_inc(self.s_out[n % self.ring], 16)

    def sp_end(self, sp, blocks):
        for u in range(self.ring):
            sp.wait_ge(self.s_out[u], 16 * self.per * ((blocks - u + self.ring - 1) // self.ring))


class Values:

    def __init__(self, env, c, name, items, bias, dst):
        self.env, self.items, self.bias, self.dst = env, items, bias, dst
        sb, sem = env.alloc(c)
        self.v = sb(name + "_v", [P, 2, 4, H * VW], F32)
        self.s_zero = sem(name + "_zero")
        self.s_ones = sem(name + "_ones")
        self.s_full = sem(name + "_vfull")
        self.s_read = sem(name + "_vread")
        self.s_v = sem(name + "_v")
        self.s_out = [sem(f"{name}_vout{u}") for u in range(2)]
        self.sent = [0, 0]
        self.sent_before = []
        for n, (b, kts, rows) in enumerate(items):
            self.sent_before.append(self.sent[n % 2])
            self.sent[n % 2] += 16 * len(kts)

    def pool_init(self, pool):
        v = self.v[:, :, :, :].rearrange("p u k n -> p (u k n)")
        pool.memset(v, 0.0).then_inc(self.s_zero, 1)
        pool.wait_ge(self.s_zero, 1)
        pool.memset(v.rearrange("p (h w) -> p h w", w=VW)[:, :, HD:HD + 1], 1.0).then_inc(self.s_ones, 1)

    def dve_copy(self, dve, n, ps):
        b, kts, rows = self.items[n]
        k = len(kts)
        if n == 0:
            dve.wait_ge(self.s_ones, 1)
        dve.wait_ge(self.s_full, n + 1)
        if n >= 2:
            dve.wait_ge(self.s_out[n % 2], self.sent_before[n])
        out = self.v[0:rows, n % 2, 0:k, :].rearrange("p k (h w) -> p (k h) w", w=VW)[:, :, 0:HD]
        src = ps[0:rows, 0:k * D].rearrange("p (k n) -> p k n", k=k)
        for i in range(k):
            last = dve.tensor_tensor(out[:, i * H:(i + 1) * H, :], src[:, i, :].rearrange("p (h d) -> p h d", d=HD),
                                     self.bias[0:rows, :].rearrange("p (h d) -> p h d", d=HD), ALU.add)
        last.then_inc(self.s_v, 1)

    def act_copy(self, act, n, ps):
        b, kts, rows = self.items[n]
        k = len(kts)
        if n == 0:
            act.wait_ge(self.s_ones, 1)
        act.wait_ge(self.s_full, n + 1)
        if n >= 2:
            act.wait_ge(self.s_out[n % 2], self.sent_before[n])
        out = self.v[0:rows, n % 2, 0:k, :].rearrange("p k (h w) -> p (k h) w", w=VW)[:, :, 0:HD]
        act.activation(out, ps[0:rows, 0:k * D].rearrange("p (h d) -> p h d", d=HD), ACT.Copy).then_inc(self.s_read, 1)

    def pool_bias(self, pool, n):
        b, kts, rows = self.items[n]
        pool.wait_ge(self.s_read, n + 1)
        for i in range(len(kts)):
            v = self.v[0:rows, n % 2, i, :].rearrange("p (h w) -> p h w", w=VW)[:, :, 0:HD]
            last = pool.tensor_tensor(v, v, self.bias[0:rows, :].rearrange("p (h d) -> p h d", d=HD), ALU.add)
        last.then_inc(self.s_v, 1)

    def sp_out(self, sp, n):
        b, kts, rows = self.items[n]
        sp.wait_ge(self.s_v, n + 1)
        for i, kt in enumerate(kts):
            sp.dma_start(self.dst[b * G:(b + 1) * G, kt * P:kt * P + rows, :].rearrange("g p n -> p g n"),
                         self.v[0:rows, n % 2, i, :].rearrange("p (g n) -> p g n", g=G)).then_inc(self.s_out[n % 2], 16)

    def sp_end(self, sp):
        for u in range(2):
            sp.wait_ge(self.s_out[u], self.sent[u])


def l0_attn(nc, env):
    w, PS = env.w, env.PS
    W3 = 3 * D
    tiles = lambda c: [s * TB + c for s in range(B)]
    PAIRS = 4 * TB
    KH = -(-CTX // 2)
    kcut = lambda p: (p % 2 * KH, min(p % 2 * KH + KH, CTX))
    vitems = [(b, kts, ctx_rows(kts[-1])) for b in range(B) for kts in ((0, 1, 2, 3), (4, 5, 6, 7), (8, 9, 10, 11), (12,))]
    assert PAIRS == len(vitems) == 2 * B * KD
    V_PS = PS[:, 4 * BANK:6 * BANK]
    K_PS = PS[:, 6 * BANK:8 * BANK]
    with ExitStack() as c_:
        sb, sem = env.alloc(c_)
        tail = Tail(env, c_, "t0", (2, 0, 2), tiles, KD)
        keys = Split(env, c_, "xk", KH, lambda p: w["x_bk"][:, p // 2 % KD:p // 2 % KD + 1],
                     lambda p: env.kx[p // 2 * P:(p // 2 + 1) * P, :, kcut(p)[0]:kcut(p)[1]], lambda p: range(3), 2,
                     width_of=lambda p: kcut(p)[1] - kcut(p)[0])
        val = Values(env, c_, "xv", vitems, w["x_bv"], env.vx)
        qkv = sb("qkv", [P, 2, B, W3], F32)
        prod = sb("prod", [P, 2, B, D], F32)
        half = sb("half", [P, 2, D], F32)
        sc = sb("sc", [P, B, B, H], F32)
        mx = sb("mx", [P, B, H], F32)
        ex = sb("ex", [P, B, B, H], F32)
        sm = sb("sm", [P, B, H], F32)
        rs = sb("rs", [P, B, H], F32)
        cx = sb("cx", [P, 2, B, D], F32)
        zt = sb("zt", [P, D], F32)
        ones3 = sb("ones3", [3, P], BF16)
        bparts = sb("bparts", [3, W3], BF16)
        brow = sb("brow", [3, 2, W3], F32)
        bpart = sb("bpart", [3, 2, W3], BF16)
        s_const = sem("ld_const")
        s_xT = [sem(f"ld_xT{c}") for c in range(TB)]
        s_x = sem("ld_x")
        s_c = [sem(f"ld_ctx{b}") for b in range(B)]
        s_w0 = sem("ld_w0")
        s_wa = sem("ld_wa")
        s_wc = sem("ld_wc")
        s_zt = sem("zero_tile")
        s_zd = sem("zero_dram", keep=True)
        s_bp = sem("a0_bparts")
        s_ps = sem("a0_ps")
        s_qkv = sem("a0_qkv")
        s_sh = sem("a0_shift")
        s_ex = sem("a0_exp")
        s_dve = sem("a0_dve")
        s_cx = sem("a0_cx")
        s_used = sem("a0_used")
        ZR = 8

        with nc.Block() as block:

            @block.sync
            def _(sp):
                sp.dma_start(env.cf[:, 0:CF_FIRST], env.d["cf"][:, 0:CF_FIRST]).then_inc(s_const, 16)
                for c in range(TB):
                    for k in range(KD):
                        sp.dma_start(env.xT[:, k, :].rearrange("p (s c n) -> p s c n", s=B, c=TB)[:, :, c, :],
                                     env.d["xT"].rearrange("(k p) (s c n) -> k c p s n", p=P, s=B, c=TB)[k][c]
                                     ).then_inc(s_xT[c], 16)
                for b in range(B):
                    sp.dma_start(env.ctxT[:, b * CTX:(b + 1) * CTX], env.d["ctxT"][:, b * CTX:(b + 1) * CTX]).then_inc(s_c[b], 16)
                    if b == 0:
                        sp.dma_start(env.x[:, :, :], env.d["x"].rearrange("(t p) n -> p t n", p=P)).then_inc(s_x, 16)
                sp.dma_start(env.cf[:, CF_FIRST:CF], env.d["cf"][:, CF_FIRST:CF]).then_inc(s_wc, 16)
                for p in range(PAIRS):
                    keys.sp_out(sp, p)
                    val.sp_out(sp, p)
                keys.sp_end(sp, PAIRS)
                val.sp_end(sp)
                sp.wait_ge(s_wc, 16 * (len(env.loads["c"]) + 1))
                sp.wait_ge(s_zd, 16 * -(-ETILES // ZR))

            @block.tensor
            def _(pe):
                def project(c, s):
                    n = c * B + s
                    if n >= 1:
                        pe.wait_ge(s_qkv, n)
                    if s == 0:
                        pe.wait_ge(s_xT[c], 16 * KD)
                        if c >= 2:
                            pe.wait_ge(tail.s_r, c - 1)
                    t = s * TB + c
                    for e in range(2):
                        o = PS[:, e * BANK:e * BANK + W3 // 2]
                        cols = slice(e * W3 // 2, (e + 1) * W3 // 2)
                        for k in range(KD):
                            pe.matmul(o, env.xT[:, k, t * P:(t + 1) * P], w["a0_in"][:, k, cols],
                                      start=(k == 0), stop=False)
                    if n == 0:
                        pe.wait_ge(s_bp, 1)
                    for e in range(2):
                        last = pe.matmul(PS[:, e * BANK:e * BANK + W3 // 2], ones3[:, :],
                                         bparts[:, e * W3 // 2:(e + 1) * W3 // 2], start=False, stop=True)
                    last.then_inc(s_ps, 1)

                def pair(p):
                    b, m = divmod(p // 2, KD)
                    if p % (2 * KD) == 0:
                        pe.wait_ge(s_c[b], 16)
                    if p >= 1:
                        keys.freed(pe, p - 1)
                    k0, k1 = kcut(p)
                    for q in range(k0, k1, BANK):
                        e = min(q + BANK, k1)
                        last = pe.matmul(K_PS[:, q - k0:e - k0], w["x_wk"][:, m * P:(m + 1) * P],
                                         env.ctxT[:, b * CTX + q:b * CTX + e], start=True, stop=True)
                    last.then_inc(keys.s_full, 1)
                    vb, kts, rows = vitems[p]
                    pe.wait_ge(s_c[vb], 16)
                    if p >= 1:
                        pe.wait_ge(val.s_read, p)
                    for j, kt in enumerate(kts):
                        last = pe.matmul(V_PS[0:rows, j * D:(j + 1) * D],
                                         env.ctxT[:, vb * CTX + kt * P:vb * CTX + kt * P + rows], w["x_wv"],
                                         start=True, stop=True)
                    last.then_inc(val.s_full, 1)

                pe.wait_ge(s_const, 16)
                pe.wait_ge(s_w0, 16 * 2)
                for s in range(B):
                    project(0, s)
                pe.wait_ge(s_wa, 16 * (len(env.loads["a"]) - 2))
                for c in range(TB):
                    ahead = c + 1 < TB
                    if ahead:
                        project(c + 1, 0)
                    pair(4 * c)
                    if ahead:
                        project(c + 1, 1)
                    pair(4 * c + 1)
                    if ahead:
                        project(c + 1, 2)
                    if c >= 1:
                        tail.pe_out(pe, c - 1)
                    pair(4 * c + 2)
                    if ahead:
                        project(c + 1, 3)
                    pair(4 * c + 3)
                    tail.pe_in(pe, c, lambda i: cx[:, c % 2, i, :], lambda i: pe.wait_ge(s_cx, c + 1))
                    pe.wait_ge(s_qkv, B * min(c + 2, TB))
                    tail.pe_proj(pe, c, lambda k: w["a0_out"][:, k, :])
                tail.pe_out(pe, TB - 1)

            @block.scalar
            def _(act):
                for n, (dst, src) in enumerate(env.loads["a"]):
                    act.dma_start(dst, src).then_inc(s_wa if n >= 2 else s_w0, 16)
                for dst, src in env.loads["c"]:
                    act.dma_start(dst, src).then_inc(s_wc, 16)
                act.wait_ge(s_const, 16)
                act.activation(env.cb[:, :], env.cf[:, 0:3 * P], ACT.Copy)

                def read(c, s):
                    act.wait_ge(s_ps, c * B + s + 1)
                    if c >= 2 and s == 0:
                        act.wait_ge(s_used, c - 1)
                    act.activation(qkv[:, c % 2, s, :].rearrange("p (e n) -> p e n", e=2),
                                   PS[:, 0:2 * BANK].rearrange("p (e n) -> p e n", e=2)[:, :, 0:W3 // 2],
                                   ACT.Copy).then_inc(s_qkv, 1)

                def pair(p):
                    if p == 0:
                        act.wait_ge(s_wa, 16 * (len(env.loads["a"]) - 2))
                    keys.act_hi(act, p, K_PS[:, 0:kcut(p)[1] - kcut(p)[0]])
                    val.act_copy(act, p, V_PS)
                    keys.act_mid(act, p)

                for s in range(B):
                    read(0, s)
                for c in range(TB):
                    ahead = c + 1 < TB
                    if ahead:
                        read(c + 1, 0)
                    pair(4 * c)
                    if ahead:
                        read(c + 1, 1)
                    act.wait_ge(s_sh, c + 1)
                    act.activation(ex[:, :, :, :].rearrange("p a b h -> p (a b h)"),
                                   sc[:, :, :, :].rearrange("p a b h -> p (a b h)"), ACT.Exp,
                                   scale=SCALE).then_inc(s_ex, 1)
                    pair(4 * c + 1)
                    if ahead:
                        read(c + 1, 2)
                    if c >= 1:
                        tail.act_out(act, c - 1)
                    pair(4 * c + 2)
                    if ahead:
                        read(c + 1, 3)
                    pair(4 * c + 3)
                    tail.act_in(act, c)
                tail.act_out(act, TB - 1)

            @block.gpsimd
            def _(pool):
                pool.memset(zt[:, :], 0.0).then_inc(s_zt, 1)
                pool.memset(env.mhalf, -0.5)
                val.pool_init(pool)
                pool.wait_ge(s_zt, 1)
                for i in range(0, ETILES, ZR):
                    n = min(ZR, ETILES - i)
                    pool.dma_start(env.xg[i * P:(i + n) * P, :].rearrange("(a p) n -> p a n", p=P),
                                   zt[:, :].unsqueeze(1).to_broadcast([P, n, D])).then_inc(s_zd, 16)
                pool.wait_ge(s_wa, 16 * (len(env.loads["a"]) - 2))
                pool.wait_ge(s_x, 16)

                def pair(p):
                    keys.pool_lo(pool, p)
                    val.pool_bias(pool, p)

                for c in range(TB):
                    tail.pool_residual(pool, c, lambda t: w["a0_bout"])
                    pair(4 * c)
                    if c >= 1:
                        tail.pool_rstd(pool, c - 1)
                    for j in range(1, 4):
                        pair(4 * c + j)
                tail.pool_rstd(pool, TB - 1)

            @block.vector
            def _(dve):
                steps = [0]

                def link(ins):
                    steps[0] += 1
                    ins.then_inc(s_dve, 1)
                    dve.wait_ge(s_dve, steps[0])

                def pair(p):
                    keys.dve_rest(dve, p, K_PS[:, 0:kcut(p)[1] - kcut(p)[0]])

                def attend(c):
                    v5 = qkv[:, c % 2, :, :].rearrange("p s (h n) -> p s h n", n=3 * HD)
                    dve.wait_ge(s_qkv, B * (c + 1))
                    for s in range(B):
                        pr = prod[:, s % 2, :, :].rearrange("p t (h d) -> p t h d", d=HD)
                        link(dve.tensor_tensor(pr, v5[:, s, :, 0:HD].unsqueeze(1).to_broadcast([P, B, H, HD]),
                                               v5[:, :, :, HD:2 * HD], ALU.mult))
                        last = dve.tensor_reduce(sc[:, s, :, :].rearrange("p t h -> p (t h)"),
                                                 prod[:, s % 2, :, :].rearrange("p t (h d) -> p (t h) d", d=HD), AX, ALU.add)
                        if s == 1:
                            pair(4 * c)
                    link(last)
                    link(dve.tensor_reduce(mx[:, :, :], sc[:, :, :, :].rearrange("p s t h -> p s h t"), AX, ALU.max))
                    dve.tensor_tensor(sc[:, :, :, :], sc[:, :, :, :],
                                      mx[:, :, :].unsqueeze(2).to_broadcast([P, B, B, H]),
                                      ALU.subtract).then_inc(s_sh, 1)
                    if c >= 1:
                        tail.dve_norm(dve, c - 1)
                    dve.wait_ge(s_ex, c + 1)
                    link(dve.tensor_reduce(sm[:, :, :], ex[:, :, :, :].rearrange("p s t h -> p s h t"), AX, ALU.add))
                    link(dve.reciprocal(rs[:, :, :], sm[:, :, :]))
                    link(dve.tensor_tensor(ex[:, :, :, :], ex[:, :, :, :],
                                           rs[:, :, :].unsqueeze(2).to_broadcast([P, B, B, H]), ALU.mult))
                    if c >= 2:
                        dve.wait_ge(tail.s_cT_ps, c - 1)
                    pair(4 * c + 1)
                    for s in range(B):
                        pr = prod[:, s % 2, :, :].rearrange("p t (h d) -> p t h d", d=HD)
                        m = dve.tensor_tensor(pr, ex[:, s, :, :].unsqueeze(3).to_broadcast([P, B, H, HD]),
                                              v5[:, :, :, 2 * HD:3 * HD], ALU.mult)
                        if s == B - 1:
                            m.then_inc(s_used, 1)
                            dve.wait_ge(s_used, c + 1)
                        else:
                            link(m)
                        link(dve.tensor_tensor(half[:, :, :], prod[:, s % 2, 0:2, :], prod[:, s % 2, 2:4, :], ALU.add))
                        last = dve.tensor_tensor(cx[:, c % 2, s, :], half[:, 0, :], half[:, 1, :], ALU.add)
                        if s == 2:
                            pair(4 * c + 2)
                    last.then_inc(s_cx, 1)
                    pair(4 * c + 3)
                    tail.dve_sum(dve, c)

                b3 = w["a0_bin"]
                dve.wait_ge(s_w0, 16 * 2)
                dve.wait_ge(s_const, 16)
                dve.memset(ones3[:, :], 1.0)
                link(dve.tensor_copy(bpart[:, 0, :], b3))
                link(dve.tensor_tensor(brow[:, 0, :], b3, bpart[:, 0, :], ALU.subtract))
                link(dve.tensor_copy(bpart[:, 1, :], brow[:, 0, :]))
                link(dve.tensor_tensor(brow[:, 1, :], brow[:, 0, :], bpart[:, 1, :], ALU.subtract))
                link(dve.tensor_scalar(brow[:, 0, :], bpart[:, 0, :], env.ident[0:3, 0:1], None, ALU.mult))
                link(dve.scalar_tensor_tensor(brow[:, 0, :], bpart[:, 1, :], env.ident[0:3, 1:2], brow[:, 0, :], ALU.mult, ALU.add))
                dve.scalar_tensor_tensor(bparts[:, :], brow[:, 1, :], env.ident[0:3, 2:3], brow[:, 0, :],
                                         ALU.mult, ALU.add).then_inc(s_bp, 1)
                for c in range(TB):
                    attend(c)
                tail.dve_norm(dve, TB - 1)


def l0_xattn(nc, env):
    w, PS = env.w, env.PS
    S_PS = PS[:, 0:4 * BANK]
    P_PS = PS[:, 4 * BANK:6 * BANK]
    M_PS = PS[:, 6 * BANK:7 * BANK]
    O_PS = PS[:, 7 * BANK:8 * BANK]
    env.logits = M_PS[:, P:P + T * E]
    NQ = B * KD
    with ExitStack() as c_:
        sb, sem = env.alloc(c_)
        ctx_sb = sb("ctx_sb", [P, B, CT, CD], F32)
        qT = sb("qT", [P, KD, N], F32)
        qk = sb("qk", [P, N], F32)
        pr = sb("pr", [P, 2, CTX], F32)
        pT = sb("pT", [P, 2, CT, P], F32)
        zT = sb("zT", [P, 2, P], F32)
        mxs = sb("mxs", [P, T], F32)
        cq = sb("cq", [P, T], F32)
        top = sb("top", [P, T], F32)
        nb = sb("nb", [P, T], F32)
        rsum = sb("rsum", [P, T], F32)
        rinv = sb("rinv", [P, T], F32)
        r = sb("r0", [P, 2, D], F32)
        st = sb("st0", [P, 6], F32)
        mv = sb("mv0", [P, 2], F32)
        ve = sb("ve0", [P, 1], F32)
        rstd = sb("rstd0", [P, 1], F32)
        s_c = [sem(f"c0_ctx{b}") for b in range(B)]
        s_qps = sem("c0_qps")
        s_q = sem("c0_q")
        s_fps = sem("c0_fps")
        s_f = sem("c0_f")
        s_cps = sem("c0_cps")
        s_cq = sem("c0_cq")
        s_sps = sem("c0_sps")
        s_mx = sem("c0_mx")
        s_nb = sem("c0_nb")
        s_pr = sem("c0_pr")
        s_pps = sem("c0_pps")
        s_pTa = sem("c0_pTa")
        s_pTd = sem("c0_pTd")
        s_zps = sem("c0_zps")
        s_z = sem("c0_z")
        s_ops = sem("c0_ops")
        s_xb = sem("c0_xb")
        s_dve = sem("c0_dve")
        s_r = sem("c0_r")
        s_ve = sem("c0_ve")
        s_rstd = sem("c0_rstd")
        s_xn = sem("c0_xn")
        s_xps = sem("c0_xps")
        s_xT = sem("c0_xT")
        ROUNDS = ((0, 8), (8, CT))
        SPLIT = BANK // P
        bank = lambda n: PS[:, n * BANK:(n + 1) * BANK]

        with nc.Block() as block:

            @block.sync
            def _(sp):
                full = (CT - 1) * P
                for b in range(B):
                    sp.dma_start(ctx_sb[:, b, 0:CT - 1, :],
                                 env.d["ctx"][b, 0:full, :].rearrange("(k p) n -> p k n", p=P)).then_inc(s_c[b], 16)
                    sp.dma_start(ctx_sb[0:ctx_rows(CT - 1), b, CT - 1, :], env.d["ctx"][b, full:CTX, :]).then_inc(s_c[b], 16)

            @block.tensor
            def _(pe):
                def half(n):
                    b, m = divmod(n, KD)
                    if n >= 4:
                        pe.wait_ge(s_q, n - 3)
                    for k in range(KD):
                        last = pe.matmul(bank(n % 4), w["c0_wq"][:, k, m * P:(m + 1) * P], env.xT[:, k, b * L:(b + 1) * L],
                                         start=(k == 0), stop=(k == KD - 1))
                    last.then_inc(s_qps, 1)

                def fold(b):
                    pe.wait_ge(s_q, KD * (b + 1))
                    if b >= 2:
                        pe.wait_ge(s_f, b - 1)
                    for m in range(KD):
                        last = pe.matmul(bank(4 + b % 2), w["c0_wkT"][:, m, :], qT[:, m, b * L:(b + 1) * L],
                                         start=(m == 0), stop=(m == KD - 1))
                    last.then_inc(s_fps, 1)

                def scores(t):
                    b = t // TB
                    pe.wait_ge(s_pr, t) if t >= 1 else pe.wait_ge(s_q, NQ)
                    if t % TB == 0:
                        pe.wait_ge(s_f, b + 1)
                    for q in range(0, CTX, BANK):
                        e = min(q + BANK, CTX)
                        last = pe.matmul(S_PS[:, q:e], qk[:, t * P:(t + 1) * P],
                                         env.ctxT[:, b * CTX + q:b * CTX + e], start=True, stop=True)
                    last.then_inc(s_sps, 1)

                def turn(t, n):
                    k0, k1 = ROUNDS[n]
                    if n == 0:
                        pe.wait_ge(s_pr, t + 1)
                        if t == 0:
                            pe.wait_ge(s_f, B)
                    else:
                        pe.wait_ge(s_pTd, t + 1)
                    if 2 * t + n >= 1:
                        pe.wait_ge(s_pTa, 2 * t + n)
                    for kt in range(k0, k1):
                        rows = ctx_rows(kt)
                        last = pe.transpose(P_PS[0:rows, (kt - k0) * P:(kt - k0 + 1) * P],
                                            pr[:, t % 2, kt * P:kt * P + rows], env.ident)
                    last.then_inc(s_pps, 1)

                def values(t):
                    b = t // TB
                    if t >= 1:
                        pe.wait_ge(s_z, t)
                    if t >= 3:
                        logits(t - 3)
                    if t % TB == 0:
                        pe.wait_ge(s_c[b], 32)
                    for n, (k0, k1) in enumerate(ROUNDS):
                        pe.wait_ge(s_pTa, 2 * t + n + 1)
                        for kt in range(k0, k1):
                            rows = ctx_rows(kt)
                            last = pe.matmul(M_PS[:, 0:P], ctx_sb[0:rows, b, kt, :], pT[0:rows, t % 2, kt, :],
                                             start=(kt == 0), stop=(kt == CT - 1))
                    last.then_inc(s_zps, 1)

                def logits(t):
                    pe.wait_ge(s_xT, t + 1)
                    for k in range(KD):
                        pe.matmul(env.logits[:, t * E:(t + 1) * E], env.xT[:, k, t * P:(t + 1) * P], w["f_router"][:, k, :],
                                  start=(k == 0), stop=(k == KD - 1))

                def project(t):
                    pe.wait_ge(s_z, t + 1)
                    if t >= 1:
                        pe.wait_ge(s_xT, t)
                    else:
                        pe.wait_ge(s_cq, 1)
                    pe.matmul(O_PS[:, 0:D], zT[:, t % 2, :], w["c0_wv"], start=True, stop=True).then_inc(s_ops, 1)

                def back(t):
                    pe.wait_ge(s_xn, t + 1)
                    for k in range(KD):
                        last = pe.transpose(O_PS[:, D + k * P:D + (k + 1) * P], env.x[:, t, k * P:(k + 1) * P], env.ident)
                    last.then_inc(s_xps, 1)

                for n in range(NQ):
                    half(n)
                    if n % KD and n >= 3:
                        fold(n // KD - 1)
                fold(B - 1)
                for t in range(T):
                    for m in range(KD):
                        last = pe.matmul(O_PS[:, t:t + 1], qT[:, m, t * P:(t + 1) * P], w["c0_bk"][:, m:m + 1],
                                         start=(m == 0), stop=(m == KD - 1))
                last.then_inc(s_cps, 1)
                for t in range(T + 3):
                    if 1 <= t <= T:
                        turn(t - 1, 0)
                    if t >= 3:
                        back(t - 3)
                    if t < T:
                        scores(t)
                    if 2 <= t <= T + 1:
                        project(t - 2)
                    if 1 <= t <= T:
                        turn(t - 1, 1)
                        values(t - 1)
                pe.wait_ge(s_z, T)
                for t in range(T - 3, T):
                    logits(t)

            @block.scalar
            def _(act):
                for n in range(NQ):
                    b, m = divmod(n, KD)
                    act.wait_ge(s_qps, n + 1)
                    act.activation(qT[:, m, b * L:(b + 1) * L], bank(n % 4), ACT.Identity,
                                   bias=w["c0_bq"][:, m:m + 1]).then_inc(s_q, 1)

                def turned(t, n):
                    act.wait_ge(s_pps, 2 * t + n + 1)
                    if t >= 2 and n == 0:
                        act.wait_ge(s_zps, t - 1)
                    k0, k1 = ROUNDS[n]
                    last = act.activation(pT[:, t % 2, k0:k0 + SPLIT, :].rearrange("p k n -> p (k n)"),
                                          P_PS[:, 0:BANK], ACT.Copy)
                    if n == 1:
                        rows = ctx_rows(CT - 1)
                        last = act.activation(pT[0:rows, t % 2, CT - 1, :], P_PS[0:rows, BANK:BANK + P], ACT.Copy)
                    last.then_inc(s_pTa, 1)

                for t in range(T + 3):
                    if 1 <= t <= T:
                        turned(t - 1, 0)
                    if t >= 3:
                        act.wait_ge(s_xps, t - 2)
                        act.activation(env.xT[:, :, (t - 3) * P:(t - 2) * P],
                                       O_PS[:, D:2 * D].rearrange("p (k n) -> p k n", k=KD), ACT.Copy).then_inc(s_xT, 1)
                    if 1 <= t <= T:
                        turned(t - 1, 1)
                    if t < T:
                        act.wait_ge(s_nb, t + 1)
                        act.activation(pr[:, t % 2, :], S_PS[:, 0:CTX], ACT.Exp, bias=nb[:, t:t + 1],
                                       accum_out=rsum[:, t:t + 1]).then_inc(s_pr, 1)
                    if 1 <= t <= T:
                        act.wait_ge(s_zps, t)
                        act.activation(zT[:, (t - 1) % 2, :], M_PS[:, 0:P], ACT.Copy).then_inc(s_z, 1)

            @block.gpsimd
            def _(pool):
                for t in range(T):
                    last = pool.tensor_tensor(env.x[:, t, :], env.x[:, t, :], w["c0_bv"], ALU.add)
                last.then_inc(s_xb, 1)
                for t in range(T):
                    pool.wait_ge(s_ve, t + 1)
                    pool.tensor_tensor(rstd[:, :], ve[:, :], env.mhalf[:, 0:1], ALU.pow).then_inc(s_rstd, 1)

            @block.vector
            def _(dve):
                steps = [0]

                def link(ins):
                    steps[0] += 1
                    ins.then_inc(s_dve, 1)
                    dve.wait_ge(s_dve, steps[0])

                def turned(t):
                    dve.wait_ge(s_pps, 2 * t + 1)
                    if t >= 2:
                        dve.wait_ge(s_zps, t - 1)
                    dve.tensor_copy(pT[:, t % 2, SPLIT:2 * SPLIT, :].rearrange("p k n -> p (k n)"),
                                    P_PS[:, BANK:2 * BANK]).then_inc(s_pTd, 1)

                def shift(t):
                    dve.wait_ge(s_sps, t + 1)
                    dve.tensor_reduce(mxs[:, t:t + 1], S_PS[:, 0:CTX], AX, ALU.max).then_inc(s_mx, 1)
                    dve.wait_ge(s_mx, t + 1)
                    link(dve.tensor_tensor(top[:, t:t + 1], mxs[:, t:t + 1], cq[:, t:t + 1], ALU.add))
                    dve.tensor_tensor(nb[:, t:t + 1], cq[:, t:t + 1], top[:, t:t + 1], ALU.subtract).then_inc(s_nb, 1)

                def norm(t):
                    dve.wait_ge(s_pr, t + 1)
                    link(dve.reciprocal(rinv[:, t:t + 1], rsum[:, t:t + 1]))
                    if t == 0:
                        dve.wait_ge(s_xb, 1)
                    dve.wait_ge(s_ops, t + 1)
                    dve.scalar_tensor_tensor(r[:, t % 2, :], O_PS[:, 0:D], rinv[:, t:t + 1], env.x[:, t, :],
                                             ALU.mult, ALU.add).then_inc(s_r, 1)
                    dve.wait_ge(s_r, t + 1)
                    link(dve.bn_stats(st[:, :], r[:, t % 2, :]))
                    link(dve.bn_aggr(mv[:, :], st[:, :]))
                    dve.tensor_scalar(ve[:, :], mv[:, 1:2], EPS, None, ALU.add).then_inc(s_ve, 1)
                    dve.wait_ge(s_rstd, t + 1)
                    dve.tensor_scalar(env.x[:, t, :], r[:, t % 2, :], mv[:, 0:1], rstd[:, 0:1],
                                      ALU.subtract, ALU.mult).then_inc(s_xn, 1)

                for b in range(B):
                    dve.wait_ge(s_fps, b + 1)
                    dve.tensor_copy(qk[:, b * L:(b + 1) * L], bank(4 + b % 2)).then_inc(s_f, 1)
                dve.wait_ge(s_cps, 1)
                dve.tensor_copy(cq[:, :], O_PS[:, 0:T]).then_inc(s_cq, 1)
                dve.wait_ge(s_cq, 1)
                for t in range(T + 2):
                    if 1 <= t <= T:
                        turned(t - 1)
                    if t < T:
                        shift(t)
                    if t >= 2:
                        norm(t - 2)


def l0_ffn(nc, env, hb):
    w, PS = env.w, env.PS
    R = 3
    with ExitStack() as c_:
        sb, sem = env.alloc(c_)
        iota, thr, iota32 = env.iota16, env.thr16, env.iota32
        tiles = lambda c: list(range(c * TB, (c + 1) * TB))
        hT = sb("hT", [P, FC, N], F32)
        slot = sb("slot", [P, T], I32)
        xs = sb("xs", [P, T, D], F32)
        s_l1 = sem("f_l1")
        s_fw = sem("f_w")
        s_dve = sem("f_dve")
        s_top = sem("f_top")
        s_ex = sem("f_exp")
        s_cnt = sem("f_cnt")
        s_rank = sem("f_rank")
        s_slot = sem("f_slot")
        s_tab = sem("f_tab")
        s_xs = sem("f_xs")
        s_scat = sem("f_scat", keep=True)
        s_sps = sem("f_sps")
        s_sg = sem("f_sg")
        s_sh = sem("f_sh")
        table = sb("table", [1, ETILES], I32)

        silu = sb("silu", [P, 2, L], F32)
        items = [(c, f) for c in range(B) for f in range(FC)]
        ROUTE_ITEMS = 9

        def shared_pe(pe, n):
            c, f = items[n]
            if n == 0:
                pe.wait_ge(s_fw, 16 * len(env.loads["f"]))
            if n >= 2:
                pe.wait_ge(s_sh, n - 1)
            for e, name in enumerate(("f_wg", "f_wu")):
                o = PS[:, (2 + 2 * (n % 2) + e) * BANK:(3 + 2 * (n % 2) + e) * BANK]
                for k in range(KD):
                    last = pe.matmul(o, w[name][:, k, f * P:(f + 1) * P], env.xT[:, k, c * L:(c + 1) * L],
                                     start=(k == 0), stop=(k == KD - 1))
            last.then_inc(s_sps, 1)

        def shared_dve(dve, n):
            c, f = items[n]
            dve.wait_ge(s_sg, n + 1)
            dve.tensor_tensor(hT[:, f, c * L:(c + 1) * L], silu[:, n % 2, :],
                              PS[:, (3 + 2 * (n % 2)) * BANK:(4 + 2 * (n % 2)) * BANK],
                              ALU.mult).then_inc(s_sh, 1)

        def shared_act(act, n):
            act.wait_ge(s_sps, n + 1)
            if n >= 2:
                act.wait_ge(s_sh, n - 1)
            act.activation(silu[:, n % 2, :], PS[:, (2 + 2 * (n % 2)) * BANK:(3 + 2 * (n % 2)) * BANK],
                           ACT.Silu).then_inc(s_sg, 1)

        with ExitStack() as c2:
            sb2, _ = env.alloc(c2)
            lg = sb2("lg", [P, T, E], F32)
            top = sb2("top1", [P, T], F32)
            lt = sb2("lt", [P, T, E], F32)
            idx = sb2("idx", [P, T], F32)
            oh = sb2("oh", [P, T, E], F32)
            en = sb2("en", [P, T], F32)
            e1 = sb2("e1", [P, T], F32)
            sg = sb2("sgm", [P, T], F32)
            pre = sb2("pre", [P, T + 1, E], F32)
            nt3 = sb2("nt3", [P, E, E], F32)
            cs = sb2("cs", [P, 2, 2 * E], F32)
            nt = sb2("nt", [P, E], F32)
            st = sb2("st1", [P, E], F32)
            sbase = sb2("sbase", [P, E], F32)
            sf = sb2("sf", [P, T], F32)
            le = sb2("le", [1, ETILES, E], F32)
            tf = sb2("tf", [1, ETILES], F32)
            tf2 = sb2("tf2", [1, ETILES], F32)

            with nc.Block() as block:

                @block.sync
                def _(sp):
                    for dst, src in env.loads["1"]:
                        sp.dma_start(dst, src).then_inc(s_l1, 16)
                    sp.wait_ge(s_l1, 16 * len(env.loads["1"]))

                @block.tensor
                def _(pe):
                    for n in range(2):
                        shared_pe(pe, n)
                    pe.wait_ge(s_cnt, 1)
                    pe.matmul(PS[:, BANK:BANK + E], env.tri, pre[:, T, :], start=True, stop=True)
                    pe.matmul(PS[:, BANK + E:BANK + 2 * E], env.ones, pre[:, T, :], start=True,
                              stop=True).then_inc(s_rank, 1)
                    for n in range(2, ROUTE_ITEMS):
                        shared_pe(pe, n)

                @block.scalar
                def _(act):
                    for dst, src in env.loads["f"]:
                        act.dma_start(dst, src).then_inc(s_fw, 16)
                    act.wait_ge(s_top, 1)
                    act.activation(en[:, :], top[:, :], ACT.Exp, scale=-1.0).then_inc(s_ex, 1)
                    for n in range(ROUTE_ITEMS):
                        shared_act(act, n)

                @block.gpsimd
                def _(pool):
                    pool.wait_ge(s_slot, 1)
                    for t in range(T):
                        pool.wait_ge(s_xs, t + 1)
                        pool.indirect_dma_start(out=env.xg, out_offset=bass.IndirectOffsetOnAxis(ap=slot[:, t:t + 1], axis=0),
                                                in_=xs[:, t, :], in_offset=None).then_inc(s_scat, 16)
                    pool.wait_ge(s_scat, 16 * T)

                @block.vector
                def _(dve):
                    steps = [0]

                    def link(ins):
                        steps[0] += 1
                        ins.then_inc(s_dve, 1)
                        dve.wait_ge(s_dve, steps[0])

                    te = lambda a: a.unsqueeze(2).to_broadcast([P, T, E])
                    ie = iota.unsqueeze(1).to_broadcast([P, T, E])
                    link(dve.tensor_copy(lg[:, :, :].rearrange("p t e -> p (t e)"), env.logits))
                    dve.tensor_reduce(top[:, :], lg[:, :, :], AX, ALU.max).then_inc(s_top, 1)
                    dve.wait_ge(s_top, 1)
                    link(dve.tensor_tensor(lt[:, :, :], lg[:, :, :], te(top[:, :]), ALU.is_lt))
                    link(dve.scalar_tensor_tensor(lg[:, :, :], lt[:, :, :], float(E), ie, ALU.mult, ALU.add))
                    link(dve.tensor_reduce(idx[:, :], lg[:, :, :], AX, ALU.min))
                    dve.memset(pre[:, 0, :], 0.0)
                    link(dve.tensor_tensor(oh[:, :, :], ie, te(idx[:, :]), ALU.is_equal))
                    for t in range(T):
                        ins = dve.tensor_tensor(pre[:, t + 1, :], pre[:, t, :], oh[:, t, :], ALU.add)
                        if t < T - 1:
                            link(ins)
                    ins.then_inc(s_cnt, 1)
                    shared_dve(dve, 0)
                    dve.wait_ge(s_ex, 1)
                    link(dve.tensor_scalar(e1[:, :], en[:, :], 1.0, None, ALU.add))
                    link(dve.reciprocal(sg[:, :], e1[:, :]))
                    for t in range(T):
                        dve.tensor_scalar(xs[:, t, :], env.x[:, t, :], sg[:, t:t + 1], None, ALU.mult).then_inc(s_xs, 1)
                    shared_dve(dve, 1)
                    link(dve.memset(cs[:, :, :], 0.0))
                    dve.wait_ge(s_rank, 1)
                    link(dve.tensor_tensor(nt3[:, :, :], PS[:, BANK + E:BANK + 2 * E].unsqueeze(2).to_broadcast([P, E, E]),
                                           thr.unsqueeze(1).to_broadcast([P, E, E]), ALU.is_gt))
                    link(dve.tensor_reduce(nt[:, :], nt3[:, :, :], AX, ALU.add))
                    link(dve.tensor_copy(cs[:, 0, E:2 * E], nt[:, :]))
                    for n in range(4):
                        a, b, d = n % 2, (n + 1) % 2, 1 << n
                        link(dve.tensor_tensor(cs[:, b, E:2 * E], cs[:, a, E:2 * E], cs[:, a, E - d:2 * E - d], ALU.add))
                    end = cs[:, 0, E:2 * E]
                    link(dve.tensor_tensor(st[:, :], end, nt[:, :], ALU.subtract))
                    link(dve.scalar_tensor_tensor(sbase[:, :], st[:, :], float(P), PS[:, BANK:BANK + E], ALU.mult, ALU.add))
                    link(dve.tensor_tensor(lt[:, :, :], pre[:, 0:T, :], sbase[:, :].unsqueeze(1).to_broadcast([P, T, E]), ALU.add))
                    link(dve.tensor_tensor(lg[:, :, :], lt[:, :, :], oh[:, :, :], ALU.mult))
                    link(dve.tensor_reduce(sf[:, :], lg[:, :, :], AX, ALU.add))
                    dve.tensor_copy(slot[:, :], sf[:, :]).then_inc(s_slot, 1)
                    link(dve.tensor_tensor(le[:, :, :], end[0:1, :].unsqueeze(1).to_broadcast([1, ETILES, E]),
                                           iota32[0:1, :].unsqueeze(2).to_broadcast([1, ETILES, E]), ALU.is_le))
                    link(dve.tensor_reduce(tf[:, :], le[:, :, :], AX, ALU.add))
                    link(dve.tensor_scalar(tf2[:, :], tf[:, :], float(E - 1), None, ALU.min))
                    dve.tensor_copy(table[:, :], tf2[:, :]).then_inc(s_tab, 1)
                    for n in range(2, ROUTE_ITEMS):
                        shared_dve(dve, n)

        with ExitStack() as c2:
            sb2, sem2 = env.alloc(c2)
            wgu = sb2("wgu", [P, R, KD, 2 * F], F32)
            wdn = sb2("wdn", [P, R, FC, D], F32)
            xt = sb2("xt", [P, R, D], F32)
            xtT = sb2("xtT", [P, R, KD, P], F32)
            sgt = sb2("sgt", [P, R, F], F32)
            ht = sb2("ht", [P, R, FC, P], F32)
            yt = sb2("yt", [P, R, D], F32)
            s_ldx = [sem2(f"e_ldx{u}") for u in range(R)]
            s_ldw = [sem2(f"e_ldw{u}") for u in range(R)]
            s_ldd = [sem2(f"e_ldd{u}") for u in range(R)]
            s_tps = sem2("e_tps")
            s_t = sem2("e_t")
            s_gu = sem2("e_gu")
            s_g = sem2("e_g")
            s_h = sem2("e_h")
            s_yps = sem2("e_yps")
            s_y = sem2("e_y")
            s_yo = [sem2(f"e_yo{u}", keep=True) for u in range(R)]
            GU = lambda u: PS[:, 2 * u * BANK:2 * (u + 1) * BANK]
            T_PS, Y_PS = PS[:, 6 * BANK:7 * BANK], PS[:, 7 * BANK:8 * BANK]
            LAST = ETILES - 1
            ROUNDS = (ETILES - 2) // R
            SP_ROUNDS = (ETILES - R - 1) // R

            with nc.Block() as block:

                @block.sync
                def _(sp):
                    expert = lambda j: sp.value_load(table[0:1, bass.ds(j, 1)], min_val=0, max_val=E - 1)

                    def load_in(j, u, free=None):
                        e = expert(j)
                        if free is not None:
                            sp.wait_ge(s_gu, free)
                        sp.dma_start(xt[:, u, :], env.xg_t[j]).then_inc(s_ldx[u], 16)
                        sp.dma_start(wgu[:, u, :, :], env.gu_t[e].rearrange("(k p) n -> p k n", p=P)).then_inc(s_ldw[u], 16)

                    def load_down(j, u, free=None):
                        e = expert(j)
                        if free is not None:
                            sp.wait_ge(s_yps, free)
                        sp.dma_start(wdn[:, u, :, :], env.dn_t[e].rearrange("(k p) n -> p k n", p=P)).then_inc(s_ldd[u], 16)

                    def reload(j, u):
                        load_in(j + R, u, j + 1)
                        load_down(j + (R - 1), (u + R - 1) % R, j)

                    for j in range(R):
                        load_in(j, j)
                        load_down(j, j)
                    load_in(R, 0, 1)
                    with sp.Fori(0, SP_ROUNDS) as i:
                        for v in range(1, R + 1):
                            reload(i * R + v, v % R)
                    for j in range(1 + SP_ROUNDS * R, ETILES - R):
                        reload(j, j % R)
                    load_down(LAST, LAST % R, ETILES - R)

                @block.tensor
                def _(pe):
                    def turn(j, u, n):
                        pe.wait_ge(s_ldx[u], 16 * (n + 1))
                        pe.wait_ge(s_t, j + 1)
                        for k in range(KD):
                            last = pe.transpose(T_PS[:, k * P:(k + 1) * P], xt[:, u, k * P:(k + 1) * P], env.ident)
                        last.then_inc(s_tps, 1)

                    def gate_up(j, u, n):
                        pe.wait_ge(s_ldw[u], 16 * (n + 1))
                        pe.wait_ge(s_t, j + 2)
                        for f in range(2 * FC):
                            for k in range(KD):
                                last = pe.matmul(GU(u)[:, f * P:(f + 1) * P], wgu[:, u, k, f * P:(f + 1) * P],
                                                 xtT[:, u, k, :], start=(k == 0), stop=(k == KD - 1))
                        last.then_inc(s_gu, 1)

                    def down(j, u, n):
                        pe.wait_ge(s_ldd[u], 16 * (n + 1))
                        pe.wait_ge(s_h, j + 1)
                        pe.wait_ge(s_y, j + 1)
                        for f in range(FC):
                            last = pe.matmul(Y_PS[:, 0:D], ht[:, u, f, :], wdn[:, u, f, :],
                                             start=(f == 0), stop=(f == FC - 1))
                        last.then_inc(s_yps, 1)

                    for n in range(ROUTE_ITEMS, len(items)):
                        shared_pe(pe, n)
                    turn(0, 0, 0)
                    gate_up(0, 0, 0)
                    pe.wait_ge(s_sh, len(items))
                    turn(1, 1, 0)
                    with pe.Fori(0, ROUNDS) as i:
                        for m in range(R):
                            j = i * R + (m + 1)
                            gate_up(j, (m + 1) % R, i + (m + 1) // R)
                            turn(j + 1, (m + 2) % R, i + (m + 2) // R)
                            down(j - 1, m, i)
                    for j in range(ROUNDS * R + 1, ETILES):
                        gate_up(j, j % R, j // R)
                        if j < LAST:
                            turn(j + 1, (j + 1) % R, (j + 1) // R)
                        down(j - 1, (j - 1) % R, (j - 1) // R)
                    down(LAST, LAST % R, LAST // R)

                @block.scalar
                def _(act):
                    def turn(j, u):
                        act.wait_ge(s_tps, j + 1)
                        act.activation(xtT[:, u, :, :].rearrange("p k n -> p (k n)"), T_PS[:, 0:D], ACT.Copy).then_inc(s_t, 1)

                    def gate(j, u):
                        act.wait_ge(s_gu, j + 1)
                        act.activation(sgt[:, u, :], GU(u)[:, 0:F], ACT.Silu).then_inc(s_g, 1)

                    act.sem_inc(s_t, 1)
                    for n in range(ROUTE_ITEMS, len(items)):
                        shared_act(act, n)
                    turn(0, 0)
                    gate(0, 0)
                    turn(1, 1)
                    with act.Fori(0, ROUNDS) as i:
                        for m in range(R):
                            j = i * R + (m + 1)
                            gate(j, (m + 1) % R)
                            turn(j + 1, (m + 2) % R)
                    for j in range(ROUNDS * R + 1, ETILES):
                        gate(j, j % R)
                        if j < LAST:
                            turn(j + 1, (j + 1) % R)

                @block.vector
                def _(dve):
                    def hidden(j, u):
                        dve.wait_ge(s_g, j + 1)
                        dve.tensor_tensor(ht[:, u, :, :].rearrange("p f n -> p (f n)"), sgt[:, u, :],
                                          GU(u)[:, F:2 * F], ALU.mult).then_inc(s_h, 1)

                    def out(j, u, n):
                        dve.wait_ge(s_yps, j + 1)
                        if n is not None:
                            dve.wait_ge(s_yo[u], 16 * n)
                        dve.tensor_copy(yt[:, u, :], Y_PS[:, 0:D]).then_inc(s_y, 1)

                    dve.sem_inc(s_y, 1)
                    for n in range(ROUTE_ITEMS, len(items)):
                        shared_dve(dve, n)
                    hidden(0, 0)
                    for j in range(1, R + 1):
                        hidden(j, j % R)
                        out(j - 1, j - 1, None)
                    with dve.Fori(1, ROUNDS) as i:
                        for m in range(R):
                            j = i * R + (m + 1)
                            hidden(j, (m + 1) % R)
                            out(j - 1, m, i)
                    for j in range(ROUNDS * R + 1, ETILES):
                        hidden(j, j % R)
                        out(j - 1, (j - 1) % R, (j - 1) // R)
                    out(LAST, LAST % R, LAST // R)

                @block.gpsimd
                def _(pool):
                    def out(j, u):
                        pool.wait_ge(s_y, j + 2)
                        pool.dma_start(env.yg_t[j], yt[:, u, :]).then_inc(s_yo[u], 16)

                    with pool.Fori(0, ETILES // R) as i:
                        for u in range(R):
                            out(i * R + u, u)
                    for j in range(ETILES // R * R, ETILES):
                        out(j, j % R)
                    for u in range(R):
                        pool.wait_ge(s_yo[u], 16 * ((ETILES - u + R - 1) // R))

        env.next_layer()
        return combine_and_prepare(nc, env, hT, xs, slot, hb)


def combine_and_prepare(nc, env, hT, xs, slot, hb):
    w, PS = env.w, env.PS
    LAG, AHEAD = 4, 3
    FIRST_LOAD = 12
    blocks = [(b, name, m) for b in range(B) for name in ("q", "k") for m in range(KD)]
    STEPS = LAG + len(blocks) // KD + 1
    blocks_at = lambda c: range((c - LAG) * KD, (c - LAG + 1) * KD) if 0 <= (c - LAG) * KD < len(blocks) else ()
    with ExitStack() as c_:
        _, sem = env.alloc(c_)
        tail = Tail(env, c_, "t2", (0, 0, 2), PAIR_TILES, FC, inputs=False)
        hb.semaphores(sem, "sa")
        s_all = sem("f_all")
        s_ga = [sem(f"f_ga{c}", keep=True) for c in range(CHUNKS)]

        def bias(n):
            b, name, m = blocks[n]
            return w["s_b" + name][:, m:m + 1], w["s_b" + name][:, 1 - m:2 - m]

        def dst(n):
            b, name, m = blocks[n]
            return (env.qs if name == "q" else env.ks).rearrange("(b p m s) l -> b m p s l", b=B, p=P, m=KD)[b][m]

        sp_ = Split(env, c_, "sqk", L, bias, dst, lambda n: Q_PARTS if blocks[n][1] == "q" else K_PARTS, 4,
                    rope=lambda n: (env.cos, env.sin_neg if blocks[n][2] == 0 else env.sin))
        val = Values(env, c_, "sv", [(b, tuple(range(TB)), P) for b in range(B)], w["s_bv"], env.vs)
        pair = lambda item: PS[:, (4 + 2 * (item % 2)) * BANK:(6 + 2 * (item % 2)) * BANK]
        item_of = lambda n: 3 * (n // 4) + n % 4 // KD

        def item_free(pe, item):
            b, what = divmod(item - 2, 3)
            if b >= 0:
                pe.wait_ge(val.s_v, b + 1) if what == 2 else sp_.freed(pe, 4 * b + KD * what + 1)

        with nc.Block() as block:

            @block.gpsimd
            def _(pool):
                def gather(c):
                    for t in PAIR_TILES(c):
                        pool.indirect_dma_start(out=xs[:, t, :], out_offset=None, in_=env.yg,
                                                in_offset=bass.IndirectOffsetOnAxis(ap=slot[:, t:t + 1], axis=0)
                                                ).then_inc(s_ga[c], 16)

                for c in range(AHEAD):
                    gather(c)
                for c in range(STEPS):
                    if c < CHUNKS:
                        tail.pool_rstd(pool, c)
                    if c + AHEAD < CHUNKS:
                        gather(c + AHEAD)
                    if c == LAG - 2:
                        val.pool_init(pool)
                    for n in blocks_at(c):
                        sp_.pool_whole(pool, n)
                    for n in blocks_at(c - 1):
                        sp_.pool_lo(pool, n)

            @block.tensor
            def _(pe):
                for c in range(STEPS):
                    if c < CHUNKS:
                        tail.pe_proj(pe, c, lambda k: w["f_wd"][:, k, :],
                                     lambda i, k: hT[:, k, (2 * c + i) * P:(2 * c + i + 1) * P])
                    if 2 <= c < CHUNKS + 2:
                        tail.pe_out(pe, c - 2)
                    for n in blocks_at(c):
                        b, name, m = blocks[n]
                        if m == 0:
                            pe.wait_ge(tail.s_xT, TB // 2 * (b + 1))
                            item_free(pe, item_of(n))
                        for k in range(KD):
                            last = pe.matmul(pair(item_of(n))[:, m * L:(m + 1) * L], w["s_w" + name][:, k, m * P:(m + 1) * P],
                                             env.xT[:, k, b * L:(b + 1) * L], start=(k == 0), stop=(k == KD - 1))
                        last.then_inc(sp_.s_full, 1)
                        if n % 4 == 3:
                            item_free(pe, 3 * b + 2)
                            for j in range(TB):
                                t = b * TB + j
                                for k in range(KD):
                                    last = pe.matmul(pair(3 * b + 2)[:, j * D:(j + 1) * D], env.xT[:, k, t * P:(t + 1) * P],
                                                     w["s_wv"][:, k, :], start=(k == 0), stop=(k == KD - 1))
                            last.then_inc(val.s_full, 1)

            @block.scalar
            def _(act):
                for c in range(STEPS):
                    if 2 <= c < CHUNKS + 2:
                        tail.act_out(act, c - 2)
                    for n in blocks_at(c - 1):
                        sp_.act_mid(act, n)
                    for n in blocks_at(c):
                        sp_.act_hi(act, n, None)

            @block.vector
            def _(dve):
                for c in range(STEPS):
                    if c < CHUNKS:
                        u = c % tail.ring
                        tail.dve_sum(dve, c, biased=False)
                        dve.wait_ge(tail.s_r, c + 1)
                        dve.wait_ge(s_ga[c], 16 * 2)
                        dve.tensor_tensor(tail.r[:, u, :, :], tail.r[:, u, :, :], xs[:, 2 * c:2 * c + 2, :],
                                          ALU.add).then_inc(s_all, 1)
                        tail.dve_stats(dve, c, ready=s_all)
                    if 1 <= c <= CHUNKS:
                        tail.dve_apply(dve, c - 1)
                    if len(blocks_at(c - 1)) and blocks_at(c - 1)[-1] % 4 == 3:
                        b = blocks_at(c - 1)[-1] // 4
                        val.dve_copy(dve, b, pair(3 * b + 2))
                    for n in blocks_at(c):
                        m = blocks[n][2]
                        ps = pair(item_of(n))
                        sp_.dve_rot(dve, n, n - m + KD, ps[:, m * L:(m + 1) * L], ps[:, (1 - m) * L:(2 - m) * L])
                    for n in blocks_at(c - 1):
                        sp_.dve_rest(dve, n)

            @block.sync
            def _(sp):
                def load(g):
                    hb.load_q(sp, g, g)
                    hb.load_k(sp, g, g)

                for n in range(len(blocks)):
                    if n == FIRST_LOAD:
                        sp_.sp_end(sp, 4)
                        sp.wait_ge(val.s_out[0], val.sent_before[2])
                    if FIRST_LOAD <= n < FIRST_LOAD + hb.RING:
                        load(n - FIRST_LOAD)
                    if n % 4 == 3:
                        val.sp_out(sp, n // 4)
                    sp_.sp_out(sp, n)

    def stored(sp):
        sp_.sp_end(sp, len(blocks))
        val.sp_end(sp)

    return stored


class HeadBuffers:

    RING = 3

    def __init__(self, env, c, name, NK, causal, qp, kp, vp, Q=None):
        self.NK, self.causal, self.qp, self.kp, self.vp = NK, causal, qp, kp, vp
        self.KLOADS = 1 if causal else len(K_PARTS)
        sb, _ = env.alloc(c)
        R = self.RING
        self.K = sb(name + "_K", [P, R, G, NK], BF16)
        self.Q = Q if Q is not None else sb(name + "_Q", [P, R, G, L], BF16)

    def semaphores(self, sem, name):
        self.s_k = [sem(f"{name}_k{u}") for u in range(self.RING)]
        self.s_q = [sem(f"{name}_q{u}") for u in range(self.RING)]

    def load_q(self, sp, g, u):
        sp.dma_start(self.Q[0:QK_ROWS, u, :, :], self.qp(g)).then_inc(self.s_q[u], 16)

    def load_k(self, sp, g, u):
        if self.causal:
            sp.dma_start(self.K[0:QK_ROWS, u, :, :], self.kp(g)).then_inc(self.s_k[u], 16)
        else:
            for j, part in enumerate(K_PARTS):
                sp.dma_start(self.K[j:QK_ROWS:len(K_PARTS), u, :, :], self.kp(g, part)).then_inc(self.s_k[u], 16)


def heads_loop(nc, env, name, hb, OT, stored=None):
    PS = env.PS
    NK, causal, R = hb.NK, hb.causal, hb.RING
    Kst, Qst, s_k, s_q, KLOADS = hb.K, hb.Q, hb.s_k, hb.s_q, hb.KLOADS
    KT = -(-NK // P)
    STEPS = KT * G
    rows = lambda kt: min(P, NK - kt * P)
    q0 = lambda kt: kt * P if causal else 0
    CUTS = -(-NK // BANK)
    KU = -(-NK // CUTS)
    units = [(h, qt, e) for h in range(G) for qt in range(TB) for e in range(CUTS)]
    keys_of = lambda qt, e: (0, (qt + 1) * P) if causal else (e * KU, min((e + 1) * KU, NK))
    R1 = 4
    U = len(units)
    EARLY = U // 2 + 2 if causal else U // 4
    M_STEP = (U - EARLY) * STEPS // U + 3
    S1 = STEPS + 1
    def pos(g, n):
        return n + (n > M_STEP and not (type(g) is int and g == GROUPS - 1))

    M_POS = M_STEP + 1
    COLS = G * TB
    VLOADS = 1 if NK % P == 0 else 2
    LEAD = 8
    ROUNDS = (GROUPS - R - 1) // R
    assert U % R1 == 0 and GROUPS == R * ROUNDS + R + 1

    with ExitStack() as c:
        sb, sem = env.alloc(c)
        Vg = sb(name + "_V", [P, R, KT, G * VW], F32)
        Pr = sb(name + "_P", [P, R, G, L], F32)
        part = sb(name + "_part", [P, COLS, CUTS], F32)
        mx = sb(name + "_mx", [P, COLS], F32)
        mh = sb(name + "_mh", [P, 2, COLS], BF16)
        mrow = sb(name + "_mrow", [2 * COLS, P], BF16)
        s_ones = sem(name + "_ones")
        s_v = [sem(f"{name}_v{u}") for u in range(R)]
        s_mq = [sem(f"{name}_mq{u}") for u in range(R)]
        s_1 = sem(name + "_1")
        s_1free = sem(name + "_1free")
        s_step = sem(name + "_step")
        s_mh = sem(name + "_mh")
        s_2 = sem(name + "_2")
        s_exp = sem(name + "_exp")
        s_pv = sem(name + "_pv")
        s_ot = sem(name + "_ot")
        ring1 = lambda n: PS[:, n % R1 * BANK:(n % R1 + 1) * BANK]
        ring2 = lambda n: PS[:, (4 + n % R) * BANK:(5 + n % R) * BANK]
        O_PS = PS[:, 7 * BANK:8 * BANK]
        ONE = QK_ROWS


        with nc.Block() as block:

            @block.sync
            def _(sp):
                def load_v(g, u):
                    full = NK // P
                    sp.dma_start(Vg[:, u, 0:full, :],
                                 hb.vp[g][0:full * P, :].rearrange("(k p) n -> p k n", p=P)).then_inc(s_v[u], 16)
                    if full < KT:
                        sp.dma_start(Vg[0:rows(full), u, full, :], hb.vp[g][full * P:NK, :]).then_inc(s_v[u], 16)

                def maxima(items_before, u):
                    sp.wait_ge(s_exp, items_before + 1)
                    for e in range(2):
                        sp.dma_start(Qst[ONE + e:ONE + e + 1, u, :, :].rearrange("p h (t n) -> p (h t) n", n=P),
                                     mrow[e * COLS:(e + 1) * COLS, :]).then_inc(s_mq[u], 16)

                def reload(g, u):
                    sp.wait_ge(s_2, g * S1 + (1 + S1))
                    hb.load_q(sp, g + R, u)
                    hb.load_k(sp, g + R, u)
                    sp.wait_ge(s_pv, g * KT + (R + KT))
                    load_v(g + R, u)

                for g in range(R):
                    load_v(g, g)
                maxima(0, 0)
                if stored:
                    stored(sp)
                with sp.Fori(0, ROUNDS) as i:
                    for u in range(R):
                        g = i * R + u
                        maxima(g * S1 + (1 + M_POS), (u + 1) % R)
                        reload(g, u)
                for g in range(ROUNDS * R, GROUPS - 1):
                    maxima(g * S1 + (1 + M_POS), (g + 1) % R)
                    if g + R < GROUPS:
                        reload(g, g % R)

            @block.gpsimd
            def _(pool):
                for u in range(R):
                    pool.memset(Kst[ONE:ONE + 2, u, :, :].rearrange("p h n -> p (h n)"), 1.0).then_inc(s_ones, 1)

            @block.tensor
            def _(pe):
                def unit(g, u, n, first):
                    if n == 0:
                        pe.wait_ge(s_k[u], 16 * KLOADS * (first + 1))
                        pe.wait_ge(s_q[u], 16 * (first + 1))
                    if n >= R1 or type(g) is not int or g:
                        pe.wait_ge(s_1free, g * U + (n - R1 + 1))
                    h, qt, e = units[n]
                    k0, k1 = keys_of(qt, e)
                    o = ring1(n)[:, 0:k1 - k0]
                    last = pe.matmul(o, Qst[0:QK_ROWS, u, h, qt * P:(qt + 1) * P], Kst[0:QK_ROWS, u, h, k0:k1],
                                     start=True, stop=not causal)
                    if causal:
                        last = pe.matmul(o[:, k1 - P:k1], env.identb, env.mask_q, start=False, stop=True)
                    last.then_inc(s_1, 1)

                def maxima(g, item):
                    pe.wait_ge(s_mh, g + 1)
                    pe.matmul(ring2(item)[0:2 * COLS, 0:P], mh[:, :, :].rearrange("p e c -> p (e c)"), env.identb,
                              start=True, stop=True).then_inc(s_2, 1)

                def bank_free(g, p):
                    if type(g) is not int or g or p >= 2:
                        pe.wait_ge(s_exp, g * S1 + (p - 1))

                def score(g, u, kt, h, first):
                    n = kt * G + h
                    if n == 0:
                        pe.wait_ge(s_ones, R)
                        pe.wait_ge(s_mq[u], 32 * (first + 1))
                    bank_free(g, pos(g, n))
                    o = ring2(1 + u * S1 + pos(g, n))
                    r = rows(kt)
                    w_ = L - q0(kt)
                    last = pe.matmul(o[0:r, 0:w_], Kst[0:ONE + 2, u, h, kt * P:kt * P + r], Qst[0:ONE + 2, u, h, q0(kt):L],
                                     start=True, stop=not causal)
                    if causal:
                        last = pe.matmul(o[0:r, 0:P], env.identb, env.mask_k, start=False, stop=True)
                    last.then_inc(s_2, 1)

                def values(g, u, kt, first):
                    r = rows(kt)
                    if kt == 0:
                        pe.wait_ge(s_v[u], 16 * VLOADS * (first + 1))
                        pe.wait_ge(s_ot, g + 1)
                    pe.wait_ge(s_exp, g * S1 + (2 + pos(g, kt * G + G - 1)))
                    for h in range(G):
                        last = pe.matmul(O_PS[h * VW:(h + 1) * VW, q0(kt):L], Vg[0:r, u, kt, h * VW:(h + 1) * VW],
                                         Pr[0:r, (u * KT + kt) % R, h, 0:L - q0(kt)],
                                         start=(kt == 0), stop=(kt == KT - 1), tile_position=(0, h * VW))
                    last.then_inc(s_pv, 1)

                def group(g, u, first, before, ahead):
                    after = [(1, n) for n in range(EARLY if before else LEAD, U)] * (ahead >= 1)
                    due = [min(len(after), -(-len(after) * (n + 1) // (M_STEP - 3))) for n in range(STEPS)]
                    if ahead >= 2:
                        late = STEPS - (M_STEP - 3)
                        due = [d + max(0, -(-EARLY * (n + 1 - (M_STEP - 3)) // late)) for n, d in enumerate(due)]
                        after += [(2, n) for n in range(EARLY)]
                    done = 0
                    for kt in range(KT):
                        for h in range(G):
                            n = kt * G + h
                            score(g, u, kt, h, first)
                            while done < due[n]:
                                a, m = after[done]
                                unit(g + a, (u + a) % R, m, first + (u + a) // R)
                                done += 1
                            if n == M_STEP and ahead:
                                bank_free(g, M_POS)
                                maxima(g + 1, 1 + u * S1 + M_POS)
                        if kt >= 1:
                            values(g, u, kt - 1, first)
                        elif before:
                            values(g - 1, (u + R - 1) % R, KT - 1, None)

                for n in range(U):
                    unit(0, 0, n, 0)
                for n in range(LEAD):
                    if n == LEAD // 2:
                        maxima(0, 0)
                    unit(1, 1, n, 0)
                group(0, 0, 0, False, 2)
                with pe.Fori(0, ROUNDS) as i:
                    for v in range(1, R + 1):
                        group(i * R + v, v % R, i + v // R, True, 2)
                for g in range(ROUNDS * R + 1, GROUPS):
                    group(g, g % R, g // R, True, GROUPS - 1 - g)
                values(GROUPS - 1, (GROUPS - 1) % R, KT - 1, None)

            @block.scalar
            def _(act):
                def maxima(item, bank):
                    act.wait_ge(s_2, item + 1)
                    act.activation(mrow[:, :], ring2(bank)[0:2 * COLS, 0:P], ACT.Copy).then_inc(s_exp, 1)

                def output(g):
                    act.wait_ge(s_pv, g * KT + (R + KT))
                    act.activation(OT[:, bass.ds(g, 1), :].rearrange("p g n -> p (g n)"), O_PS, ACT.Copy).then_inc(s_ot, 1)

                def group(g, u, before, ahead):
                    for kt in range(KT):
                        act.wait_ge(s_pv, g * KT + (kt + 1))
                        r = rows(kt)
                        w_ = L - q0(kt)
                        for h in range(G):
                            n = kt * G + h
                            act.wait_ge(s_2, g * S1 + (2 + pos(g, n)))
                            act.activation(Pr[0:r, (u * KT + kt) % R, h, 0:w_], ring2(1 + u * S1 + pos(g, n))[0:r, 0:w_],
                                           ACT.Exp, scale=SCALE).then_inc(s_exp, 1)
                            if n == M_STEP and ahead:
                                maxima(g * S1 + (1 + M_POS), 1 + u * S1 + M_POS)
                        if kt == 0 and before:
                            output(g - 1)

                act.sem_inc(s_pv, R)
                act.sem_inc(s_ot, 1)
                maxima(0, 0)
                group(0, 0, False, 2)
                with act.Fori(0, ROUNDS) as i:
                    for v in range(1, R + 1):
                        group(i * R + v, v % R, True, 2)
                for g in range(ROUNDS * R + 1, GROUPS):
                    group(g, g % R, True, GROUPS - 1 - g)
                output(GROUPS - 1)

            @block.vector
            def _(dve):
                def maxima(g):
                    for n in range(U):
                        dve.wait_ge(s_1, g * U + (n + 1))
                        h, qt, e = units[n]
                        k0, k1 = keys_of(qt, e)
                        dve.tensor_reduce(part[:, h * TB + qt, e:e + 1], ring1(n)[:, 0:k1 - k0], AX, ALU.max).then_inc(s_1free, 1)
                    dve.wait_ge(s_1free, g * U + U)
                    dve.tensor_reduce(mx[:, :], part[:, :, :], AX, ALU.max).then_inc(s_step, 1)
                    dve.wait_ge(s_step, g * 2 + 1)
                    dve.tensor_scalar(mh[:, 0, :], mx[:, :], -1.0, None, ALU.mult).then_inc(s_step, 1)
                    dve.wait_ge(s_step, g * 2 + 2)
                    dve.scalar_tensor_tensor(mh[:, 1, :], mx[:, :], -1.0, mh[:, 0, :], ALU.mult, ALU.subtract).then_inc(s_mh, 1)

                maxima(0)
                with dve.Fori(1, GROUPS) as g:
                    maxima(g)


def heads_tail(nc, env, name, OT, wo, bo, hb=None):
    w, PS = env.w, env.PS
    queries = hb is not None
    STEPS = CHUNKS + (4 if queries else 3)
    blocks_at = lambda c: range((c - 5) // 2 * KD, (c - 3) // 2 * KD) if queries and c >= 5 and c % 2 else ()
    with ExitStack() as c_:
        sb, sem = env.alloc(c_)
        tail = Tail(env, c_, name, (2, 4, 2), PAIR_TILES, KD, behind=3)
        if queries:
            sp_ = Split(env, c_, "xq", L, lambda n: w["x_bq"][:, n % KD:n % KD + 1],
                        lambda n: env.qx.rearrange("(n p s) l -> n p s l", p=P, s=len(Q_PARTS))[n], lambda n: Q_PARTS, 4)
            hb.semaphores(sem, "xa")
            s_wd = sem("l1_wd")
        Q_PS = lambda n: PS[:, (6 + n % 2) * BANK:(7 + n % 2) * BANK]
        rc = sb(name + "_rc", [P, 2, H], F32)
        cx = sb(name + "_cx", [P, 4, D], F32)
        s_ops = sem(name + "_ops")
        s_rc = sem(name + "_rc")
        s_cx = sem(name + "_cx")

        with nc.Block() as block:

            @block.tensor
            def _(pe):
                def by_query(t):
                    b, i = divmod(t, TB)
                    if t >= 2:
                        pe.wait_ge(s_cx, t - 1)
                    for g in range(G):
                        last = pe.transpose(PS[:, (t % 2) * BANK + g * P:(t % 2) * BANK + (g + 1) * P],
                                            OT[:, b * G + g, i * P:(i + 1) * P], env.ident)
                    last.then_inc(s_ops, 1)

                def query_block(n):
                    b, m = divmod(n, KD)
                    pe.wait_ge(tail.s_xT, TB // 2 * (b + 1))
                    if n >= 2:
                        sp_.freed(pe, n - 2)
                    for k in range(KD):
                        last = pe.matmul(Q_PS(n), w["x_wq"][:, k, m * P:(m + 1) * P], env.xT[:, k, b * L:(b + 1) * L],
                                         start=(k == 0), stop=(k == KD - 1))
                    last.then_inc(sp_.s_full, 1)

                for c in range(STEPS):
                    if c < CHUNKS:
                        for t in PAIR_TILES(c):
                            by_query(t)
                    for n in blocks_at(c):
                        query_block(n)
                    if 3 <= c < CHUNKS + 3:
                        pe.wait_ge(tail.s_cT, min(c, CHUNKS))
                        tail.pe_out(pe, c - 3)
                    if 1 <= c <= CHUNKS:
                        tail.pe_proj(pe, c - 1, lambda k: wo[:, k, :])
                    if c < CHUNKS:
                        tail.pe_in(pe, c, lambda i: cx[:, (2 * c + i) % 4, :], lambda i: pe.wait_ge(s_cx, 2 * c + i + 1))

            @block.scalar
            def _(act):
                for c in range(STEPS):
                    for n in blocks_at(c):
                        sp_.act_hi(act, n, Q_PS(n))
                    if 3 <= c < CHUNKS + 3:
                        tail.act_out(act, c - 3)
                    if c < CHUNKS:
                        tail.act_in(act, c)
                    for n in blocks_at(c):
                        sp_.act_mid(act, n)

            @block.gpsimd
            def _(pool):
                for c in range(STEPS):
                    if c < CHUNKS:
                        tail.pool_residual(pool, c, lambda t: bo)
                    if 1 <= c <= CHUNKS:
                        tail.pool_rstd(pool, c - 1)
                    for n in blocks_at(c):
                        sp_.pool_lo(pool, n)

            @block.vector
            def _(dve):
                def context(t):
                    if t >= 4:
                        dve.wait_ge(tail.s_cT_ps, t // 2 - 1)
                    o = PS[:, (t % 2) * BANK:(t % 2 + 1) * BANK].rearrange("p (h n) -> p h n", n=VW)
                    dve.wait_ge(s_ops, t + 1)
                    dve.reciprocal(rc[:, t % 2, :], o[:, :, HD:HD + 1].rearrange("p h n -> p (h n)")).then_inc(s_rc, 1)
                    dve.wait_ge(s_rc, t + 1)
                    dve.tensor_tensor(cx[:, t % 4, :].rearrange("p (h d) -> p h d", d=HD), o[:, :, 0:HD],
                                      rc[:, t % 2, :].unsqueeze(2).to_broadcast([P, H, HD]), ALU.mult).then_inc(s_cx, 1)

                for c in range(STEPS):
                    if c < CHUNKS:
                        for t in PAIR_TILES(c):
                            context(t)
                    if 2 <= c < CHUNKS + 2:
                        tail.dve_apply(dve, c - 2)
                    if 1 <= c <= CHUNKS:
                        tail.dve_sum(dve, c - 1)
                        tail.dve_stats(dve, c - 1)
                    for n in blocks_at(c):
                        sp_.dve_rest(dve, n, Q_PS(n))

            if queries:

                @block.sync
                def _(sp):
                    for g in range(hb.RING):
                        hb.load_k(sp, g, g)
                    for dst, src in env.loads["d"]:
                        sp.dma_start(dst, src).then_inc(s_wd, 16)
                    for n in range(B * KD):
                        if n == 2 * KD:
                            sp_.sp_end(sp, KD)
                            for g in range(hb.RING):
                                hb.load_q(sp, g, g)
                        sp_.sp_out(sp, n)
                    sp_.sp_end(sp, B * KD)
                    sp.wait_ge(s_wd, 16 * len(env.loads["d"]))


def l1_tree(nc, env):
    w, PS = env.w, env.PS
    M = D
    NG = M - 1
    DEPTH = 8
    TC = 2
    with ExitStack() as c_:
        sb, sem = env.alloc(c_)
        tail = Tail(env, c_, "t5", (2, 4, 6), PAIR_TILES, KD)
        wr = sb("wr", [P, KD, M], F32)
        lw = sb("lw", [P, KD, D], F32)
        og = sb("og", [P, 2, TB, M, 2], F32)
        lp = sb("lp", [P, 2, TB, M // 2], F32)
        leaf = sb("leaf", [P, 2, TB, M], F32)
        s_wps = sem("d_wps")
        s_w = sem("d_w")
        s_gps = sem("d_gps")
        s_og = sem("d_og")
        s_dve = sem("d_dve")
        s_leaf = sem("d_leaf")
        s_out = sem("d_out")

        with nc.Block() as block:

            @block.tensor
            def _(pe):
                for n, (a, b_, width) in enumerate((("d_wq", "d_rT", NG), ("d_lvT", "d_woT", D))):
                    for m in range(KD):
                        for k in range(KD):
                            last = pe.matmul(PS[:, n * BANK + m * M:n * BANK + m * M + width], w[a][:, k, m * P:(m + 1) * P],
                                             w[b_][:, k, 0:width], start=(k == 0), stop=(k == KD - 1))
                    last.then_inc(s_wps, 1)
                pe.wait_ge(s_w, 2)

                def gates(b):
                    if b >= 1:
                        pe.wait_ge(s_og, b)
                    for i in range(TB):
                        t = b * TB + i
                        for k in range(KD):
                            last = pe.matmul(PS[:, i * M:i * M + NG], env.xT[:, k, t * P:(t + 1) * P], wr[:, k, 0:NG],
                                             start=(k == 0), stop=(k == KD - 1))
                    last.then_inc(s_gps, 1)

                gates(0)
                for c in range(CHUNKS + 1):
                    if c % TC == 0 and c // TC + 1 < B:
                        gates(c // TC + 1)
                    if c >= 1:
                        tail.pe_proj(pe, c - 1, lambda k: lw[:, k, :])
                    if c < CHUNKS:
                        tail.pe_in(pe, c, lambda i: leaf[:, c // TC % 2, c % TC * TC + i, :],
                                   lambda i: pe.wait_ge(s_leaf, c // TC + 1))

            @block.scalar
            def _(act):
                act.wait_ge(s_wps, 1)
                act.activation(wr[:, :, 0:NG], PS[:, 0:KD * M].rearrange("p (k n) -> p k n", k=KD)[:, :, 0:NG],
                               ACT.Copy).then_inc(s_w, 1)
                act.wait_ge(s_wps, 2)
                act.activation(lw[:, :, :], PS[:, BANK:BANK + KD * D].rearrange("p (k n) -> p k n", k=KD),
                               ACT.Copy).then_inc(s_w, 1)

                def gates(b):
                    act.wait_ge(s_gps, b + 1)
                    if b >= 2:
                        act.wait_ge(s_leaf, b - 1)
                    logits = PS[:, 0:TB * M].rearrange("p (t n) -> p t n", t=TB)[:, :, 0:NG]
                    for e, sign in enumerate((-1.0, 1.0)):
                        last = act.activation(og[:, b % 2, :, 0:NG, e], logits, ACT.Sigmoid, scale=sign)
                    last.then_inc(s_og, 1)

                gates(0)
                for c in range(CHUNKS):
                    if c % TC == 0 and c // TC + 1 < B:
                        gates(c // TC + 1)
                    tail.act_in(act, c)

            @block.gpsimd
            def _(pool):
                for c in range(CHUNKS):
                    tail.pool_residual(pool, c, lambda t: w["d_bout"])
                for c in range(CHUNKS):
                    tail.pool_rstd(pool, c)

            @block.vector
            def _(dve):
                steps = [0]

                def link(ins):
                    steps[0] += 1
                    ins.then_inc(s_dve, 1)
                    dve.wait_ge(s_dve, steps[0])

                def leaves(b):
                    dve.wait_ge(s_og, b + 1)
                    if b >= 2:
                        dve.wait_ge(tail.s_cT_ps, (b - 1) * TC)
                    above = og[:, b % 2, :, 0, :]
                    for level in range(1, DEPTH):
                        n = 1 << level
                        dst = leaf[:, b % 2, :, :] if level == DEPTH - 1 else lp[:, level % 2, :, 0:2 * n]
                        last = dve.tensor_tensor(dst.rearrange("p t (n e) -> p t n e", e=2),
                                                 above.unsqueeze(3).to_broadcast([P, TB, n, 2]),
                                                 og[:, b % 2, :, n - 1:2 * n - 1, :], ALU.mult)
                        above = dst
                        if level < DEPTH - 1:
                            link(last)
                    last.then_inc(s_leaf, 1)

                for c in range(CHUNKS + 2):
                    if c % TC == 0 and c < CHUNKS:
                        leaves(c // TC)
                    if c >= 2:
                        tail.dve_apply(dve, c - 2)
                    if 1 <= c <= CHUNKS:
                        tail.dve_sum(dve, c - 1)
                        tail.dve_stats(dve, c - 1)

            @block.sync
            def _(sp):
                for c in range(CHUNKS):
                    sp.wait_ge(tail.s_xn, c + 1)
                    sp.dma_start(env.d["out"][c * TC * P:(c + 1) * TC * P, :].rearrange("(t p) n -> p t n", p=P),
                                 env.x[:, c * TC:(c + 1) * TC, :]).then_inc(s_out, 16)
                sp.wait_ge(s_out, 16 * CHUNKS)


CF = 5 * P + 2 * E + ETILES + 3 * L

CF_FIRST = 5 * P + 2 * E + ETILES

MATS = {
    "a0_in": (D, 3 * D, "a"), "a0_out": (D, D, "a"), "x_wk": (CD, D, "a"), "x_wv": (CD, D, "a"),
    "c0_wq": (D, D, "c"), "c0_wkT": (D, CD, "c"), "c0_wv": (CD, D, "c"), "f_router": (D, E, "c"),
    "f_wg": (D, F, "f"), "f_wu": (D, F, "f"), "f_wd": (F, D, "f"),
    "s_wq": (D, D, "1"), "s_wk": (D, D, "1"), "s_wv": (D, D, "1"), "s_wo": (D, D, "1"),
    "x_wq": (D, D, "1"), "x_wo": (D, D, "1"),
    "d_wq": (D, D, "d"), "d_rT": (D, D - 1, "d"), "d_lvT": (D, D, "d"), "d_woT": (D, D, "d"),
}
ROWS = {"a0_bout": "a", "x_bv": "a", "c0_bv": "c", "s_bv": "1", "s_bo": "1", "x_bo": "1", "d_bout": "d"}
COLS = {"x_bk": "a", "c0_bq": "c", "c0_bk": "c", "s_bq": "1", "s_bk": "1", "x_bq": "1"}


def build(nc, d):
    env = Env()
    env.d = d
    with ExitStack() as ctx:
        layer_sems = []

        def alloc(c):
            def sb(name, shape, dt):
                return c.enter_context(nc.sbuf_tensor(name, shape, dt))

            def sem(name, keep=False):
                handle = nc.alloc_semaphore(name)
                if not keep:
                    layer_sems.append(handle)
                return handle

            return sb, sem

        def next_layer():
            with nc.Block() as block:

                @block.sync
                def _(sp):
                    for handle in layer_sems:
                        sp.sem_clear(handle)

            for handle in layer_sems:
                nc.release_semaphore(handle)
            layer_sems.clear()

        env.alloc, env.next_layer = alloc, next_layer
        sb, sem = alloc(ctx)
        scratch = lambda name, shape, dt: nc.dram_tensor(name, shape, dt, kind="Internal").ap()
        env.kx = scratch("kx", (B * D, 3, CTX), BF16)
        env.qx = scratch("qx", (B * H * QK_ROWS, L), BF16)
        env.vx = scratch("vx", (GROUPS, CTX, G * VW), F32)
        env.ks = scratch("ks", (B * H * QK_ROWS, L), BF16)
        env.qs = scratch("qs", (B * H * QK_ROWS, L), BF16)
        env.vs = scratch("vs", (GROUPS, L, G * VW), F32)
        env.xg = scratch("xg", (ETILES * P, D), F32)
        env.yg = scratch("yg", (ETILES * P, D), F32)
        env.xg_t = env.xg.rearrange("(j p) n -> j p n", p=P)
        env.yg_t = env.yg.rearrange("(j p) n -> j p n", p=P)
        env.gu_t, env.dn_t = d["f_gu"], d["f_dn"]

        psum = ctx.enter_context(nc.psum_tensor("psum", [P, 8 * BANK], F32))
        env.PS = psum[:, :]
        env.x = sb("x_sb", [P, T, D], F32)
        env.xT = sb("xT_sb", [P, KD, N], F32)
        env.cf = sb("cf_sb", [P, CF], F32)
        env.cb = sb("cb_sb", [P, 3 * P], BF16)
        mh = sb("mhalf", [P, TB], F32)
        env.mhalf = mh[:, :]
        at = 0
        parts = []
        for n in (P, P, P, P, P, E, E, ETILES, L, L, L):
            parts.append(env.cf[:, at:at + n])
            at += n
        env.ident, _, _, env.tri, env.ones, env.iota16, env.thr16, env.iota32, env.cos, env.sin, env.sin_neg = parts
        env.identb, env.mask_q, env.mask_k = (env.cb[:, i * P:(i + 1) * P] for i in range(3))

        env.w, env.loads = {}, {"a": [], "c": [], "f": [], "1": [], "d": []}

        def weights(layer, c):
            sbw, _ = alloc(c)
            for name, (k, n, l) in MATS.items():
                if l == layer:
                    if k == P:
                        t = sbw(name + "_sb", [P, n], F32)
                        env.w[name] = t[:, :]
                        env.loads[layer].append((t[:, :], d[name]))
                    else:
                        t = sbw(name + "_sb", [P, k // P, n], F32)
                        env.w[name] = t
                        env.loads[layer].append((t[:, :, :], d[name].rearrange("(k p) n -> p k n", p=P)))
            if layer == "a":
                t = sbw("a0_bin_sb", [3, 3 * D], F32)
                env.w["a0_bin"] = t[:, :]
                env.loads[layer].insert(1, (t[:, :], d["a0_bin"].partition_broadcast(3)))

            for name, l in ROWS.items():
                if l == layer:
                    t = sbw(name + "_sb", [P, D], F32)
                    env.w[name] = t[:, :]
                    env.loads[layer].append((t[:, :], d[name].partition_broadcast(P)))
            for name, l in COLS.items():
                if l == layer:
                    t = sbw(name + "_sb", [P, KD], F32)
                    env.w[name] = t[:, :]
                    env.loads[layer].append((t[:, :], d[name]))
        with ExitStack() as c0:
            sbc, _ = alloc(c0)
            ctxT_sb = sbc("ctxT_sb", [CD, B * CTX], F32)
            env.ctxT = ctxT_sb
            weights("c", c0)
            with ExitStack() as c1:
                weights("a", c1)
                l0_attn(nc, env)
            l0_xattn(nc, env)
        weights("1", ctx)
        stacks = lambda a: lambda g: a.rearrange("(g h r) n -> g r h n", g=GROUPS, r=QK_ROWS)[g]
        kx_part = lambda g, j: env.kx.rearrange("(g h d) j n -> j g d h n", g=GROUPS, d=HD)[j][g]
        sa = HeadBuffers(env, ctx, "sa", L, True, stacks(env.qs), stacks(env.ks), env.vs)
        with ExitStack() as c0:
            weights("f", c0)
            stored = l0_ffn(nc, env, sa)
        weights("d", ctx)
        with ExitStack() as c1:
            sb1, _ = alloc(c1)
            OT = sb1("OT", [P, GROUPS, L], F32)
            heads_loop(nc, env, "sa", sa, OT, stored)
            with ExitStack() as c2:
                xa = HeadBuffers(env, c2, "xa", CTX, False, stacks(env.qx), kx_part, env.vx, Q=sa.Q)
                heads_tail(nc, env, "t3", OT, env.w["s_wo"], env.w["s_bo"], xa)
                heads_loop(nc, env, "xa", xa, OT)
            heads_tail(nc, env, "t4", OT, env.w["x_wo"], env.w["x_bo"])
        l1_tree(nc, env)


def constants():
    f = np.zeros((P, CF), np.float32)
    i = np.arange(P)
    at = 0

    def put(a):
        nonlocal at
        f[:, at:at + a.shape[1]] = a
        at += a.shape[1]

    put(np.eye(P, dtype=np.float32))
    hide = np.where(i[:, None] >= i[None, :], 0.0, -1e30).astype(np.float32)
    put(hide)
    put(hide.T)
    put((i[:, None] < i[None, :]).astype(np.float32))
    put(np.ones((P, P), np.float32))
    put(np.tile(np.arange(E, dtype=np.float32), (P, 1)))
    put(np.tile(P * np.arange(E, dtype=np.float32), (P, 1)))
    put(np.tile(np.arange(ETILES, dtype=np.float32), (P, 1)))
    frac = (2 * np.arange(HD // 2) / HD).astype(np.float32)
    scale = np.power(np.float32(2500), frac).astype(np.float32)
    angle = np.arange(L).astype(np.float32)[None, :] / scale[:, None]
    cos, sin = np.cos(angle).astype(np.float32), np.sin(angle).astype(np.float32)
    for table in (cos, sin, -sin):
        put(np.tile(table, (2 * P // HD, 1)))
    return f


def kernel(**inputs):
    import concourse.bacc as bacc
    from concourse.bass_utils import run_bass_kernel_spmd

    a = {k: np.asarray(v) for k, v in inputs.items()}
    c = np.ascontiguousarray
    cols = lambda v: c(v.reshape(KD, P).T)
    halves = np.arange(D).reshape(H, 2, HD // 2).transpose(1, 0, 2).reshape(-1)
    cf = constants()
    arrays = {
        "x": c(a["x"].reshape(N, D)), "xT": c(a["x"].reshape(N, D).T), "ctx": c(a["ctx_512"]),
        "ctxT": c(a["ctx_512"].reshape(B * CTX, CD).T), "cf": cf,
        "a0_in": c(a["L0_attn_in_proj_weight"].T), "a0_bin": c(a["L0_attn_in_proj_bias"]),
        "a0_out": c(a["L0_attn_out_proj_weight"].T), "a0_bout": c(a["L0_attn_out_proj_bias"]),
        "c0_wq": c(a["L0_xattn_Wq"]), "c0_bq": cols(a["L0_xattn_bq"]), "c0_wkT": c(a["L0_xattn_Wk"].T),
        "c0_bk": cols(a["L0_xattn_bk"]), "c0_wv": c(a["L0_xattn_Wv"]), "c0_bv": c(a["L0_xattn_bv"]),
        "f_router": c(a["L0_ffn_w_router"].T), "f_gu": c(a["L0_ffn_gate_up_proj"]), "f_dn": c(a["L0_ffn_down_proj"]),
        "f_wg": c(a["L0_ffn_w_gate"].T), "f_wu": c(a["L0_ffn_w_up"].T), "f_wd": c(a["L0_ffn_w_down"].T),
        "s_wq": c(a["L1_attn_wq_w"][:, halves]), "s_bq": cols(a["L1_attn_wq_b"][halves]),
        "s_wk": c(a["L1_attn_wk_w"][:, halves]), "s_bk": cols(a["L1_attn_wk_b"][halves]), "s_wv": c(a["L1_attn_wv_w"]),
        "s_bv": c(a["L1_attn_wv_b"]), "s_wo": c(a["L1_attn_wo_w"]), "s_bo": c(a["L1_attn_wo_b"]),
        "x_wq": c(a["L1_xattn_Wq"]), "x_bq": cols(a["L1_xattn_bq"]), "x_wk": c(a["L1_xattn_Wk"]),
        "x_bk": cols(a["L1_xattn_bk"]), "x_wv": c(a["L1_xattn_Wv"]), "x_bv": c(a["L1_xattn_bv"]),
        "x_wo": c(a["L1_xattn_Wo"]), "x_bo": c(a["L1_xattn_bo"]),
        "d_wq": c(a["L1_ffn_Wq"]), "d_rT": c(a["L1_ffn_routers"].T), "d_lvT": c(a["L1_ffn_leaf_values"].T),
        "d_woT": c(a["L1_ffn_Wout_w"].T), "d_bout": c(a["L1_ffn_Wout_b"]),
    }
    nc = bacc.Bacc("TRN2", target_bir_lowering=False, num_devices=1)
    d = {}
    for name, arr in arrays.items():
        d[name] = nc.dram_tensor("in_" + name, arr.shape, mybir.dt.from_np(arr.dtype), kind="ExternalInput").ap()
    d["out"] = nc.dram_tensor("out_0", (N, D), F32, kind="ExternalOutput").ap()
    build(nc, d)
    r = run_bass_kernel_spmd(nc, [{"in_" + k: v for k, v in arrays.items()}], core_ids=[0])
    return r.results[0]["out_0"].reshape(B, L, D)
```
